# Optimizing a Trainium2 kernel written in Bass

```python
import numpy as np
import jax
import jax.numpy as jnp

def _softmax(x, axis=-1):
    return jax.nn.softmax(x, axis=axis)

def _gelu(x):
    return jax.nn.gelu(x, approximate=True)

def _silu(x):
    return jax.nn.silu(x)

def _sigmoid(x):
    return jax.nn.sigmoid(x)

def _layernorm(x, axis=-1, eps=1e-05):
    m = jnp.mean(x, axis=axis, keepdims=True)
    v = jnp.var(x, axis=axis, keepdims=True)
    return (x - m) / jnp.sqrt(v + eps)

def _scatter_add(tgt, idx, src, axis=0):
    return tgt.at[idx].add(src)

def _segment_sum(src, seg, n):
    return jax.ops.segment_sum(src, seg, n)
kernel_name = 'mk_seq_preln_d1_jaxref_r8_3dfc24'

def setup_inputs(seed: int=0):
    np.random.seed(seed)
    _w = jnp.asarray

    def _L0_attn_setup():
        import jax, jax.numpy as jnp
        import numpy as np
        B, N, D, H = (2, 256, 256, 16)
        HD = D // H
        CHUNK = 64
        BASE = 10000.0

        def _l2norm(x, eps=1e-06):
            return x * jax.lax.rsqrt(jnp.sum(x * x, axis=-1, keepdims=True) + eps)

        def _rope(x):
            n, d = (x.shape[1], x.shape[-1])
            inv = 1.0 / BASE ** (jnp.arange(0, d, 2, dtype=jnp.float32) / d)
            th = jnp.arange(n, dtype=jnp.float32)[:, None] * inv
            cos = jnp.cos(th)[None, :, None, :]
            sin = jnp.sin(th)[None, :, None, :]
            x1, x2 = jnp.split(x, 2, axis=-1)
            return jnp.concatenate([x1 * cos - x2 * sin, x1 * sin + x2 * cos], axis=-1)

        def _kernel_regression(k, v, beta):
            b, n, h, dk = k.shape
            dv = v.shape[-1]
            nc = n // CHUNK
            Kc = k.reshape(b, nc, CHUNK, h, dk).transpose(1, 0, 3, 2, 4)
            Vc = v.reshape(b, nc, CHUNK, h, dv).transpose(1, 0, 3, 2, 4)
            Bc = beta.reshape(b, nc, CHUNK, h).transpose(1, 0, 3, 2)
            eye = jnp.eye(CHUNK, dtype=k.dtype)

            def step(S, inp):
                K, V, bt = inp
                A = jnp.tril(jnp.einsum('bhik,bhjk->bhij', K, K) * bt[:, :, None, :], -1)
                rhs = V - jnp.einsum('bhck,bhkv->bhcv', K, S)
                Vn = jax.scipy.linalg.solve_triangular(eye + A, rhs, lower=True)
                S = S + jnp.einsum('bhck,bhcv->bhkv', K * bt[..., None], Vn)
                return (S, Vn)
            S0 = jnp.zeros((b, h, dk, dv), k.dtype)
            S, Vn = jax.lax.scan(step, S0, (Kc, Vc, Bc))
            v_new = Vn.transpose(1, 0, 3, 2, 4).reshape(b, n, h, dv)
            return (v_new, S)
        key = jax.random.key(seed)
        ks = jax.random.split(key, 6)
        s = 0.02
        return {'x': jax.random.normal(ks[0], (B, N, D), jnp.float32), 'Wq': jax.random.normal(ks[1], (D, D), jnp.float32) * s, 'Wk': jax.random.normal(ks[2], (D, D), jnp.float32) * s, 'Wv': jax.random.normal(ks[3], (D, D), jnp.float32) * s, 'Wo': jax.random.normal(ks[4], (D, D), jnp.float32) * s, 'Wb': jax.random.normal(ks[5], (D, H), jnp.float32) * s}
    _L0_attn_in = _L0_attn_setup()

    def _L0_ffn_setup():
        import jax, jax.numpy as jnp
        import numpy as np
        B, S, H = (2, 128, 256)
        E, K = (8, 2)
        I = 176
        IS = 704
        WSCALE = 0.02
        key = jax.random.key(seed)
        ks = jax.random.split(key, 9)
        f32 = jnp.float32
        return {'hidden_states': jax.random.normal(ks[0], (B, S, H), dtype=f32), 'gate_w': jax.random.normal(ks[1], (E, H), dtype=f32) * WSCALE, 'w_gate': jax.random.normal(ks[2], (E, H, I), dtype=f32) * WSCALE, 'w_up': jax.random.normal(ks[3], (E, H, I), dtype=f32) * WSCALE, 'w_down': jax.random.normal(ks[4], (E, I, H), dtype=f32) * WSCALE, 'sw_gate': jax.random.normal(ks[5], (H, IS), dtype=f32) * WSCALE, 'sw_up': jax.random.normal(ks[6], (H, IS), dtype=f32) * WSCALE, 'sw_down': jax.random.normal(ks[7], (IS, H), dtype=f32) * WSCALE, 'shared_gate_w': jax.random.normal(ks[8], (H, 1), dtype=f32) * WSCALE}
    _L0_ffn_in = _L0_ffn_setup()
    _d = {'L0_attn_x': _L0_attn_in['x'], 'L0_attn_Wq': _L0_attn_in['Wq'], 'L0_attn_Wk': _L0_attn_in['Wk'], 'L0_attn_Wv': _L0_attn_in['Wv'], 'L0_attn_Wo': _L0_attn_in['Wo'], 'L0_attn_Wb': _L0_attn_in['Wb'], 'L0_ffn_gate_w': _L0_ffn_in['gate_w'], 'L0_ffn_w_gate': _L0_ffn_in['w_gate'], 'L0_ffn_w_up': _L0_ffn_in['w_up'], 'L0_ffn_w_down': _L0_ffn_in['w_down'], 'L0_ffn_sw_gate': _L0_ffn_in['sw_gate'], 'L0_ffn_sw_up': _L0_ffn_in['sw_up'], 'L0_ffn_sw_down': _L0_ffn_in['sw_down'], 'L0_ffn_shared_gate_w': _L0_ffn_in['shared_gate_w']}
    _x0 = _d['L0_attn_x']
    _d['L0_attn_x'] = jax.random.normal(jax.random.fold_in(jax.random.key(seed), 1), (4, 1024, 256), dtype=_x0.dtype)
    del _x0
    return _d

def reference(L0_attn_x, L0_attn_Wq, L0_attn_Wk, L0_attn_Wv, L0_attn_Wo, L0_attn_Wb, L0_ffn_gate_w, L0_ffn_w_gate, L0_ffn_w_up, L0_ffn_w_down, L0_ffn_sw_gate, L0_ffn_sw_up, L0_ffn_sw_down, L0_ffn_shared_gate_w):

    def _L0_attn_ref(x, Wq, Wk, Wv, Wo, Wb):
        import jax, jax.numpy as jnp
        import numpy as np
        B, N, D, H = (2, 256, 256, 16)
        HD = D // H
        CHUNK = 64
        BASE = 10000.0

        def _l2norm(x, eps=1e-06):
            return x * jax.lax.rsqrt(jnp.sum(x * x, axis=-1, keepdims=True) + eps)

        def _rope(x):
            n, d = (x.shape[1], x.shape[-1])
            inv = 1.0 / BASE ** (jnp.arange(0, d, 2, dtype=jnp.float32) / d)
            th = jnp.arange(n, dtype=jnp.float32)[:, None] * inv
            cos = jnp.cos(th)[None, :, None, :]
            sin = jnp.sin(th)[None, :, None, :]
            x1, x2 = jnp.split(x, 2, axis=-1)
            return jnp.concatenate([x1 * cos - x2 * sin, x1 * sin + x2 * cos], axis=-1)

        def _kernel_regression(k, v, beta):
            b, n, h, dk = k.shape
            dv = v.shape[-1]
            nc = n // CHUNK
            Kc = k.reshape(b, nc, CHUNK, h, dk).transpose(1, 0, 3, 2, 4)
            Vc = v.reshape(b, nc, CHUNK, h, dv).transpose(1, 0, 3, 2, 4)
            Bc = beta.reshape(b, nc, CHUNK, h).transpose(1, 0, 3, 2)
            eye = jnp.eye(CHUNK, dtype=k.dtype)

            def step(S, inp):
                K, V, bt = inp
                A = jnp.tril(jnp.einsum('bhik,bhjk->bhij', K, K) * bt[:, :, None, :], -1)
                rhs = V - jnp.einsum('bhck,bhkv->bhcv', K, S)
                Vn = jax.scipy.linalg.solve_triangular(eye + A, rhs, lower=True)
                S = S + jnp.einsum('bhck,bhcv->bhkv', K * bt[..., None], Vn)
                return (S, Vn)
            S0 = jnp.zeros((b, h, dk, dv), k.dtype)
            S, Vn = jax.lax.scan(step, S0, (Kc, Vc, Bc))
            v_new = Vn.transpose(1, 0, 3, 2, 4).reshape(b, n, h, dv)
            return (v_new, S)
        b, n, d = x.shape
        q = (x @ Wq).reshape(b, n, H, HD)
        k = _l2norm((x @ Wk).reshape(b, n, H, HD))
        v = (x @ Wv).reshape(b, n, H, HD)
        beta = 2.0 * jax.nn.sigmoid(x @ Wb)
        q = _rope(q)
        k = _rope(k)
        v, _state = _kernel_regression(k, v, beta)
        k = k * beta[..., None]
        scale = HD ** (-0.5)
        scores = jnp.einsum('bqhd,bkhd->bhqk', q, k) * scale
        mask = jnp.tril(jnp.ones((n, n), bool))
        scores = jnp.where(mask, scores, -jnp.inf)
        attn = jax.nn.softmax(scores, axis=-1)
        out = jnp.einsum('bhqk,bkhd->bqhd', attn, v).reshape(b, n, d)
        return out @ Wo

    def _L0_ffn_ref(hidden_states, gate_w, w_gate, w_up, w_down, sw_gate, sw_up, sw_down, shared_gate_w):
        import jax, jax.numpy as jnp
        import numpy as np
        B, S, H = (2, 128, 256)
        E, K = (8, 2)
        I = 176
        IS = 704
        WSCALE = 0.02
        x = hidden_states
        logits = jnp.einsum('bsh,eh->bse', x, gate_w)
        probs = jax.nn.softmax(logits, axis=-1)
        top_w, top_i = jax.lax.top_k(probs, K)
        top_w = top_w / jnp.sum(top_w, axis=-1, keepdims=True)
        onehot = jax.nn.one_hot(top_i, E, dtype=x.dtype)
        combine = jnp.einsum('bsk,bske->bse', top_w, onehot)
        g = jnp.einsum('bsh,ehi->besi', x, w_gate)
        u = jnp.einsum('bsh,ehi->besi', x, w_up)
        h = jax.nn.silu(g) * u
        expert_out = jnp.einsum('besi,eih->besh', h, w_down)
        moe_out = jnp.einsum('besh,bse->bsh', expert_out, combine)
        sh = jax.nn.silu(x @ sw_gate) * (x @ sw_up)
        shared_out = sh @ sw_down
        shared_gate = jax.nn.sigmoid(x @ shared_gate_w)
        return moe_out + shared_out * shared_gate
    x = L0_attn_x
    x = x + _L0_attn_ref(_layernorm(x, axis=-1), L0_attn_Wq, L0_attn_Wk, L0_attn_Wv, L0_attn_Wo, L0_attn_Wb)
    x = x + _L0_ffn_ref(_layernorm(x, axis=-1), L0_ffn_gate_w, L0_ffn_w_gate, L0_ffn_w_up, L0_ffn_w_down, L0_ffn_sw_gate, L0_ffn_sw_up, L0_ffn_sw_down, L0_ffn_shared_gate_w)
    return x

_drawn_inputs = setup_inputs


def setup_inputs(seed=0):
    import zlib

    import numpy as np

    out = dict(_drawn_inputs(seed))
    spreads = {}
    factors = {'L0_attn_Wq': 8.0,
     'L0_attn_Wk': 8.0,
     'L0_attn_Wv': 5.362,
     'L0_attn_Wo': 5.289,
     'L0_attn_Wb': 8.0,
     'L0_ffn_gate_w': 6.52,
     'L0_ffn_w_gate': 5.739,
     'L0_ffn_w_up': 5.682,
     'L0_ffn_w_down': 5.671,
     'L0_ffn_sw_gate': 4.016,
     'L0_ffn_sw_up': 3.976,
     'L0_ffn_sw_down': 3.986,
     'L0_ffn_shared_gate_w': 8.0}
    for name, (base, spread) in spreads.items():
        noise = np.random.default_rng([zlib.crc32(name.encode()), seed]).standard_normal(out[name].shape)
        drawn = base * np.exp(spread * noise) if base else spread * noise
        out[name] = jnp.asarray(drawn.astype(out[name].dtype))
    for name, factor in factors.items():
        out[name] = (out[name] * factor).astype(out[name].dtype)
    return out
```

```python
from contextlib import ExitStack

import concourse.bass as bass
import numpy as np
from concourse import mybir
from concourse.alu_op_type import AluOpType as ALU

F32 = mybir.dt.float32
BF16 = mybir.dt.bfloat16
ACT = mybir.ActivationFunctionType
AX = mybir.AxisListType.X

P = 128
NB, N, D, H, HD = 4, 1024, 256, 16, 16
CT = 32
NC = N // CT
SUB = 16
NQ = N // P
NG = H // 4
E, I, IS = 8, 176, 704
IT = E * I + IS
NI = -(-IT // P)
LAST = IT - P * (NI - 1)
GP = 4
TG = 512
NTG = NB * N // TG
HALF = D // 2
TERMS = 6
QROWS = TERMS * HD
SROWS = QROWS + 3
NEG = -1.0e30
Q_PARTS = (0, 0, 1, 1, 2, 0)
K_PARTS = (0, 1, 0, 1, 0, 2)


class Memory:
    pass


def flat(ap):
    return ap.rearrange("p a b -> p (a b)")


def bc(ap, axis, n):
    shape = list(ap.shape)
    shape.insert(axis, n)
    return ap.unsqueeze(axis).broadcast_to(shape)


def hold(engine, semaphore, value, held):
    engine.wait_ge(semaphore, value)
    engine.sem_inc(held, 1)


def load_constants(nc, m):
    loads = [
        (m.cosq[:], m.c_cos), (m.sinq[:], m.c_sin), (m.ident[:], m.c_ident),
        (m.rowmask[:], m.c_rowmask), (m.pairmask[:], m.c_pairmask),
        (m.w_in[:, :, 0:D], m.Wq.rearrange("(k p) n -> p k n", p=P)),
        (m.w_in[:, :, D:2 * D], m.Wk.rearrange("(k p) n -> p k n", p=P)),
        (m.w_in[:, :, 2 * D:3 * D], m.Wv.rearrange("(k p) n -> p k n", p=P)),
        (m.w_in[:, :, 3 * D:3 * D + H], m.Wb.rearrange("(k p) n -> p k n", p=P)),
    ]
    with nc.Block() as block:

        @block.sync
        def _(sp):
            for k in range(4):
                for b in range(NB):
                    sp.dma_start(m.x[32 * b:32 * b + 32, 8 * k:8 * k + 8, :],
                                 m.x_in[b].rearrange("(c i) d -> i c d", i=CT)[:, 8 * k:8 * k + 8, :]) \
                        .then_inc(m.x_loaded[k], 16)

        @block.scalar
        def _(act):
            for dst, src in loads:
                act.dma_start(dst, src).then_inc(m.const_loaded, 16)
            act.wait_ge(m.ln_ready, NC + 2)
            nc.scalar.activation(m.rstd[:], m.rstd[:], ACT.Sqrt).then_inc(m.ln_sqrt, 1)

        @block.vector
        def _(dve):
            for semaphore, value in m.starts:
                dve.sem_inc(semaphore, value)
            dve.wait_ge(m.const_loaded, 16 * len(loads))
            nc.vector.tensor_copy(m.ident16[:], m.ident[:]).then_inc(m.const_done, 1)
            for c in range(NC):
                if c % 8 == 0:
                    dve.wait_ge(m.x_loaded[c // 8], 16 * NB)
                nc.vector.bn_stats(m.stats[:, c, :], m.x[:, c, :]).then_inc(m.bn_done, 1)
            for c in range(NC):
                dve.wait_ge(m.bn_done, c + 1)
                nc.vector.bn_aggr(m.mv[:, c, :], m.stats[:, c, :]).then_inc(m.ln_ready, 1)
            dve.wait_ge(m.ln_ready, NC)
            nc.vector.tensor_scalar(m.rstd[:], m.mv[:, :, 1], 1e-5, None, ALU.add).then_inc(m.ln_ready, 1)
            nc.vector.tensor_copy(m.mean[:], m.mv[:, :, 0]).then_inc(m.ln_ready, 1)
            dve.wait_ge(m.ln_sqrt, 1)
            nc.vector.reciprocal(m.rstd[:], m.rstd[:]).then_inc(m.ln_done, 1)


def projections(nc, m):
    bank = m.bank
    with nc.Block() as block:

        @block.vector
        def _(dve):
            with dve.Fori(0, NC // 2) as cc:
                for u in range(2):
                    c = cc * 2 + u
                    dve.wait_ge(m.p_xt, c + 1)
                    nc.vector.tensor_scalar(
                        m.xn[:, u, :], m.x[:, bass.ds(c, 1), :].rearrange("p a d -> p (a d)"),
                        m.mean[:, bass.ds(c, 1)], m.rstd[:, bass.ds(c, 1)],
                        ALU.subtract, ALU.mult).then_inc(m.p_xn, 1)
                    dve.wait_ge(m.p_qk, c + 1)
                    dve.wait_ge(m.p_rope, c + 1)
                    qk = bank(2 + u)[:, 0:2 * D].rearrange("p (h w e) -> p h w e", h=2 * H, w=2)
                    for w in range(2):
                        cos = bc(m.cosq[:, bass.ds(c, 1), :].rearrange("p a e -> p (a e)"), 1, 2 * H)
                        sin = bc(m.sinq[:, bass.ds(c, 1), :].rearrange("p a e -> p (a e)"), 1, 2 * H)
                        nc.vector.tensor_tensor(m.rc[:, u, :, w, :], qk[:, :, w, :], cos, ALU.mult).then_inc(m.p_rot, 1)
                        nc.vector.tensor_tensor(m.rs[:, u, :, w, :], qk[:, :, 1 - w, :], sin, ALU.mult).then_inc(m.p_rot, 1)

        @block.gpsimd
        def _(pool):
            with pool.Fori(0, NC // 2) as cc:
                for u in range(2):
                    c = cc * 2 + u
                    pool.wait_ge(m.p_rot, 4 * c + 9)
                    for i in range(2):
                        out = (m.q[:, bass.ds(c, 1), :] if i == 0 else m.kv[:, bass.ds(c, 1), 0, :]) \
                            .rearrange("p a (h w e) -> p (a h) w e", h=H, w=2)
                        hs = slice(H * i, H * i + H)
                        for w, op in ((0, ALU.subtract), (1, ALU.add)):
                            last = nc.gpsimd.tensor_tensor(
                                out[:, :, w, :], m.rc[:, u, hs, w, :], m.rs[:, u, hs, w, :], op)
                    last.then_inc(m.p_rope, 1)

        @block.tensor
        def _(pe):
            with pe.Fori(0, NC // 2) as cc:
                for u in range(2):
                    c = cc * 2 + u
                    pe.wait_ge(m.p_xn, c + 1)
                    pe.wait_ge(m.p_xte, c + 1)
                    for k in range(2):
                        last = nc.tensor.transpose(bank(0)[:, k * P:(k + 1) * P],
                                                   m.xn[:, u, k * P:(k + 1) * P], m.ident[:])
                    last.then_inc(m.p_xt, 1)
                    pe.wait_ge(m.p_xte, c + 2)
                    pe.wait_ge(m.p_rot, 4 * c + 1)
                    pe.wait_ge(m.p_v, c + 1)
                    for k in range(2):
                        nc.tensor.matmul(bank(2 + u)[:, 0:2 * D], m.xnt[:, u, k, :], m.w_in[:, k, 0:2 * D],
                                         start=k == 0, stop=k == 1)
                    for k in range(2):
                        last = nc.tensor.matmul(bank(4)[:, 0:D + H], m.xnt[:, u, k, :],
                                                m.w_in[:, k, 2 * D:3 * D + H], start=k == 0, stop=k == 1)
                    last.then_inc(m.p_qk, 1)

        @block.scalar
        def _(act):
            with act.Fori(0, NC // 2) as cc:
                for u in range(2):
                    c = cc * 2 + u
                    act.wait_ge(m.p_xt, c + 2)
                    nc.scalar.copy(flat(m.xnt[:, u, :, :]), bank(0)[:, 0:D]).then_inc(m.p_xte, 1)
                    act.wait_ge(m.p_qk, c + 1)
                    nc.scalar.copy(m.kv[:, bass.ds(c, 1), 1, :].rearrange("p a d -> p (a d)"), bank(4)[:, 0:D])
                    nc.scalar.copy(m.beta[:, bass.ds(c, 1), :].rearrange("p a h -> p (a h)"),
                                   bank(4)[:, D:D + H]).then_inc(m.p_v, 1)


def normalise_keys(nc, m):
    k_all = m.kv[:, :, 0, :].rearrange("p c (h e) -> p c h e", h=H)
    with nc.Block() as block:

        @block.vector
        def _(dve):
            nc.vector.tensor_scalar(m.q[:, :, :], m.q[:, :, :], HD ** -0.5, None, ALU.mult).then_inc(m.k_q, 1)
            sq = m.sq[:].rearrange("p c (h e) -> p c h e", h=H)
            for j in range(4):
                cs = slice(8 * j, 8 * j + 8)
                nc.vector.tensor_tensor(m.sq[:, cs, :], m.kv[:, cs, 0, :], m.kv[:, cs, 0, :],
                                        ALU.mult).then_inc(m.k_sq, 1)
            for j in range(4):
                cs = slice(8 * j, 8 * j + 8)
                dve.wait_ge(m.k_sq, j + 1)
                nc.vector.tensor_reduce(m.rn[:, cs, :], sq[:, cs], AX, ALU.add).then_inc(m.k_ss, 1)
            dve.wait_ge(m.k_ss, 4)
            nc.vector.tensor_scalar(m.rn[:], m.rn[:], 1e-6, None, ALU.add).then_inc(m.k_ss, 1)
            dve.wait_ge(m.k_sqrt, 1)
            nc.vector.reciprocal(m.rn[:], m.rn[:]).then_inc(m.k_ss, 1)
            dve.wait_ge(m.k_sqrt, 2)
            nc.vector.tensor_scalar(m.beta[:], m.beta[:], 1.0, None, ALU.add).then_inc(m.k_beta, 1)
            dve.wait_ge(m.k_beta, 1)
            nc.vector.reciprocal(m.beta[:], m.beta[:]).then_inc(m.k_beta, 1)
            dve.wait_ge(m.k_beta, 2)
            nc.vector.tensor_scalar(m.beta[:], m.beta[:], 2.0, None, ALU.mult).then_inc(m.k_beta, 1)
            dve.wait_ge(m.k_ss, 6)
            for j in range(4):
                cs = slice(8 * j, 8 * j + 8)
                for c in range(8 * j, 8 * j + 8):
                    last = nc.vector.tensor_tensor(k_all[:, c], k_all[:, c], bc(m.rn[:, c, :], 2, HD), ALU.mult)
                last.then_inc(m.k_norm, 1)
            dve.wait_ge(m.k_beta, 3)
            for s in range(2):
                nc.vector.tensor_scalar(m.beta_half[:, s, :], m.beta[:].rearrange("p c h -> p (c h)"),
                                        m.rowmask[:, s:s + 1], None, ALU.mult).then_inc(m.k_beta, 1)
            nc.vector.transpose(m.beta_lane[:], m.beta[:].rearrange("p c h -> p (c h)")).then_inc(m.k_lane, 1)
            dve.wait_ge(m.k_lane, 1)
            nc.vector.tensor_scalar(m.beta_lane[:], m.beta_lane[:], -1.0, None, ALU.mult).then_inc(m.k_lane, 1)

        @block.scalar
        def _(act):
            act.wait_ge(m.k_ss, 5)
            nc.scalar.activation(m.rn[:], m.rn[:], ACT.Sqrt).then_inc(m.k_sqrt, 1)
            nc.scalar.activation(m.beta[:], m.beta[:], ACT.Exp, scale=-1.0).then_inc(m.k_sqrt, 1)

        @block.gpsimd
        def _(pool):
            pool.wait_ge(m.k_beta, 3)
            for j in range(4):
                pool.wait_ge(m.k_norm, j + 1)
                for c in range(8 * j, 8 * j + 8):
                    last = nc.gpsimd.tensor_tensor(
                        m.sq[:, c, :].rearrange("p (h e) -> p h e", h=H), k_all[:, c],
                        bc(m.beta[:, c, :], 2, HD), ALU.mult)
                last.then_inc(m.k_kb, 1)

        @block.sync
        def _(sp):
            sp.wait_ge(m.k_q, 1)
            sp.dma_start(m.q_dram, m.q[:]).then_inc(m.k_stored, 16)
            for j in range(4):
                sp.wait_ge(m.k_kb, j + 1)
                sp.dma_start(m.kb_dram[:, 8 * j:8 * j + 8, :], m.sq[:, 8 * j:8 * j + 8, :]).then_inc(m.k_stored, 16)
            sp.wait_ge(m.k_stored, 16 * 5)


def triangular_inverses(nc, m):
    bank = m.bank
    solve_steps = 2 + 4 * (SUB - 1)

    with nc.Block() as block:

        @block.gpsimd
        def _(pool):
            with pool.Fori(0, NC // 2 // GP) as gg:
                for i in range(2 * GP):
                    c = gg * (2 * GP) + i
                    hold(pool, m.g_kt, c + 1, m.held_pool)
                    nc.gpsimd.tensor_copy(m.kc[:], m.kv[:, bass.ds(c, 1), 0, :].rearrange("p a d -> p (a d)")) \
                        .then_inc(m.g_kc, 1)
                hold(pool, m.x_back, gg * GP + GP + 1, m.held_pool)
                nc.gpsimd.tensor_copy(m.xt[:, bass.ds(gg * GP, GP), :], m.xb[:]).then_inc(m.x_copy, 1)

        @block.tensor
        def _(pe):
            with pe.Fori(0, NC) as c:
                pe.wait_ge(m.g_kc, c + 1)
                pe.wait_ge(m.g_kt1, c + 1)
                for k in range(2):
                    last = nc.tensor.transpose(bank(0)[:, k * P:(k + 1) * P], m.kc[:, k * P:(k + 1) * P], m.ident[:])
                last.then_inc(m.g_kt, 1)
                pe.wait_ge(m.g_kt2, 2 * c + 2)
                hold(pe, m.g_out, 2 * c + 1, m.held)
                for k in range(2):
                    for b in range(NB):
                        for j in range(4):
                            r = slice(32 * j, 32 * j + 32)
                            out = bank(4 + j)[32 * b:32 * b + 32, 64 * k:64 * k + 64].rearrange("p (s t) -> p s t", s=2)
                            last = nc.tensor.matmul(out, m.kt1[r, k, 32 * b:32 * b + 32],
                                                    m.kt2[r, :, k, 32 * b:32 * b + 32], start=True, stop=True)
                last.then_inc(m.g_mm, 1)

        @block.scalar
        def _(act):
            with act.Fori(0, NC // 2) as g:
                for u in range(2):
                    c = g * 2 + u
                    act.wait_ge(m.g_kt, c + 2)
                    act.wait_ge(m.g_mm, c + 1)
                    nc.scalar.copy(flat(m.kt1[:]), bank(0)[:, 0:D]).then_inc(m.g_kt1, 1)
                    act.wait_ge(m.g_kt1, c + 2)
                    for s in range(2):
                        nc.scalar.activation(flat(m.kt2[:, s, :, :]), flat(m.kt1[:]), ACT.Copy,
                                             scale=m.pairmask[:, 32 + s:33 + s]).then_inc(m.g_kt2, 1)
                    act.wait_ge(m.g_mm, c + 2)
                    if u == 0:
                        act.wait_ge(m.g_tr, g + 1)
                    for k in range(2):
                        src = m.psum[:, 4:8, 64 * k:64 * k + 64].rearrange("p j (s t) -> p j s t", s=2)
                        dst = m.gs[:].rearrange("p (t u k j s) -> p u k j s t", t=32, u=2, k=2, j=4)[:, u, k]
                        nc.scalar.copy(dst, src).then_inc(m.g_out, 1)

        @block.vector
        def _(dve):
            xl = m.xl[:].rearrange("p g (i k) -> p g i k", i=32)
            gram = m.gram[:].rearrange("p (j i) -> p i j", j=32)
            with dve.Fori(0, NC // 2 // GP) as gg:
                n = 0
                base = gg * solve_steps
                dve.wait_ge(m.x_back, gg * GP + 1)
                nc.vector.memset(m.xl[:], 0.0).then_inc(m.solve, 1)
                n += 1
                dve.wait_ge(m.solve, base + n)
                nc.vector.memset(m.xl[:, :, 0:1024:33], 1.0).then_inc(m.solve, 1)
                n += 1
                for g in range(GP):
                    dve.wait_ge(m.g_out, gg * (4 * GP) + g * 4 + 5)
                    dve.wait_ge(m.g_an, gg * (2 * GP) + 2 * g + 1)
                    nc.vector.transpose(m.gram[:], m.gs[:]).then_inc(m.g_tr, 1)
                    dve.wait_ge(m.g_tr, gg * GP + g + 2)
                    beta = m.beta_lane[:, bass.ds(gg * GP + g, 1), :].rearrange("p a j -> p (a j)")
                    for s in range(2):
                        r = slice(SUB * s, SUB * s + SUB)
                        nc.vector.tensor_tensor(m.an[:, s, g], gram[:, r, r], bc(beta[:, r], 1, SUB),
                                                ALU.mult).then_inc(m.g_an, 1)
                dve.wait_ge(m.g_an, gg * (2 * GP) + 2 * GP + 1)
                for i in range(1, SUB):
                    for s in range(2):
                        dve.wait_ge(m.solve, base + n - s)
                        r = slice(SUB * s, SUB * s + i)
                        nc.vector.tensor_tensor(m.prod[:, s, :, 0:i, 0:i], bc(m.an[:, s, :, i, 0:i], 2, i),
                                                xl[:, :, r, r].rearrange("p g j k -> p g k j"),
                                                ALU.mult).then_inc(m.solve, 1)
                        n += 1
                    for s in range(2):
                        dve.wait_ge(m.solve, base + n - 1)
                        nc.vector.tensor_reduce(xl[:, :, SUB * s + i, SUB * s:SUB * s + i],
                                                m.prod[:, s, :, 0:i, 0:i], AX, ALU.add).then_inc(m.solve, 1)
                        n += 1
                assert n == solve_steps
                dve.wait_ge(m.solve, base + n)
                dve.wait_ge(m.x_copy, gg + 1)
                for g in range(GP):
                    nc.vector.transpose(m.xb[:, g, :], m.xl[:, g, :]).then_inc(m.x_back, 1)


def recurrence(nc, m):
    bank = m.bank

    def heads_wu(pe, u, hs):
        for h in hs:
            for b in range(NB):
                r = slice(32 * b, 32 * b + 32)
                last = nc.tensor.matmul(bank(b)[r, 32 * h:32 * h + 32].rearrange("p (w e) -> p w e", w=2),
                                        m.xc[r, u, h, :], m.kvc[r, u, :, HD * h:HD * h + HD],
                                        start=True, stop=True)
        return last

    def transpose_w(pe, c, u):
        pe.wait_ge(m.r_wu, 4 * c + 4)
        for k in range(2):
            last = nc.tensor.transpose(bank(0)[:, k * P:(k + 1) * P], m.wu[:, u, 0, k * P:(k + 1) * P], m.ident[:])
        last.then_inc(m.r_wt_mm, 1)

    def steps(pe, c, u, more):
        pe.wait_ge(m.r_wt, c + 1)
        if more:
            pe.wait_ge(m.r_xc, 2 * c + 4)
        parts = [range(0, 6), range(6, 11), range(11, 16)]
        for s in range(2):
            hold(pe, m.r_s, 2 * c + s + 1, m.held)
            for b in range(NB):
                for k in range(2):
                    for j in range(4):
                        r = slice(32 * j, 32 * j + 32)
                        last = nc.tensor.matmul(bank(4 + j)[32 * b:32 * b + 32, 32 * k:32 * k + 32],
                                                m.wt[r, u, k, 32 * b:32 * b + 32], m.s[r, b, k, :],
                                                start=True, stop=True)
            last.then_inc(m.r_ws, 1)
            if more:
                last = heads_wu(pe, 1 - u, parts[2 * s])
                if s == 1:
                    last.then_inc(m.r_wu_mm, 1)
            pe.wait_ge(m.r_vn, 2 * c + s + 1)
            hold(pe, m.r_kb, 2 * c + s + 1, m.held)
            for k in range(2):
                for j in range(4):
                    for b in range(NB):
                        r = slice(32 * b, 32 * b + 32)
                        f = slice(k * P + 32 * j, k * P + 32 * j + 32)
                        last = nc.tensor.matmul(bank(4 + b)[32 * j:32 * j + 32, 64 + 32 * k:96 + 32 * k],
                                                m.kb[r, s, f], m.vn[r, s, f], start=True, stop=True)
            last.then_inc(m.r_ds, 1)
            if more and s == 0:
                heads_wu(pe, 1 - u, parts[1])
        if more:
            transpose_w(pe, c + 1, 1 - u)

    with nc.Block() as block:

        @block.gpsimd
        def _(pool):
            def fetch(g, u):
                x_t = m.xt[:, bass.ds(g, 1), :].rearrange("p a (i u h) -> p a u h i", i=32, u=2)
                nc.gpsimd.tensor_copy(m.xc[:, u], x_t[:, 0, u]).then_inc(m.r_xc, 1)

            def body(g, u, more):
                c = g * 2 + u
                for s in range(2):
                    pool.wait_ge(m.r_ds, 2 * c + s + 1)
                    nc.gpsimd.tensor_tensor(
                        m.kb[:, s].rearrange("p (h e) -> p h e", h=H),
                        m.kv[:, bass.ds(c, 1), 0, :].rearrange("p a (h e) -> p (a h) e", h=H),
                        bc(m.beta_half[:, s, bass.ds(c * H, H)], 2, HD), ALU.mult).then_inc(m.r_kb, 1)
                if more:
                    pool.wait_ge(m.r_wu_mm, c + 1)
                    fetch(g + 1, u)
                    nc.gpsimd.tensor_copy(m.kvc[:, u], m.kv[:, bass.ds(c + 2, 1), :, :].rearrange("p a w d -> p (a w) d")) \
                        .then_inc(m.r_xc, 1)
                for s in range(2):
                    hold(pool, m.r_vn, 2 * c + s + 1, m.held_pool)
                    if s == 0:
                        hold(pool, m.r_v, c + 1, m.held_pool)
                    nc.gpsimd.tensor_tensor(m.vt[:, s], m.vn[:, s], m.rowmask[:, s:s + 1].broadcast_to([P, D]),
                                            ALU.mult).then_inc(m.r_vo, 1)
                hold(pool, m.r_vo, 2 * c + 4, m.held_pool)
                nc.gpsimd.tensor_tensor(m.v[:, bass.ds(c, 1), :].rearrange("p a d -> p (a d)"), m.vt[:, 0], m.vt[:, 1],
                                        ALU.add).then_inc(m.r_v, 1)

            for u in range(2):
                fetch(0, u)
                nc.gpsimd.tensor_copy(m.kvc[:, u], m.kv[:, u]).then_inc(m.r_xc, 1)
            with pool.Fori(0, NC // 2 - 1) as g:
                for u in range(2):
                    body(g, u, True)
            for u in range(2):
                body(NC // 2 - 1, u, False)

        @block.tensor
        def _(pe):
            pe.wait_ge(m.r_xc, 2)
            heads_wu(pe, 0, range(H)).then_inc(m.r_wu_mm, 1)
            transpose_w(pe, 0, 0)
            with pe.Fori(0, NC // 2 - 1) as g:
                for u in range(2):
                    steps(pe, g * 2 + u, u, True)
            for u in range(2):
                steps(pe, NC - 2 + u, u, u == 0)

        @block.scalar
        def _(act):
            def body(c, u, first=False):
                act.wait_ge(m.r_wu_mm, c + 1)
                if not first:
                    act.wait_ge(m.r_vn, 2 * c - 2)
                for b in range(NB):
                    r = slice(32 * b, 32 * b + 32)
                    nc.scalar.copy(m.wu[r, u].rearrange("p w (h e) -> p w h e", h=H),
                                   bank(b)[r, :].rearrange("p (h w e) -> p w h e", h=H, w=2)).then_inc(m.r_wu, 1)
                act.wait_ge(m.r_wt_mm, c + 1)
                if not first:
                    act.wait_ge(m.r_ws, 2 * c - 2)
                nc.scalar.copy(flat(m.wt[:, u]), bank(0)[:, 0:D]).then_inc(m.r_wt, 1)

            body(0, 0, True)
            body(1, 1)
            with act.Fori(1, NC // 2) as g:
                for u in range(2):
                    body(g * 2 + u, u)

        @block.vector
        def _(dve):
            nc.vector.memset(m.s[:], 0.0).then_inc(m.r_s, 1)
            with dve.Fori(0, NC // 2) as g:
                for u in range(2):
                    c = g * 2 + u
                    dve.wait_ge(m.r_wu, 4 * c + 4)
                    for s in range(2):
                        dve.wait_ge(m.r_ws, 2 * c + s + 1)
                        dve.wait_ge(m.r_vo, 2 * c + s + 1)
                        split = "p (k j e) -> p k j e"
                        nc.vector.tensor_tensor(
                            m.vn[:, s].rearrange(split, k=2, j=4), m.wu[:, u, 1].rearrange(split, k=2, j=4),
                            m.psum[:, 4:8, 0:64].rearrange("p j (k e) -> p k j e", k=2),
                            ALU.subtract).then_inc(m.r_vn, 1)
                        dve.wait_ge(m.r_ds, 2 * c + s + 3)
                        nc.vector.tensor_tensor(
                            m.ds[:], m.psum[:, 4:8, 64:128].rearrange("p b (k e) -> p b k e", k=2),
                            bc(bc(m.pairmask[:, 0:32], 1, 2), 1, NB), ALU.mult).then_inc(m.r_dsm, 1)
                        dve.wait_ge(m.r_dsm, 2 * c + s + 1)
                        nc.vector.tensor_tensor(m.s[:], m.s[:], m.ds[:], ALU.add).then_inc(m.r_s, 1)

        @block.sync
        def _(sp):
            sp.wait_ge(m.r_v, NC + 1)
            sp.dma_start(m.v_dram, m.v[:]).then_inc(m.r_stored, 16)
            sp.wait_ge(m.r_stored, 16)



def split_and_stack(wait, engine, stack, x, rest, parts, done, base):
    term = [[t for t in range(TERMS) if parts[t] == k] for k in range(3)]
    n = 0
    for k in range(3):
        out = stack[:, :, term[k][0], :]
        source = x if k == 0 else rest
        if n:
            wait(done, base + n)
        engine.tensor_copy(out, source).then_inc(done, 1)
        n += 1
        wait(done, base + n)
        if k < 2:
            engine.tensor_tensor(rest, source, out, ALU.subtract).then_inc(done, 1)
            n += 1
        for t in term[k][1:]:
            engine.tensor_copy(stack[:, :, t, :], out).then_inc(done, 1)
            n += 1
    return n


STACK_STEPS = 3 + 2 + 3


def attention_operands(nc, m, seq):
    bank16 = m.bank16
    with nc.Block() as block:

        @block.sync
        def _(sp):
            for i, (dst, src) in enumerate(((m.kn, m.kb_dram), (m.qn, m.q_dram), (m.vn2, m.v_dram))):
                for cc in range(4):
                    rows = src.rearrange("(b i) (t c) d -> c b i t d", b=NB, c=4)[cc, bass.ds(seq, 1)]
                    sp.dma_start(dst[32 * cc:32 * cc + 32], rows.rearrange("b i t d -> (b i) t d")) \
                        .then_inc(m.a_loaded[i], 16)
            hold(sp, m.a_loaded[2], seq * 64 + 64, m.held_sp)

        @block.vector
        def _(dve):
            dve.wait_ge(m.a_loaded[0], seq * 64 + 64)
            split_and_stack(dve.wait_ge, nc.vector, m.stage_k[:].rearrange("p t h r e -> p (t h) r e"),
                            m.kn[:].rearrange("p t (h e) -> p (t h) e", h=H),
                            m.rest_k[:].rearrange("p (t e) -> p t e", e=HD), K_PARTS, m.a_k, seq * STACK_STEPS)
            for n in range(2 * NQ):
                t, hh = divmod(n, 2)
                dve.wait_ge(m.a_kt, seq * 16 + n + 1)
                nc.vector.tensor_copy(m.ks[0:QROWS, 8 * hh:8 * hh + 8, P * t:P * t + P],
                                      bank16(4 + n % 4)[0:QROWS, :].rearrange("p (h t) -> p h t", h=8)) \
                    .then_inc(m.a_ke, 1)

        @block.gpsimd
        def _(pool):
            hold(pool, m.a_loaded[1], seq * 64 + 64, m.held_pool)
            split_and_stack(lambda a, b: hold(pool, a, b, m.held_pool), nc.gpsimd, m.stage_q[:].rearrange("p t h r e -> p (t h) r e"),
                            m.qn[:].rearrange("p t (h e) -> p (t h) e", h=H),
                            m.rest_q[:].rearrange("p (t e) -> p t e", e=HD), Q_PARTS, m.a_q, seq * STACK_STEPS)

        @block.scalar
        def _(act):
            for n in range(2 * NQ):
                t, hh = divmod(n, 2)
                act.wait_ge(m.a_qt, seq * 16 + n + 1)
                nc.scalar.copy(m.qs[0:QROWS, 8 * hh:8 * hh + 8, P * t:P * t + P],
                               bank16(n % 4)[0:QROWS, :].rearrange("p (h t) -> p h t", h=8)).then_inc(m.a_qe, 1)

        @block.tensor
        def _(pe):
            for stage, first, staged, turned, read in ((m.stage_k, 4, m.a_k, m.a_kt, m.a_ke),
                                                       (m.stage_q, 0, m.a_q, m.a_qt, m.a_qe)):
                pe.wait_ge(staged, (seq + 1) * STACK_STEPS)
                for n in range(2 * NQ):
                    t, hh = divmod(n, 2)
                    if n >= 4:
                        pe.wait_ge(read, seq * 16 + n - 3)
                    for h in range(8):
                        last = nc.tensor.transpose(bank16(first + n % 4)[0:QROWS, P * h:P * h + P],
                                                   stage[:, t, 8 * hh + h].rearrange("p r e -> p (r e)"), m.ident16[:])
                    last.then_inc(turned, 1)


def attention_maxima(nc, m, seq):
    def pair(n):
        return flat(m.psum[:, 2 * (n % 4):2 * (n % 4) + 2, :])

    with nc.Block() as block:

        @block.tensor
        def _(pe):
            with pe.Fori(0, H) as h:
                for t in range(NQ):
                    pe.wait_ge(m.m_max, seq * (H * NQ) + h * NQ + t + 1)
                    out = pair(t)
                    q = m.qs[0:QROWS, bass.ds(h, 1), P * t:P * t + P].rearrange("p a t -> p (a t)")
                    n = P * t + P
                    for a in range(0, n, 512):
                        z = min(a + 512, n)
                        k = m.ks[0:QROWS, bass.ds(h, 1), a:z].rearrange("p a t -> p (a t)")
                        nc.tensor.matmul(out[:, a:z], q, k, start=True, stop=z < n)
                    nc.tensor.matmul(out[:, n - P:n], m.ident16[:], m.mask_qk[:], start=False,
                                     stop=True).then_inc(m.m_s, 1)
            pe.wait_ge(m.m_part, seq * 5 + 5)
            hold(pe, m.m_max, (seq + 1) * (H * NQ) + 4, m.held)
            for t in range(NQ):
                last = nc.tensor.transpose(m.bank16(0)[0:3 * H, P * t:P * t + P],
                                           m.mparts[:, t].rearrange("p r h -> p (r h)"), m.ident16[:])
            last.then_inc(m.m_t, 1)

        @block.vector
        def _(dve):
            with dve.Fori(0, H) as h:
                for t in range(NQ):
                    dve.wait_ge(m.m_s, seq * (H * NQ) + h * NQ + t + 1)
                    nc.vector.tensor_reduce(m.nmax[:, t, bass.ds(h, 1)], pair(t)[:, 0:P * t + P], AX, ALU.max,
                                            negate=True).then_inc(m.m_max, 1)
            dve.wait_ge(m.m_max, (seq + 1) * (H * NQ) + 4)
            n = 0
            for k in range(3):
                nc.vector.tensor_copy(m.mparts[:, :, k, :], m.nmax[:]).then_inc(m.m_part, 1)
                n += 1
                dve.wait_ge(m.m_part, seq * 5 + n)
                if k < 2:
                    nc.vector.tensor_tensor(m.nmax[:], m.nmax[:], m.mparts[:, :, k, :], ALU.subtract) \
                        .then_inc(m.m_part, 1)
                    n += 1
                    dve.wait_ge(m.m_part, seq * 5 + n)
            dve.wait_ge(m.m_t, seq + 1)
            nc.vector.tensor_copy(m.mrows[:], m.bank16(0)[0:3 * H, :]).then_inc(m.m_rows, 1)

        @block.sync
        def _(sp):
            sp.wait_ge(m.m_rows, seq + 1)
            sp.dma_start(m.max_dram, m.mrows[:]).then_inc(m.m_out, 16)
            sp.wait_ge(m.m_out, seq * 16 + 16)
            sp.dma_start(m.qs[QROWS:SROWS], m.max_dram.rearrange("(r h) t -> r h t", r=3)).then_inc(m.m_in, 16)
            hold(sp, m.m_in, seq * 16 + 16, m.held_sp)


def attention_values(nc, m, seq):
    def scores(n):
        return flat(m.psum[:, 2 * (n % 2):2 * (n % 2) + 2, :])

    def sums(u, r, a, z):
        return flat(m.psum[:, 4 + 2 * u:6 + 2 * u, :])[r, a:z]

    with nc.Block() as block:

        @block.gpsimd
        def _(pool):
            with pool.Fori(0, 2) as gp:
                for u in range(2):
                    g = gp * 2 + u
                    pool.wait_ge(m.v_read, seq * NG + g + 1)
                    nc.gpsimd.tensor_copy(
                        m.vg[:, u, :, :, 0:HD],
                        m.vn2[:, :, bass.ds(g * 64, 64)].rearrange("p t (j e) -> p t j e", j=4)).then_inc(m.v_vg, 1)

        @block.tensor
        def _(pe):
            def score(gp, u, kt, j):
                g = gp * 2 + u
                unit = (seq * NG + g) * (4 * NQ) + 4 * kt + j
                h = g * 4 + j
                pe.wait_ge(m.v_exp, unit + 1)
                out = scores(j)
                k = m.ks[0:SROWS, bass.ds(h, 1), P * kt:P * kt + P].rearrange("p a t -> p (a t)")
                cuts = [P * kt, 512, N] if kt < 4 else [P * kt, N]
                for a, z in zip(cuts, cuts[1:]):
                    q = m.qs[0:SROWS, bass.ds(h, 1), a:z].rearrange("p a t -> p (a t)")
                    last = nc.tensor.matmul(out[:, a:z], k, q, start=True, stop=a != P * kt)
                    if a == P * kt:
                        last = nc.tensor.matmul(out[:, a:a + P], m.ident16[:], m.mask_kq[:], start=False, stop=True)
                last.then_inc(m.v_s, 1)

            def values(gp, u, kt, piece):
                g = gp * 2 + u
                a, z = max(512 * piece, P * kt), 512 * piece + 512
                if a >= z:
                    return
                pe.wait_ge(m.v_exp, (seq * NG + g) * (4 * NQ) + 4 * kt + 6)
                if kt == 0:
                    pe.wait_ge(m.v_read, seq * NG + g + 1)
                    pe.wait_ge(m.v_vg, seq * NG + g + 1)
                for j in range(4):
                    last = nc.tensor.matmul(sums(u, slice(32 * j, 32 * j + 32), a, z), m.vg[:, u, kt, j, :],
                                            m.p[:, 4 * (kt % 2) + j, a:z], start=kt == 0,
                                            stop=kt == 4 * piece + 3)
                if piece == 1:
                    last.then_inc(m.v_o, 1)

            with pe.Fori(0, 2) as gp:
                for u in range(2):
                    for kt in range(NQ + 1):
                        for j in range(4):
                            if kt < NQ:
                                score(gp, u, kt, j)
                            if kt > 0 and j in (1, 2):
                                values(gp, u, kt - 1, j - 1)

        @block.scalar
        def _(act):
            with act.Fori(0, 2) as gp:
                for u in range(2):
                    for kt in range(NQ):
                        for j in range(4):
                            g = gp * 2 + u
                            act.wait_ge(m.v_s, (seq * NG + g) * (4 * NQ) + 4 * kt + j + 1)
                            if j == 0:
                                act.wait_ge(m.v_o, (seq * NG + g) * NQ + kt + 1)
                            nc.scalar.activation(m.p[:, 4 * (kt % 2) + j, P * kt:N], scores(j)[:, P * kt:N],
                                                 ACT.Exp).then_inc(m.v_exp, 1)

        @block.vector
        def _(dve):
            with dve.Fori(0, 2) as gp:
                for u in range(2):
                    g = gp * 2 + u
                    dve.wait_ge(m.v_o, (seq * NG + g) * NQ + NQ + 2)
                    nc.vector.tensor_copy(m.ot[:, bass.ds(g, 1), :].rearrange("p a t -> p (a t)"),
                                          sums(u, slice(0, P), 0, N)).then_inc(m.v_read, 1)


def attention_output(nc, m, seq):
    bank = m.bank
    with nc.Block() as block:

        @block.sync
        def _(sp):
            sp.dma_start(m.xres[:], m.x_seq[:, bass.ds(seq * NQ, NQ), :]).then_inc(m.o_x, 16)
            for t in range(NQ):
                sp.wait_ge(m.o_x1, seq * NQ + t + 1)
                sp.dma_start(m.x1_dram[:, bass.ds(seq * NQ + t, 1), :], m.xres[:, t:t + 1, :]).then_inc(m.o_st, 16)
            hold(sp, m.o_st, seq * (16 * NQ) + 16 * NQ, m.held_sp)

        @block.tensor
        def _(pe):
            def turn(t):
                if t >= 2:
                    pe.wait_ge(m.o_n, seq * (2 * NQ) + 2 * t - 2)
                for g in range(NG):
                    last = nc.tensor.transpose(bank(t % 2)[:, P * g:P * g + P], m.ot[:, g, P * t:P * t + P], m.ident[:])
                last.then_inc(m.o_t, 1)

            turn(0)
            for t in range(NQ):
                if t + 1 < NQ:
                    turn(t + 1)
                pe.wait_ge(m.o_n, seq * (2 * NQ) + 2 * t + 2)
                if t >= 2:
                    pe.wait_ge(m.o_te, seq * NQ + t - 1)
                for k in range(2):
                    last = nc.tensor.transpose(bank(2 + t % 2)[:, P * k:P * k + P],
                                               m.on[:, t % 2, P * k:P * k + P], m.ident[:])
                last.then_inc(m.o_tt, 1)
                pe.wait_ge(m.o_te, seq * NQ + t + 1)
                if t >= 2:
                    pe.wait_ge(m.o_x1, seq * NQ + t - 1)
                for k in range(2):
                    last = nc.tensor.matmul(bank(4 + t % 2)[:, 0:D], m.ont[:, t % 2, k, :], m.wo[:, k, :],
                                            start=k == 0, stop=k == 1)
                last.then_inc(m.o_mm, 1)

        @block.scalar
        def _(act):
            for t in range(NQ):
                act.wait_ge(m.o_tt, seq * NQ + t + 1)
                if t >= 2:
                    act.wait_ge(m.o_mm, seq * NQ + t - 1)
                nc.scalar.copy(flat(m.ont[:, t % 2]), bank(2 + t % 2)[:, 0:D]).then_inc(m.o_te, 1)

        @block.vector
        def _(dve):
            def divide(t):
                dve.wait_ge(m.o_t, seq * NQ + t + 1)
                o = bank(t % 2).rearrange("p (h e) -> p h e", h=H)
                nc.vector.reciprocal(m.rsum[:, t % 2], o[:, :, HD]).then_inc(m.o_n, 1)
                dve.wait_ge(m.o_n, seq * (2 * NQ) + 2 * t + 1)
                if t >= 2:
                    dve.wait_ge(m.o_tt, seq * NQ + t - 1)
                nc.vector.tensor_tensor(m.on[:, t % 2].rearrange("p (h e) -> p h e", h=H), o[:, :, 0:HD],
                                        bc(m.rsum[:, t % 2], 2, HD), ALU.mult).then_inc(m.o_n, 1)

            divide(0)
            dve.wait_ge(m.o_x, seq * 16 + 16)
            for t in range(NQ):
                if t + 1 < NQ:
                    divide(t + 1)
                dve.wait_ge(m.o_mm, seq * NQ + t + 1)
                nc.vector.tensor_tensor(m.xres[:, t, :], bank(4 + t % 2)[:, 0:D], m.xres[:, t, :], ALU.add) \
                    .then_inc(m.o_x1, 1)
            for t in range(NQ):
                dve.wait_ge(m.o_x1, seq * NQ + t + 1)
                nc.vector.bn_stats(m.stats2[:, bass.ds(seq * NQ + t, 1), :].rearrange("p a f -> p (a f)"),
                                   m.xres[:, t, :]).then_inc(m.o_bn, 1)


def attention(nc, m):
    with nc.Block() as block:

        @block.sync
        def _(sp):
            sp.dma_start(m.wo[:], m.wo_dram).then_inc(m.a_const, 16)
            sp.dma_start(m.masks[:], m.c_masks).then_inc(m.a_const, 16)

        @block.gpsimd
        def _(pool):
            nc.gpsimd.memset(m.vg[:], 0.0).then_inc(m.a_vg, 1)
            pool.wait_ge(m.a_vg, 1)
            nc.gpsimd.memset(m.vg[:, :, :, :, HD:HD + 1], 1.0)

        @block.vector
        def _(dve):
            nc.vector.memset(m.ks[QROWS:SROWS], 1.0)
            dve.wait_ge(m.a_const, 32)
            nc.vector.tensor_copy(m.mask_qk[:], m.masks[:, 0, :])
            nc.vector.tensor_copy(m.mask_kq[:], m.masks[:, 1, :])

    with nc.Fori(0, NB) as seq:
        attention_operands(nc, m, seq)
        attention_maxima(nc, m, seq)
        attention_values(nc, m, seq)
        attention_output(nc, m, seq)


def second_norm(nc, m):
    bank = m.bank
    with nc.Block() as block:

        @block.sync
        def _(sp):
            loads = [
                (m.gt[:], m.router_w.rearrange("(k p) e -> p k e", p=P)),
                (m.sel32[:], m.c_sel), (m.key[:], m.c_key),
                (m.wg[:, :, E * I:IT], m.sw_gate.rearrange("(k p) i -> p k i", p=P)),
                (m.wu_ffn[:, :, E * I:IT], m.sw_up.rearrange("(k p) i -> p k i", p=P)),
            ]
            for k in range(2):
                for dst, src in ((m.wg, m.w_gate), (m.wu_ffn, m.w_up)):
                    loads.append((dst[:, k, 0:E * I].rearrange("p (e i) -> p e i", e=E),
                                  src.rearrange("e (k p) i -> k p e i", p=P)[k]))
            n = E * I // P
            loads.append((m.wd[:, 0:n, :], m.w_down.rearrange("e i h -> (e i) h").rearrange("(n p) h -> p n h", p=P)))
            loads.append((m.wd[:, n:NI - 1, :], m.sw_down[0:IS - LAST, :].rearrange("(n p) h -> p n h", p=P)))
            loads.append((m.wd[0:LAST, NI - 1, :], m.sw_down[IS - LAST:IS, :]))
            sp.wait_ge(m.f_pad, 3)
            for i, (dst, src) in enumerate(loads):
                sp.dma_start(dst, src).then_inc(m.f_gate if i == 0 else m.f_const, 16)
            with sp.Fori(0, NTG // 2) as ss:
                for u in range(2):
                    sp.wait_ge(m.f_xn, ss * 2 + u + 1)
                    sp.dma_start(m.xg[:, u], m.x1_dram[:, bass.ds(ss * 8 + 4 * u, 4), :]).then_inc(m.f_x[u], 16)
            sp.wait_ge(m.f_const, 16 * (len(loads) - 1))

        @block.vector
        def _(dve):
            nc.vector.memset(m.wg[:, :, IT:], 0.0).then_inc(m.f_pad, 1)
            nc.vector.memset(m.wu_ffn[:, :, IT:], 0.0).then_inc(m.f_pad, 1)
            nc.vector.memset(m.wd[:, NI - 1, :], 0.0).then_inc(m.f_pad, 1)
            for t in range(NB * NQ):
                last = nc.vector.bn_aggr(m.mv[:, t, :], m.stats2[:, t, :])
            last.then_inc(m.f_ln, 1)
            dve.wait_ge(m.f_ln, 1)
            nc.vector.tensor_scalar(m.rstd[:], m.mv[:, :, 1], 1e-5, None, ALU.add).then_inc(m.f_ln, 1)
            nc.vector.tensor_copy(m.mean[:], m.mv[:, :, 0]).then_inc(m.f_ln, 1)
            dve.wait_ge(m.f_sqrt, 1)
            nc.vector.reciprocal(m.rstd[:], m.rstd[:]).then_inc(m.f_ln, 1)
            dve.wait_ge(m.f_ln, 4)
            with dve.Fori(0, NTG // 2) as ss:
                for u in range(2):
                    s = ss * 2 + u
                    dve.wait_ge(m.f_x[u], ss * 16 + 16)
                    dve.wait_ge(m.f_t, s + 1)
                    for q in range(4):
                        last = nc.vector.tensor_scalar(
                            m.xm[:, q, :], m.xg[:, u, q, :], m.mean[:, bass.ds(s * 4 + q, 1)],
                            m.rstd[:, bass.ds(s * 4 + q, 1)], ALU.subtract, ALU.mult)
                    last.then_inc(m.f_xn, 1)
                    dve.wait_ge(m.f_lg, s + 1)
                    nc.vector.tensor_copy(m.lg[:, bass.ds(s * 4, 4), :],
                                          bank(2)[:, 0:4 * (E + 1)].rearrange("p (q e) -> p q e", q=4)) \
                        .then_inc(m.f_lge, 1)

        @block.tensor
        def _(pe):
            pe.wait_ge(m.f_gate, 16)
            with pe.Fori(0, NTG // 2) as ss:
                for u in range(2):
                    s = ss * 2 + u
                    pe.wait_ge(m.f_xn, s + 3)
                    pe.wait_ge(m.f_te, s * 2 + 1)
                    for k in range(2):
                        for q in range(4):
                            last = nc.tensor.transpose(bank(k)[:, P * q:P * q + P], m.xm[:, q, P * k:P * k + P],
                                                       m.ident[:])
                    last.then_inc(m.f_t, 1)
                    pe.wait_ge(m.f_te, s * 2 + 3)
                    pe.wait_ge(m.f_lge, s + 1)
                    for q in range(4):
                        for k in range(2):
                            last = nc.tensor.matmul(bank(2)[:, (E + 1) * q:(E + 1) * (q + 1)],
                                                    m.xs[:, u, k, P * q:P * q + P], m.gt[:, k, :],
                                                    start=k == 0, stop=k == 1)
                    last.then_inc(m.f_lg, 1)

        @block.scalar
        def _(act):
            act.wait_ge(m.f_ln, 3)
            nc.scalar.activation(m.rstd[:], m.rstd[:], ACT.Sqrt).then_inc(m.f_sqrt, 1)
            with act.Fori(0, NTG // 2) as ss:
                for u in range(2):
                    s = ss * 2 + u
                    act.wait_ge(m.f_t, s + 2)
                    act.wait_ge(m.f_copy, s + 1)
                    for k in range(2):
                        nc.scalar.copy(m.xs[:, u, k, :], bank(k)[:]).then_inc(m.f_te, 1)

        @block.gpsimd
        def _(pool):
            with pool.Fori(0, NTG // 2) as ss:
                for u in range(2):
                    s = ss * 2 + u
                    pool.wait_ge(m.f_te, s * 2 + 3)
                    nc.gpsimd.tensor_copy(m.xt2[:, :, bass.ds(s * TG, TG)], m.xs[:, u]).then_inc(m.f_copy, 1)


def router(nc, m):
    NT = NB * NQ
    le, ex, gate = m.lg[:, :, 0:E], m.ex[:], m.lg[:, :, E]
    with nc.Block() as block:

        @block.gpsimd
        def _(pool):
            nc.gpsimd.tensor_copy(m.sel[:], m.sel32[:])

        @block.vector
        def _(dve):
            n = 0

            def step(instruction):
                nonlocal n
                n += 1
                instruction.then_inc(m.t_dve, 1)
                dve.wait_ge(m.t_dve, n)

            key = bc(m.key[:], 1, NT)
            step(nc.vector.tensor_reduce(m.top[:], le, AX, ALU.max))
            step(nc.vector.tensor_tensor(ex, le, bc(m.top[:], 2, E), ALU.subtract))
            dve.wait_ge(m.t_exp, 2)
            step(nc.vector.tensor_reduce(m.top[:], ex, AX, ALU.max))
            step(nc.vector.tensor_copy(m.total[:], m.top[:]))
            step(nc.vector.tensor_copy(m.left[:], ex))
            for rank in range(2):
                step(nc.vector.tensor_tensor(m.hit[:], m.left[:], bc(m.top[:], 2, E), ALU.is_equal))
                step(nc.vector.tensor_tensor(m.hit[:], m.hit[:], key, ALU.mult))
                step(nc.vector.tensor_reduce(m.top[:], m.hit[:], AX, ALU.max))
                step(nc.vector.tensor_tensor(m.hit[:], key, bc(m.top[:], 2, E), ALU.is_equal))
                if rank == 0:
                    step(nc.vector.tensor_copy(m.chosen[:], m.hit[:]))
                    step(nc.vector.scalar_tensor_tensor(m.left[:], m.hit[:], -2.0, m.left[:], ALU.mult, ALU.add))
                    step(nc.vector.tensor_reduce(m.top[:], m.left[:], AX, ALU.max))
                    step(nc.vector.tensor_tensor(m.total[:], m.total[:], m.top[:], ALU.add))
                else:
                    step(nc.vector.tensor_tensor(m.chosen[:], m.chosen[:], m.hit[:], ALU.add))
            step(nc.vector.reciprocal(m.total[:], m.total[:]))
            step(nc.vector.tensor_tensor(m.chosen[:], m.chosen[:], ex, ALU.mult))
            step(nc.vector.tensor_tensor(m.comb[:, :, 0:E], m.chosen[:], bc(m.total[:], 2, E), ALU.mult))
            step(nc.vector.tensor_scalar(gate, gate, 1.0, None, ALU.add))
            step(nc.vector.reciprocal(m.comb[:, :, E], gate))
            for k in range(3):
                step(nc.vector.tensor_copy(m.cparts[:, :, k, :], m.comb[:]))
                if k < 2:
                    step(nc.vector.tensor_tensor(m.comb[:], m.comb[:], m.cparts[:, :, k, :], ALU.subtract))
            for g in range(4):
                dve.wait_ge(m.t_turn, g + 1)
                nc.vector.tensor_copy(m.ct[:, 1024 * g:1024 * g + 1024], m.bank16(g)[0:3 * (E + 1), :]) \
                    .then_inc(m.t_out, 1)

        @block.scalar
        def _(act):
            act.wait_ge(m.t_dve, 2)
            nc.scalar.activation(ex, ex, ACT.Exp).then_inc(m.t_exp, 1)
            nc.scalar.activation(gate, gate, ACT.Exp, scale=-1.0).then_inc(m.t_exp, 1)

        @block.tensor
        def _(pe):
            pe.wait_ge(m.t_dve, 5 + 8 + 5 + 5 + 5)
            for t in range(NT):
                last = nc.tensor.transpose(m.bank16(t // 8)[0:3 * (E + 1), P * (t % 8):P * (t % 8) + P],
                                           m.cparts[:, t].rearrange("p r e -> p (r e)"), m.ident16[:])
                if t % 8 == 7:
                    last.then_inc(m.t_turn, 1)


def experts(nc, m):
    bank = m.bank

    def before(s, n):
        return s * NI + n - 1 if n >= 2 else s * NI

    with nc.Block() as block:

        @block.sync
        def _(sp):
            with sp.Fori(0, NTG) as s:
                sp.wait_ge(m.e_st, s * 16 + 1)
                sp.dma_start(m.xg[:, 0], m.x1_dram[:, bass.ds(s * 4, 4), :]).then_inc(m.e_x, 16)
                sp.wait_ge(m.e_y, s * 2 + 3)
                sp.dma_start(m.out_seq[:, bass.ds(s * 4, 4), :], m.xg[:, 0]).then_inc(m.e_st, 16)
            sp.wait_ge(m.e_st, 16 * NTG + 1)

        @block.tensor
        def _(pe):
            def up(s, n):
                pe.wait_ge(m.e_h, before(s, n) + 1)
                f = slice(P * n, P * n + P)
                tokens = bass.ds(s * TG, TG)
                for i, w in enumerate((m.wg, m.wu_ffn)):
                    for k in range(2):
                        nc.tensor.matmul(bank(3 * (n % 2) + i)[:], w[:, k, f],
                                         m.xt2[:, k, tokens], start=k == 0, stop=k == 1)
                nc.tensor.matmul(bank(3 * (n % 2) + 2)[:], m.sel[:, n, :], m.ct[:, tokens],
                                 start=True, stop=True).then_inc(m.e_g, 1)

            def down(s, n):
                pe.wait_ge(m.e_h, s * NI + n + 2)
                if n == 0:
                    pe.wait_ge(m.e_y, s * 2 + 1)
                for q in range(4):
                    last = nc.tensor.matmul(bank(6 + q // 2)[:, D * (q % 2):D * (q % 2) + D],
                                            m.h[:, n % 2, P * q:P * q + P], m.wd[:, n, :],
                                            start=n == 0 and q % 2 == 0, stop=n == NI - 1, skip_group_check=True)
                last.then_inc(m.e_d, 1)

            with pe.Fori(0, NTG) as s:
                up(s, 0)
                for n in range(NI):
                    if n + 1 < NI:
                        up(s, n + 1)
                    down(s, n)

        @block.scalar
        def _(act):
            with act.Fori(0, NTG) as s:
                for n in range(NI):
                    act.wait_ge(m.e_g, s * NI + n + 1)
                    act.wait_ge(m.e_h, before(s, n) + 1)
                    nc.scalar.activation(m.sg[:, n % 2, :], bank(3 * (n % 2))[:], ACT.Silu).then_inc(m.e_s, 1)

        @block.vector
        def _(dve):
            with dve.Fori(0, NTG) as s:
                for n in range(NI):
                    dve.wait_ge(m.e_s, s * NI + n + 1)
                    nc.vector.tensor_tensor(m.sg[:, n % 2, :], m.sg[:, n % 2, :], bank(3 * (n % 2) + 1)[:],
                                            ALU.mult).then_inc(m.e_t, 1)
                    dve.wait_ge(m.e_t, s * NI + n + 1)
                    dve.wait_ge(m.e_d, before(s, n) + 1)
                    nc.vector.tensor_tensor(m.h[:, n % 2, :], m.sg[:, n % 2, :], bank(3 * (n % 2) + 2)[:],
                                            ALU.mult).then_inc(m.e_h, 1)
                dve.wait_ge(m.e_d, s * NI + NI + 1)
                dve.wait_ge(m.e_x, s * 16 + 16)
                for i in range(2):
                    x = flat(m.xg[:, 0, 2 * i:2 * i + 2, :])
                    nc.vector.tensor_tensor(x, bank(6 + i)[:], x, ALU.add).then_inc(m.e_y, 1)





def layer(nc, ins, consts, out):
    m = Memory()
    (m.x_in, m.Wq, m.Wk, m.Wv, m.wo_dram, m.Wb, m.w_gate, m.w_up, m.w_down, m.sw_gate, m.sw_up, m.sw_down,
     m.router_w) = ins
    (m.c_cos, m.c_sin, m.c_ident, m.c_rowmask, m.c_pairmask, m.c_masks, m.c_sel, m.c_key) = consts
    m.x_seq = m.x_in.rearrange("b (t p) d -> p (b t) d", p=P)
    m.out_seq = out.rearrange("b (t p) d -> p (b t) d", p=P)
    m.wo_dram = m.wo_dram.rearrange("(k p) n -> p k n", p=P)

    def dram(name, shape, dt=F32):
        return nc.dram_tensor(name, shape, dt, kind="Internal").ap()

    m.q_dram = dram("q_dram", [P, NC, D])
    m.kb_dram = dram("kb_dram", [P, NC, D])
    m.v_dram = dram("v_dram", [P, NC, D])
    m.x1_dram = dram("x1_dram", [P, NB * NQ, D])
    m.max_dram = dram("max_dram", [3 * H, N], BF16)

    with ExitStack() as whole:
        def sems(names):
            return [whole.enter_context(nc.semaphore(name)) for name in names.split()]

        m.const_loaded, m.const_done, m.ln_ready, m.ln_sqrt, m.ln_done, m.bn_done = sems("const_loaded const_done ln_ready ln_sqrt ln_done bn_done")
        m.p_xn, m.p_xt, m.p_xte, m.p_qk, m.p_rot, m.p_rope, m.p_v = sems("p_xn p_xt p_xte p_qk p_rot p_rope p_v")
        m.k_q, m.k_sq, m.k_ss, m.k_sqrt, m.k_beta, m.k_lane, m.k_norm = sems("k_q k_sq k_ss k_sqrt k_beta k_lane k_norm")
        m.k_kb, m.k_stored = sems("k_kb k_stored")
        m.g_kc, m.g_kt, m.g_kt1, m.g_kt2, m.g_mm, m.g_out, m.g_tr = sems("g_kc g_kt g_kt1 g_kt2 g_mm g_out g_tr")
        m.solve, m.x_back, m.x_copy, m.g_an, m.held, m.held_sp, m.held_pool = sems("solve x_back x_copy g_an held held_sp held_pool")
        m.r_xc, m.r_wu_mm, m.r_wu, m.r_wt_mm, m.r_wt, m.r_kb, m.r_ws = sems("r_xc r_wu_mm r_wu r_wt_mm r_wt r_kb r_ws")
        m.r_vn, m.r_ds, m.r_dsm, m.r_s, m.r_vo, m.r_v, m.r_stored = sems("r_vn r_ds r_dsm r_s r_vo r_v r_stored")
        m.a_const, m.a_vg, m.a_k, m.a_q, m.a_kt, m.a_qt, m.a_ke = sems("a_const a_vg a_k a_q a_kt a_qt a_ke")
        m.a_qe, = sems("a_qe")
        m.m_max, m.m_s, m.m_part, m.m_t, m.m_rows, m.m_out, m.m_in = sems("m_max m_s m_part m_t m_rows m_out m_in")
        m.v_read, m.v_vg, m.v_exp, m.v_s, m.v_o = sems("v_read v_vg v_exp v_s v_o")
        m.o_x, m.o_x1, m.o_st, m.o_n, m.o_t, m.o_te, m.o_tt = sems("o_x o_x1 o_st o_n o_t o_te o_tt")
        m.o_mm, m.o_bn = sems("o_mm o_bn")
        m.f_gate, m.f_pad, m.f_const, m.f_xn, m.f_copy, m.f_ln, m.f_sqrt = sems("f_gate f_pad f_const f_xn f_copy f_ln f_sqrt")
        m.f_t, m.f_lg, m.f_lge, m.f_te = sems("f_t f_lg f_lge f_te")
        m.t_dve, m.t_exp, m.t_turn, m.t_out = sems("t_dve t_exp t_turn t_out")
        m.e_st, m.e_x, m.e_y, m.e_h, m.e_g, m.e_d, m.e_t = sems("e_st e_x e_y e_h e_g e_d e_t")
        m.e_s, = sems("e_s")
        m.starts = [
            (m.e_d, 1), (m.e_h, 1), (m.e_st, 1), (m.e_y, 1), (m.f_copy, 2), (m.f_lge, 1), (m.f_t, 1),
            (m.f_te, 1), (m.f_xn, 2), (m.g_an, 1), (m.g_kt, 1), (m.g_kt1, 1), (m.g_mm, 1), (m.g_out, 1),
            (m.g_tr, 1), (m.m_max, 4), (m.p_rope, 2), (m.p_rot, 5), (m.p_v, 1), (m.p_xt, 1), (m.p_xte, 1),
            (m.r_ds, 2), (m.r_v, 1), (m.r_vo, 2), (m.v_exp, 2), (m.v_o, 2), (m.v_read, 2), (m.x_back, 1),
            (m.x_copy, 1),
        ]
        m.x_loaded = sems("x_loaded0 x_loaded1 x_loaded2 x_loaded3")
        m.a_loaded = sems("a_loaded0 a_loaded1 a_loaded2")
        m.f_x = sems("f_x0 f_x1")
        m.psum = whole.enter_context(nc.psum_tensor("psum", [P, 8, 512], F32))[:]
        m.bank = lambda i: m.psum[:, i, :]
        m.bank16 = lambda i: m.psum[:, i, :].bitcast(BF16)

        def sb(stack, name, shape, dt=F32):
            return stack.enter_context(nc.sbuf_tensor(name, shape, dt))[:]

        m.ident = sb(whole, "ident", [P, P])
        m.ident16 = sb(whole, "ident16", [P, P], BF16)
        m.mv = sb(whole, "mv", [P, NC, 2])
        m.mean = sb(whole, "mean", [P, NC])
        m.rstd = sb(whole, "rstd", [P, NC])
        m.stats2 = sb(whole, "stats2", [P, NC, 6])
        with ExitStack() as first:
            m.q = sb(first, "q", [P, NC, D])
            m.kv = sb(first, "kv", [P, NC, 2, D])
            m.beta = sb(first, "beta", [P, NC, H])
            m.beta_half = sb(first, "beta_half", [P, 2, NC * H])
            m.beta_lane = sb(first, "beta_lane", [P, NC // 2, 2 * H])
            m.rowmask = sb(first, "rowmask", [P, 2])
            m.pairmask = sb(first, "pairmask", [P, 34])
            with ExitStack() as stack:
                m.x = sb(stack, "x", [P, NC, D])
                m.cosq = sb(stack, "cosq", [P, NC, 8])
                m.sinq = sb(stack, "sinq", [P, NC, 8])
                m.w_in = sb(stack, "w_in", [P, 2, 3 * D + H])
                m.stats = sb(stack, "stats", [P, NC, 6])
                m.xn = sb(stack, "xn", [P, 2, D])
                m.xnt = sb(stack, "xnt", [P, 2, 2, P])
                m.rc = sb(stack, "rc", [P, 2, 2 * H, 2, 8])
                m.rs = sb(stack, "rs", [P, 2, 2 * H, 2, 8])
                m.rn = sb(stack, "rn", [P, NC, H])
                m.sq = m.x
                load_constants(nc, m)
                projections(nc, m)
                normalise_keys(nc, m)
            with ExitStack() as stack:
                m.xt = sb(stack, "xt", [P, NC // 2, 1024])
                with ExitStack() as inner:
                    m.an = sb(inner, "an", [P, 2, GP, SUB, SUB])
                    m.prod = sb(inner, "prod", [P, 2, GP, SUB - 1, SUB - 1])
                    m.gs = sb(inner, "gs", [P, 1024])
                    m.gram = sb(inner, "gram", [P, 1024])
                    m.kc = sb(inner, "kc", [P, D])
                    m.kt1 = sb(inner, "kt1", [P, 2, P])
                    m.kt2 = sb(inner, "kt2", [P, 2, 2, P])
                    scratch = m.q.rearrange("p c d -> p (c d)")
                    m.xl, m.xb = (scratch[:, i * GP * 1024:(i + 1) * GP * 1024].rearrange("p (g f) -> p g f", g=GP)
                                  for i in range(2))
                    triangular_inverses(nc, m)
                with ExitStack() as inner:
                    m.xc = sb(inner, "xc", [P, 2, H, CT])
                    m.kvc = sb(inner, "kvc", [P, 2, 2, D])
                    m.wu = sb(inner, "wu", [P, 2, 2, D])
                    m.wt = sb(inner, "wt", [P, 2, 2, P])
                    m.kb = sb(inner, "kb", [P, 2, D])
                    m.vn = sb(inner, "vn", [P, 2, D])
                    m.vt = sb(inner, "vt", [P, 2, D])
                    m.s = sb(inner, "s", [P, NB, 2, 32])
                    m.ds = sb(inner, "ds", [P, NB, 2, 32])
                    m.v = m.q
                    recurrence(nc, m)
        with ExitStack() as stack:
            m.kn = sb(stack, "kn", [P, NQ, D])
            m.qn = sb(stack, "qn", [P, NQ, D])
            m.vn2 = sb(stack, "vn2", [P, NQ, D])
            m.rest_k = sb(stack, "rest_k", [P, NQ * D])
            m.rest_q = sb(stack, "rest_q", [P, NQ * D])
            m.stage_k = sb(stack, "stage_k", [P, NQ, H, TERMS, HD], BF16)
            m.stage_q = sb(stack, "stage_q", [P, NQ, H, TERMS, HD], BF16)
            m.ks = sb(stack, "ks", [P, H, N], BF16)
            m.qs = sb(stack, "qs", [P, H, N], BF16)
            m.wo = sb(stack, "wo", [P, 2, D])
            m.masks = sb(stack, "masks", [P, 2, P])
            m.mask_qk = sb(stack, "mask_qk", [P, P], BF16)
            m.mask_kq = sb(stack, "mask_kq", [P, P], BF16)
            m.nmax = sb(stack, "nmax", [P, NQ, H])
            m.mparts = sb(stack, "mparts", [P, NQ, 3, H], BF16)
            m.mrows = sb(stack, "mrows", [3 * H, N], BF16)
            m.rsum = sb(stack, "rsum", [P, 2, H])
            m.vg = sb(stack, "vg", [P, 2, NQ, 4, 32])
            m.p = sb(stack, "p", [P, 8, N])
            m.ot = m.stage_k.rearrange("p t h r e -> p (t h r e)").bitcast(F32)[:, 0:NG * N] \
                .rearrange("p (g t) -> p g t", g=NG)
            m.xres = m.kn
            m.on = m.rest_k[:, 0:2 * D].rearrange("p (u d) -> p u d", u=2)
            m.ont = m.rest_k[:, 2 * D:4 * D].rearrange("p (u k t) -> p u k t", u=2, k=2)
            attention(nc, m)
        with ExitStack() as stack:
            m.xt2 = sb(stack, "xt2", [P, 2, NB * N])
            m.wg = sb(stack, "wg", [P, 2, NI * P])
            m.wu_ffn = sb(stack, "wu_ffn", [P, 2, NI * P])
            m.wd = sb(stack, "wd", [P, NI, D])
            m.gt = sb(stack, "gt", [P, 2, E + 1])
            m.sel32 = sb(stack, "sel32", [3 * (E + 1), NI, P])
            m.sel = sb(stack, "sel", [3 * (E + 1), NI, P], BF16)
            m.key = sb(stack, "key", [P, E])
            m.xg = sb(stack, "xg", [P, 2, 4, D])
            m.xm = sb(stack, "xm", [P, 4, D])
            m.xs = sb(stack, "xs", [P, 2, 2, TG])
            m.lg = sb(stack, "lg", [P, NC, E + 1])
            m.ex = sb(stack, "ex", [P, NC, E])
            m.left = sb(stack, "left", [P, NC, E])
            m.hit = sb(stack, "hit", [P, NC, E])
            m.chosen = sb(stack, "chosen", [P, NC, E])
            m.top = sb(stack, "top", [P, NC])
            m.total = sb(stack, "total", [P, NC])
            m.comb = sb(stack, "comb", [P, NC, E + 1])
            m.cparts = sb(stack, "cparts", [P, NC, 3, E + 1], BF16)
            m.ct = sb(stack, "ct", [3 * (E + 1), NB * N], BF16)
            m.sg = sb(stack, "sg", [P, 2, TG])
            m.h = sb(stack, "h", [P, 2, TG])
            second_norm(nc, m)
            router(nc, m)
            experts(nc, m)


def constants():
    p = np.arange(P)
    pos = (p[:, None] % CT + CT * np.arange(NC)[None, :]).astype(np.float32)
    inv = (np.float32(1.0) / np.float32(10000.0) ** (np.arange(0, HD, 2, dtype=np.float32) / np.float32(HD)))
    angle = pos[:, :, None] * inv.astype(np.float32)
    pair = np.zeros((P, 34), np.float32)
    pair[:, 0:32] = (p[:, None] % 32 // HD) == (np.arange(32)[None, :] // HD)
    pair[:, 32], pair[:, 33] = p % 32 < HD, p % 32 >= HD
    unit = np.arange(NI * P)
    owner = np.minimum(unit // I, E)
    sel = np.zeros((3 * (E + 1), NI * P), np.float32)
    for k in range(3):
        sel[k * (E + 1) + owner, unit] = 1.0
    return {
        "c_cos": np.cos(angle).astype(np.float32), "c_sin": np.sin(angle).astype(np.float32),
        "c_ident": np.eye(P, dtype=np.float32),
        "c_rowmask": np.stack([p % CT < SUB, p % CT >= SUB], 1).astype(np.float32), "c_pairmask": pair,
        "c_masks": np.stack([np.where(p[None, :] > p[:, None], NEG, 0.0),
                             np.where(p[:, None] > p[None, :], NEG, 0.0)], 1).astype(np.float32),
        "c_sel": sel.reshape(-1, NI, P),
        "c_key": np.tile(np.arange(E, 0, -1, dtype=np.float32), (P, 1)),
    }


_INS = ["L0_attn_x", "L0_attn_Wq", "L0_attn_Wk", "L0_attn_Wv", "L0_attn_Wo", "L0_attn_Wb", "L0_ffn_w_gate",
        "L0_ffn_w_up", "L0_ffn_w_down", "L0_ffn_sw_gate", "L0_ffn_sw_up", "L0_ffn_sw_down"]


def kernel(**inputs):
    import numpy as _np
    import concourse.bacc as _bacc
    from concourse import mybir as _mybir
    from concourse.bass_utils import run_bass_kernel_spmd as _run

    nc = _bacc.Bacc("TRN2", target_bir_lowering=False, num_devices=1)
    given = {f"in_{name}_dram": _np.ascontiguousarray(inputs[name]) for name in _INS}
    given["in_router_dram"] = _np.ascontiguousarray(_np.concatenate(
        [_np.asarray(inputs["L0_ffn_gate_w"]).T, _np.asarray(inputs["L0_ffn_shared_gate_w"])], axis=1))
    tables = constants()

    def tensor(name, a):
        return nc.dram_tensor(name, a.shape, _mybir.dt.from_np(a.dtype), kind="ExternalInput").ap()

    ins = [tensor(name, a) for name, a in given.items()]
    consts = [tensor(name, a) for name, a in tables.items()]
    out = nc.dram_tensor("out_0_dram", (NB, N, D), _mybir.dt.float32, kind="ExternalOutput").ap()
    layer(nc, ins, consts, out)
    r = _run(nc, [{**given, **tables}], core_ids=[0])
    return r.results[0]["out_0_dram"]
```

```python
from contextlib import ExitStack

import concourse.bass as bass
import numpy as np
from concourse import mybir
from concourse.alu_op_type import AluOpType as ALU

F32 = mybir.dt.float32
BF16 = mybir.dt.bfloat16
F32R = mybir.dt.float32r
ACT = mybir.ActivationFunctionType
AX = mybir.AxisListType.X

P = 128
NB, N, D, H, HD = 4, 1024, 256, 16, 16
CT = 32
NC = N // CT
SUB = 16
NQ = N // P
NG = H // 4
E, I, IS = 8, 176, 704
IT = E * I + IS
NI = -(-IT // P)
LAST = IT - P * (NI - 1)
GP = 4
TG = 512
NTG = NB * N // TG
HALF = D // 2
TERMS = 6
QROWS = TERMS * HD
SROWS = QROWS + 3
NEG = -1.0e30
Q_PARTS = (0, 0, 1, 1, 2, 0)
K_PARTS = (0, 1, 0, 1, 0, 2)
PRODUCTS = ((0, 1), (1, 0), (0, 0))


class Memory:
    pass


def flat(ap):
    return ap.rearrange("p a b -> p (a b)")


def bc(ap, axis, n):
    shape = list(ap.shape)
    shape.insert(axis, n)
    return ap.unsqueeze(axis).broadcast_to(shape)


def hold(engine, semaphore, value, held):
    engine.wait_ge(semaphore, value)
    engine.sem_inc(held, 1)


def load_constants(nc, m):
    loads = [
        (m.cosq[:], m.c_cos), (m.sinq[:], m.c_sin), (m.ident[:], m.c_ident),
        (m.rowmask[:], m.c_rowmask), (m.pairmask[:], m.c_pairmask),
        (m.w_in[:, :, 0:D], m.Wq.rearrange("(k p) n -> p k n", p=P)),
        (m.w_in[:, :, D:2 * D], m.Wk.rearrange("(k p) n -> p k n", p=P)),
        (m.w_in[:, :, 2 * D:3 * D], m.Wv.rearrange("(k p) n -> p k n", p=P)),
        (m.w_in[:, :, 3 * D:3 * D + H], m.Wb.rearrange("(k p) n -> p k n", p=P)),
    ]
    with nc.Block() as block:

        @block.sync
        def _(sp):
            for k in range(4):
                for b in range(NB):
                    sp.dma_start(m.x[32 * b:32 * b + 32, 8 * k:8 * k + 8, :],
                                 m.x_in[b].rearrange("(c i) d -> i c d", i=CT)[:, 8 * k:8 * k + 8, :]) \
                        .then_inc(m.x_loaded[k], 16)

        @block.scalar
        def _(act):
            for dst, src in loads:
                act.dma_start(dst, src).then_inc(m.const_loaded, 16)
            act.wait_ge(m.ln_ready, NC + 2)
            nc.scalar.activation(m.rstd[:], m.rstd[:], ACT.Sqrt).then_inc(m.ln_sqrt, 1)

        @block.vector
        def _(dve):
            for semaphore, value in m.starts:
                dve.sem_inc(semaphore, value)
            dve.wait_ge(m.const_loaded, 16 * len(loads))
            nc.vector.tensor_copy(m.ident16[:], m.ident[:])
            nc.vector.tensor_scalar(m.w_in[:, :, 0:D], m.w_in[:, :, 0:D], HD ** -0.5, None, ALU.mult) \
                .then_inc(m.w_split, 1)
            dve.wait_ge(m.w_split, 1)
            nc.vector.tensor_copy(m.w_parts[:, 0], m.w_in[:]).then_inc(m.w_split, 1)
            dve.wait_ge(m.w_split, 2)
            nc.vector.tensor_tensor(m.w_parts[:, 1], m.w_in[:], m.w_parts[:, 0].bitcast(F32), ALU.subtract)
            for c in range(NC):
                if c % 8 == 0:
                    dve.wait_ge(m.x_loaded[c // 8], 16 * NB)
                nc.vector.bn_stats(m.stats[:, c, :], m.x[:, c, :]).then_inc(m.bn_done, 1)
            for c in range(NC):
                dve.wait_ge(m.bn_done, c + 1)
                nc.vector.bn_aggr(m.mv[:, c, :], m.stats[:, c, :]).then_inc(m.ln_ready, 1)
            dve.wait_ge(m.ln_ready, NC)
            nc.vector.tensor_scalar(m.rstd[:], m.mv[:, :, 1], 1e-5, None, ALU.add).then_inc(m.ln_ready, 1)
            nc.vector.tensor_copy(m.mean[:], m.mv[:, :, 0]).then_inc(m.ln_ready, 1)
            dve.wait_ge(m.ln_sqrt, 1)
            nc.vector.reciprocal(m.rstd[:], m.rstd[:]).then_inc(m.ln_done, 1)


def projections(nc, m):
    bank = m.bank

    def everywhere(engine, start, iteration):
        start()
        with engine.Fori(0, NC // 2 - 2) as cc:
            for u in range(2):
                iteration(cc * 2 + u, u, 3)
        for c in range(NC - 4, NC):
            iteration(c, c % 2, NC - 1 - c)

    def nothing():
        pass

    with nc.Block() as block:

        @block.vector
        def _(dve):
            def normalise(c, u):
                if not isinstance(c, int) or c >= 2:
                    dve.wait_ge(m.p_xt, c - 1)
                nc.vector.tensor_scalar(
                    m.xn[:, u, :], m.x[:, bass.ds(c, 1), :].rearrange("p a d -> p (a d)"),
                    m.mean[:, bass.ds(c, 1)], m.rstd[:, bass.ds(c, 1)],
                    ALU.subtract, ALU.mult).then_inc(m.p_xn, 1)

            def rest(c, u):
                dve.wait_ge(m.p_high, c + 1)
                nc.vector.tensor_tensor(flat(m.xnt[:, u, 1]), bank(u)[:, 0:D],
                                        flat(m.xnt[:, u, 0]).bitcast(F32), ALU.subtract).then_inc(m.p_low, 1)

            def start():
                for c in range(3):
                    normalise(c, c % 2)
                rest(0, 0)

            def iteration(c, u, ahead):
                if ahead >= 3:
                    normalise(c + 3, 1 - u)
                if ahead >= 1:
                    rest(c + 1, 1 - u)
                dve.wait_ge(m.p_qk, c + 1)
                dve.wait_ge(m.p_rope, c + 1)
                qk = bank(2 + u)[:, 0:2 * D].rearrange("p (h w e) -> p h w e", h=2 * H, w=2)
                cos = bc(m.cosq[:, bass.ds(c, 1), :].rearrange("p a e -> p (a e)"), 1, 2 * H)
                sin = bc(m.sinq[:, bass.ds(c, 1), :].rearrange("p a e -> p (a e)"), 1, 2 * H)
                for w in range(2):
                    nc.vector.tensor_tensor(m.rc[:, u, :, w, :], qk[:, :, w, :], cos, ALU.mult).then_inc(m.p_rot, 1)
                    nc.vector.tensor_tensor(m.rs[:, u, :, w, :], qk[:, :, 1 - w, :], sin, ALU.mult) \
                        .then_inc(m.p_rot, 1)

            everywhere(dve, start, iteration)

        @block.gpsimd
        def _(pool):
            def iteration(c, u, ahead):
                pool.wait_ge(m.p_rot, 4 * c + 9)
                for i in range(2):
                    out = (m.q[:, bass.ds(c, 1), :] if i == 0 else m.kv[:, bass.ds(c, 1), 0, :]) \
                        .rearrange("p a (h w e) -> p (a h) w e", h=H, w=2)
                    hs = slice(H * i, H * i + H)
                    for w, op in ((0, ALU.subtract), (1, ALU.add)):
                        last = nc.gpsimd.tensor_tensor(
                            out[:, :, w, :], m.rc[:, u, hs, w, :], m.rs[:, u, hs, w, :], op)
                last.then_inc(m.p_rope, 1)

            everywhere(pool, nothing, iteration)

        @block.tensor
        def _(pe):
            def turn(c, u):
                pe.wait_ge(m.p_xn, c + 1)
                for k in range(2):
                    last = nc.tensor.transpose(bank(u)[:, k * P:(k + 1) * P],
                                               m.xn[:, u, k * P:(k + 1) * P], m.ident[:])
                last.then_inc(m.p_xt, 1)

            def start():
                turn(0, 0)
                turn(1, 1)

            def iteration(c, u, ahead):
                pe.wait_ge(m.p_low, c + 1)
                pe.wait_ge(m.p_rot, 4 * c + 1)
                pe.wait_ge(m.p_v, c + 1)
                for out, columns in ((bank(2 + u), slice(0, 2 * D)), (bank(4 + u), slice(2 * D, 3 * D + H))):
                    for k in range(2):
                        for a, b in PRODUCTS:
                            last = nc.tensor.matmul(out[:, 0:columns.stop - columns.start], m.xnt[:, u, a, k, :],
                                                    m.w_parts[:, b, k, columns],
                                                    start=(k, a, b) == (0, 0, 1), stop=(k, a, b) == (1, 0, 0))
                last.then_inc(m.p_qk, 1)
                if ahead >= 2:
                    turn(c + 2, u)

            everywhere(pe, start, iteration)

        @block.scalar
        def _(act):
            def high(c, u):
                act.wait_ge(m.p_xt, c + 1)
                nc.scalar.copy(flat(m.xnt[:, u, 0]), bank(u)[:, 0:D]).then_inc(m.p_high, 1)

            def start():
                high(0, 0)
                high(1, 1)

            def iteration(c, u, ahead):
                act.wait_ge(m.p_qk, c + 1)
                nc.scalar.copy(m.kv[:, bass.ds(c, 1), 1, :].rearrange("p a d -> p (a d)"), bank(4 + u)[:, 0:D])
                nc.scalar.copy(m.beta[:, bass.ds(c, 1), :].rearrange("p a h -> p (a h)"),
                               bank(4 + u)[:, D:D + H]).then_inc(m.p_v, 1)
                if ahead >= 2:
                    high(c + 2, u)

            everywhere(act, start, iteration)


def normalise_keys(nc, m):
    k_all = m.kv[:, :, 0, :].rearrange("p c (h e) -> p c h e", h=H)
    with nc.Block() as block:

        @block.vector
        def _(dve):
            sq = m.sq[:].rearrange("p c (h e) -> p c h e", h=H)
            for j in range(4):
                cs = slice(8 * j, 8 * j + 8)
                dve.wait_ge(m.k_sq, j + 1)
                nc.vector.tensor_reduce(m.rn[:, cs, :], sq[:, cs], AX, ALU.add).then_inc(m.k_ss, 1)
            dve.wait_ge(m.k_ss, 4)
            nc.vector.tensor_scalar(m.rn[:], m.rn[:], 1e-6, None, ALU.add).then_inc(m.k_ss, 1)
            dve.wait_ge(m.k_sqrt, 1)
            nc.vector.reciprocal(m.rn[:], m.rn[:]).then_inc(m.k_ss, 1)
            dve.wait_ge(m.k_sqrt, 2)
            nc.vector.tensor_scalar(m.beta[:], m.beta[:], 1.0, None, ALU.add).then_inc(m.k_beta, 1)
            dve.wait_ge(m.k_beta, 1)
            nc.vector.reciprocal(m.beta[:], m.beta[:]).then_inc(m.k_beta, 1)
            dve.wait_ge(m.k_beta, 2)
            nc.vector.tensor_scalar(m.beta[:], m.beta[:], 2.0, None, ALU.mult).then_inc(m.k_beta, 1)
            dve.wait_ge(m.k_ss, 6)
            for j in range(4):
                cs = slice(8 * j, 8 * j + 8)
                for c in range(8 * j, 8 * j + 8):
                    last = nc.vector.tensor_tensor(k_all[:, c], k_all[:, c], bc(m.rn[:, c, :], 2, HD), ALU.mult)
                last.then_inc(m.k_norm, 1)
            dve.wait_ge(m.k_norm, 4)
            dve.wait_ge(m.k_beta, 3)
            for c in range(24, NC):
                last = nc.vector.tensor_tensor(
                    m.sq[:, c, :].rearrange("p (h e) -> p h e", h=H), k_all[:, c],
                    bc(m.beta[:, c, :], 2, HD), ALU.mult)
            last.then_inc(m.k_kb_last, 1)
            for s in range(2):
                nc.vector.tensor_scalar(m.beta_half[:, s, :], m.beta[:].rearrange("p c h -> p (c h)"),
                                        m.rowmask[:, s:s + 1], None, ALU.mult).then_inc(m.k_beta, 1)
            nc.vector.transpose(m.beta_lane[:], m.beta[:].rearrange("p c h -> p (c h)")).then_inc(m.k_lane, 1)
            dve.wait_ge(m.k_lane, 1)
            nc.vector.tensor_scalar(m.beta_lane[:], m.beta_lane[:], -1.0, None, ALU.mult).then_inc(m.k_lane, 1)

        @block.scalar
        def _(act):
            for j in range(4):
                cs = slice(8 * j, 8 * j + 8)
                nc.scalar.activation(m.sq[:, cs, :], m.kv[:, cs, 0, :], ACT.Square).then_inc(m.k_sq, 1)
            act.wait_ge(m.k_ss, 5)
            nc.scalar.activation(m.rn[:], m.rn[:], ACT.Sqrt).then_inc(m.k_sqrt, 1)
            nc.scalar.activation(m.beta[:], m.beta[:], ACT.Exp, scale=-1.0).then_inc(m.k_sqrt, 1)

        @block.gpsimd
        def _(pool):
            pool.wait_ge(m.k_beta, 3)
            for j in range(3):
                pool.wait_ge(m.k_norm, j + 1)
                for c in range(8 * j, 8 * j + 8):
                    last = nc.gpsimd.tensor_tensor(
                        m.sq[:, c, :].rearrange("p (h e) -> p h e", h=H), k_all[:, c],
                        bc(m.beta[:, c, :], 2, HD), ALU.mult)
                last.then_inc(m.k_kb, 1)

        @block.sync
        def _(sp):
            sp.dma_start(m.q_dram, m.q[:]).then_inc(m.k_stored, 16)
            for j in range(4):
                if j < 3:
                    sp.wait_ge(m.k_kb, j + 1)
                else:
                    sp.wait_ge(m.k_kb_last, 1)
                sp.dma_start(m.kb_dram[:, 8 * j:8 * j + 8, :], m.sq[:, 8 * j:8 * j + 8, :]).then_inc(m.k_stored, 16)
            sp.wait_ge(m.k_stored, 16 * 5)


PT = 2 * GP
ROW_STEPS = 4
WHOLE_ROWS = 10
SLOTS = GP + WHOLE_ROWS + 2 * (SUB - 1 - WHOLE_ROWS) + 2


def delta_rule(nc, m):
    bank = m.bank

    def everywhere(engine, iteration, prelude):
        iteration(-2, False, False, True)
        iteration(-1, False, True, True)
        prelude()
        with engine.Fori(0, NC // PT - 2) as p:
            iteration(p, True, True, True)
        iteration(NC // PT - 2, True, True, False)
        iteration(NC // PT - 1, True, False, False)

    def nothing():
        pass

    with nc.Block() as block:

        @block.gpsimd
        def _(pool):
            def keys(c):
                hold(pool, m.g_kt, c + 1, m.held_pool)
                nc.gpsimd.tensor_copy(m.kc[:], m.kv[:, bass.ds(c, 1), 0, :].rearrange("p a d -> p (a d)")) \
                    .then_inc(m.g_kc, 1)

            def steps(p, i, recur, gram, more):
                c = p * PT + i
                if recur:
                    for s in range(2):
                        pool.wait_ge(m.r_ds, 2 * c + s + 1)
                        nc.gpsimd.tensor_tensor(
                            m.kb[:, s].rearrange("p (h e) -> p h e", h=H),
                            m.kv[:, bass.ds(c, 1), 0, :].rearrange("p a (h e) -> p (a h) e", h=H),
                            bc(m.beta_half[:, s, bass.ds(c * H, H)], 2, HD), ALU.mult).then_inc(m.r_kb, 1)
                if gram:
                    keys(c + 2 * PT)
                if recur:
                    if more:
                        hold(pool, m.r_wu_mm, c + 1, m.held_pool)
                        fetch(p, i + 2)
                    for s in range(2):
                        hold(pool, m.r_vn, 2 * c + s + 1, m.held_pool)
                        if s == 0:
                            hold(pool, m.r_v, c + 1, m.held_pool)
                        nc.gpsimd.tensor_tensor(m.vt[:, s], m.vn[:, s], m.rowmask[:, s:s + 1].broadcast_to([P, D]),
                                                ALU.mult).then_inc(m.r_vo, 1)
                    hold(pool, m.r_vo, 2 * c + 4, m.held_pool)
                    nc.gpsimd.tensor_tensor(m.v[:, bass.ds(c, 1), :].rearrange("p a d -> p (a d)"), m.vt[:, 0],
                                            m.vt[:, 1], ALU.add).then_inc(m.r_v, 1)

            def fetch(p, i):
                c, u, g = p * PT + i, i % 2, i % PT // 2
                hold(pool, m.x_back, p * GP + i // 2 + 1, m.held_pool)
                x_t = m.xb[:, g].rearrange("p (i u h) -> p u h i", i=32, u=2)
                nc.gpsimd.tensor_copy(m.xc[:, u], x_t[:, u]).then_inc(m.r_xc, 1)
                nc.gpsimd.tensor_copy(m.kvc[:, u], m.kv[:, bass.ds(c, 1), :, :].rearrange("p a w d -> p (a w) d")) \
                    .then_inc(m.r_xc, 1)

            def iteration(p, recur, solve, gram):
                for i in range(PT):
                    steps(p, i, recur, gram, solve or i < PT - 2)

            def prelude():
                fetch(0, 0)
                fetch(0, 1)

            everywhere(pool, iteration, prelude)

        @block.tensor
        def _(pe):
            def turn_keys(c):
                pe.wait_ge(m.g_kc, c + 1)
                pe.wait_ge(m.g_out, 2 * c + 1)
                for k in range(2):
                    last = nc.tensor.transpose(bank(1)[:, k * P:(k + 1) * P], m.kc[:, k * P:(k + 1) * P], m.ident[:])
                last.then_inc(m.g_kt, 1)

            def gram_matrices(c):
                hold(pe, m.g_kt2, 2 * c + 2, m.held)
                for k in range(2):
                    for shift in range(4):
                        for j in range(4):
                            b = (j + shift) % NB
                            r = slice(32 * j, 32 * j + 32)
                            out = bank(j)[32 * b:32 * b + 32, 64 * k:64 * k + 64].rearrange("p (s t) -> p s t", s=2)
                            last = nc.tensor.matmul(out, m.kt1[r, k, 32 * b:32 * b + 32],
                                                    m.kt2[r, :, k, 32 * b:32 * b + 32], start=True, stop=True)
                last.then_inc(m.g_mm, 1)

            def heads_wu(u, hs):
                for h in hs:
                    for b in range(NB):
                        r = slice(32 * b, 32 * b + 32)
                        last = nc.tensor.matmul(bank(b)[r, 32 * h:32 * h + 32].rearrange("p (w e) -> p w e", w=2),
                                                m.xc[r, u, h, :], m.kvc[r, u, :, HD * h:HD * h + HD],
                                                start=True, stop=True)
                return last

            def transpose_w(c, u):
                pe.wait_ge(m.r_wu, 4 * c + 4)
                for k in range(2):
                    last = nc.tensor.transpose(bank(0)[:, k * P:(k + 1) * P], m.wu[:, u, 0, k * P:(k + 1) * P],
                                               m.ident[:])
                last.then_inc(m.r_wt_mm, 1)

            def steps(p, i, gram, more):
                c, u = p * PT + i, i % 2
                hold(pe, m.r_wt, c + 1, m.held)
                for s in range(2):
                    hold(pe, m.r_s, 2 * c + s + 1, m.held)
                    for k in range(2):
                        for shift in range(4):
                            for j in range(4):
                                b = (j + shift) % NB
                                r = slice(32 * j, 32 * j + 32)
                                last = nc.tensor.matmul(bank(4 + j)[32 * b:32 * b + 32, 32 * k:32 * k + 32],
                                                        m.wt[r, u, k, 32 * b:32 * b + 32], m.s[r, b, k, :],
                                                        start=True, stop=True)
                    last.then_inc(m.r_ws, 1)
                    if s == 0:
                        if more >= 1:
                            transpose_w(c + 1, 1 - u)
                        if gram:
                            turn_keys(c + 2 * PT)
                    elif more == 2:
                        hold(pe, m.r_wt, c + 2, m.held)
                        if gram:
                            hold(pe, m.g_out, 2 * (c + 2 * PT) + 3, m.held)
                        hold(pe, m.r_xc, 2 * c + 6, m.held)
                        heads_wu(u, range(H // 2))
                    pe.wait_ge(m.r_vn, 2 * c + s + 1)
                    hold(pe, m.r_kb, 2 * c + s + 1, m.held)
                    for k in range(2):
                        for shift in range(4):
                            for b in range(NB):
                                j = (b + shift) % 4
                                r = slice(32 * b, 32 * b + 32)
                                f = slice(k * P + 32 * j, k * P + 32 * j + 32)
                                last = nc.tensor.matmul(bank(4 + b)[32 * j:32 * j + 32, 64 + 32 * k:96 + 32 * k],
                                                        m.kb[r, s, f], m.vn[r, s, f], start=True, stop=True)
                    last.then_inc(m.r_ds, 1)
                    if s == 0:
                        if gram:
                            hold(pe, m.r_wt, c + 2, m.held)
                            gram_matrices(c + 2 * PT)
                    elif more == 2:
                        heads_wu(u, range(H // 2, H)).then_inc(m.r_wu_mm, 1)

            def iteration(p, recur, solve, gram):
                for i in range(PT):
                    if recur:
                        steps(p, i, gram, 2 if solve else min(2, PT - 1 - i))
                    else:
                        turn_keys(p * PT + i + 2 * PT)
                        gram_matrices(p * PT + i + 2 * PT)

            def prelude():
                pe.wait_ge(m.g_out, 4 * PT + 1)
                pe.wait_ge(m.r_xc, 2)
                heads_wu(0, range(H)).then_inc(m.r_wu_mm, 1)
                transpose_w(0, 0)
                pe.wait_ge(m.r_xc, 4)
                pe.wait_ge(m.r_wt, 1)
                heads_wu(1, range(H)).then_inc(m.r_wu_mm, 1)

            everywhere(pe, iteration, prelude)

        @block.scalar
        def _(act):
            def keys(c):
                act.wait_ge(m.g_kt, c + 2)
                act.wait_ge(m.g_mm, c + 1)
                nc.scalar.copy(flat(m.kt1[:]), bank(1)[:, 0:D]).then_inc(m.g_kt1, 1)
                act.wait_ge(m.g_kt1, c + 2)
                for s in range(2):
                    nc.scalar.activation(flat(m.kt2[:, s, :, :]), flat(m.kt1[:]), ACT.Copy,
                                         scale=m.pairmask[:, 32 + s:33 + s]).then_inc(m.g_kt2, 1)

            def gram_out(i):
                for k in range(2):
                    src = m.psum[:, 0:4, 64 * k:64 * k + 64].rearrange("p j (s t) -> p j s t", s=2)
                    dst = m.gs[:, i // 2].rearrange("p (t u k j s) -> p u k j s t", t=32, u=2, k=2, j=4)[:, i % 2, k]
                    nc.scalar.copy(dst, src).then_inc(m.g_out, 1)

            def w_and_u(c, u):
                act.wait_ge(m.r_wu_mm, c + 1)
                for b in range(NB):
                    r = slice(32 * b, 32 * b + 32)
                    nc.scalar.copy(m.wu[r, u].rearrange("p w (h e) -> p w h e", h=H),
                                   bank(b)[r, :].rearrange("p (h w e) -> p w h e", h=H, w=2)).then_inc(m.r_wu, 1)

            def w_turned(c, u):
                act.wait_ge(m.r_wt_mm, c + 1)
                nc.scalar.copy(flat(m.wt[:, u]), bank(0)[:, 0:D]).then_inc(m.r_wt, 1)

            def iteration(p, recur, solve, gram):
                for i in range(PT):
                    c = p * PT + i
                    if recur and (solve or i < PT - 1):
                        w_turned(c + 1, 1 - i % 2)
                    if gram:
                        keys(c + 2 * PT)
                        act.wait_ge(m.g_mm, c + 2 * PT + 2)
                        if i % 2 == 0 and not (isinstance(p, int) and p == -2):
                            act.wait_ge(m.g_tr, (p + 1) * GP + i // 2 + 1)
                        gram_out(i)
                    if recur and (solve or i < PT - 2):
                        w_and_u(c + 2, i % 2)

            def prelude():
                w_and_u(0, 0)
                w_turned(0, 0)
                w_and_u(1, 1)

            everywhere(act, iteration, prelude)

        @block.vector
        def _(dve):
            xl = m.xl[:].rearrange("p g (i k) -> p g i k", i=32)
            gram_t = m.gram[:].rearrange("p (j i) -> p i j", j=32)

            def systems(p, g):
                pair = p * GP + g
                dve.wait_ge(m.g_out, 4 * pair + 5)
                dve.wait_ge(m.g_an, 2 * pair + 1)
                nc.vector.transpose(m.gram[:], m.gs[:, g]).then_inc(m.g_tr, 1)
                dve.wait_ge(m.g_tr, pair + 1)
                beta = m.beta_lane[:, bass.ds(pair, 1), :].rearrange("p a j -> p (a j)")
                for s in range(2):
                    r = slice(SUB * s, SUB * s + SUB)
                    nc.vector.tensor_tensor(m.an[:, s, g], gram_t[:, r, r], bc(beta[:, r], 1, SUB),
                                            ALU.mult).then_inc(m.g_an, 1)

            def products(p, i):
                done = p * (ROW_STEPS * (SUB - 1)) + ROW_STEPS * (i - 1)
                if i == 1:
                    dve.wait_ge(m.g_an, (p + 1) * (2 * GP) + 1)
                for s in range(2):
                    if i > 1:
                        dve.wait_ge(m.solve, done - 1 + s)
                    r = slice(SUB * s, SUB * s + i)
                    nc.vector.tensor_tensor(m.prod[:, s, :, 0:i, 0:i], bc(m.an[:, s, :, i, 0:i], 2, i),
                                            xl[:, :, r, r].rearrange("p g j k -> p g k j"),
                                            ALU.mult).then_inc(m.solve, 1)

            def sums(p, i):
                done = p * (ROW_STEPS * (SUB - 1)) + ROW_STEPS * (i - 1)
                for s in range(2):
                    dve.wait_ge(m.solve, done + 1 + s)
                    nc.vector.tensor_reduce(xl[:, :, SUB * s + i, SUB * s:SUB * s + i],
                                            m.prod[:, s, :, 0:i, 0:i], AX, ALU.add).then_inc(m.solve, 1)

            def back(p, half):
                if half == 0:
                    dve.wait_ge(m.solve, (p + 1) * (ROW_STEPS * (SUB - 1)))
                    if not isinstance(p, int) or p > 0:
                        dve.wait_ge(m.r_xc, p * (2 * PT))
                for g in range(half * GP // 2, (half + 1) * GP // 2):
                    nc.vector.transpose(m.xb[:, g, :], m.xl[:, g, :]).then_inc(m.x_back, 1)
                if half == 1:
                    dve.wait_ge(m.x_back, (p + 1) * GP)

            def solve_slot(p, n):
                if n < GP:
                    systems(p, n)
                elif n < GP + WHOLE_ROWS:
                    products(p, n - GP + 1)
                    sums(p, n - GP + 1)
                elif n < SLOTS - 2:
                    i, part = divmod(n - GP - WHOLE_ROWS, 2)
                    (products, sums)[part](p, WHOLE_ROWS + 1 + i)
                elif n < SLOTS:
                    back(p, n - (SLOTS - 2))

            def iteration(p, recur, solve, gram):
                if not recur:
                    for n in range(SLOTS if solve else 0):
                        solve_slot(p + 1, n)
                    return
                for i in range(PT):
                    c, u = p * PT + i, i % 2
                    dve.wait_ge(m.r_wu, 4 * c + 4)
                    for s in range(2):
                        dve.wait_ge(m.r_ws, 2 * c + s + 1)
                        dve.wait_ge(m.r_vo, 2 * c + s + 1)
                        split = "p (k j e) -> p k j e"
                        nc.vector.tensor_tensor(
                            m.vn[:, s].rearrange(split, k=2, j=4), m.wu[:, u, 1].rearrange(split, k=2, j=4),
                            m.psum[:, 4:8, 0:64].rearrange("p j (k e) -> p k j e", k=2),
                            ALU.subtract).then_inc(m.r_vn, 1)
                        if solve:
                            solve_slot(p + 1, 4 * i + 2 * s)
                        dve.wait_ge(m.r_ds, 2 * c + s + 3)
                        nc.vector.tensor_tensor(
                            m.ds[:], m.psum[:, 4:8, 64:128].rearrange("p b (k e) -> p b k e", k=2),
                            bc(bc(m.pairmask[:, 0:32], 1, 2), 1, NB), ALU.mult).then_inc(m.r_dsm, 1)
                        dve.wait_ge(m.r_dsm, 2 * c + s + 1)
                        nc.vector.tensor_tensor(m.s[:], m.s[:], m.ds[:], ALU.add).then_inc(m.r_s, 1)
                        if solve:
                            solve_slot(p + 1, 4 * i + 2 * s + 1)

            nc.vector.memset(m.xl[:], 0.0).then_inc(m.x_clear, 1)
            dve.wait_ge(m.x_clear, 1)
            nc.vector.memset(m.xl[:, :, 0:1024:33], 1.0).then_inc(m.x_clear, 1)
            nc.vector.memset(m.s[:], 0.0).then_inc(m.r_s, 1)
            dve.wait_ge(m.x_clear, 2)
            everywhere(dve, iteration, nothing)

        @block.sync
        def _(sp):
            for p in range(NC // PT):
                sp.wait_ge(m.r_v, PT * (p + 1) + 1)
                sp.dma_start(m.v_dram[:, PT * p:PT * p + PT, :], m.v[:, PT * p:PT * p + PT, :]).then_inc(m.r_stored, 16)
            sp.wait_ge(m.r_stored, 16 * (NC // PT))


def split_and_stack(pool, held, stack, x, rest, parts, done, base):
    term = [[t for t in range(TERMS) if parts[t] == k] for k in range(3)]
    n = 0
    for k in range(3):
        out = stack[:, :, :, term[k][0], :]
        source = x if k == 0 else rest
        if n:
            hold(pool, done, base + n, held)
        pool.tensor_copy(out, source).then_inc(done, 1)
        n += 1
        hold(pool, done, base + n, held)
        if k < 2:
            pool.tensor_tensor(rest, source, out, ALU.subtract).then_inc(done, 1)
            n += 1
        for t in term[k][1:]:
            pool.tensor_copy(stack[:, :, :, t, :], out).then_inc(done, 1)
            n += 1
    return n


STACK_STEPS = 3 + 2 + 3
FILLS = 8
MAX_TILES = [(j, t) for i in range(NQ // 2) for j in range(4) for t in (NQ - 1 - i, i)]
PIECES = [(j, t, a, min(a + 512, P * t + P)) for j, t in MAX_TILES for a in range(0, P * t + P, 512)]
NP = len(PIECES)
STEPS = 4 * NQ
MAX_STEPS = STEPS - 8
PARTS_STEP = MAX_STEPS + 2
FILL_STEPS = [MAX_STEPS, MAX_STEPS + 1] + [PARTS_STEP + 1 + i for i in range(FILLS - 2)]
FILL_BANKS = (6, 7, 7, 6, 7, 6, 7, 6)
MAX_OPS = 6


def attention(nc, m):
    bank, bank16 = m.bank, m.bank16

    def everywhere(engine, iteration):
        iteration(-1, NG - 2, False, True)
        iteration(-1, NG - 1, True, True)
        with engine.Fori(0, NB - 1) as seq:
            for g in range(NG):
                iteration(seq, g, True, True)
        for g in range(NG):
            iteration(NB - 1, g, g < NG - 1, g < NG - 2)

    def copy_operand(copy, operand, g, n):
        h = 4 * ((g + 2) % NG)
        return copy(operand[0:QROWS, h:h + 4, 2 * P * (n % 4):2 * P * (n % 4) + 2 * P],
                    bank16(FILL_BANKS[n])[0:QROWS, :].rearrange("p (h t) -> p h t", h=4))

    def scores(n):
        return flat(m.psum[:, 2 * (n % 2):2 * (n % 2) + 2, :])

    sums = flat(m.psum[:, 4:6, :])

    with nc.Block() as block:

        @block.sync
        def _(sp):
            def load(buffers, seq):
                for i in buffers:
                    dst, src = ((m.kn, m.kb_dram), (m.qn, m.q_dram), (m.vn2, m.v_dram))[i]
                    for cc in range(4):
                        rows = src.rearrange("(b i) (t c) d -> c b i t d", b=NB, c=4)[cc, bass.ds(seq, 1)]
                        sp.dma_start(dst[32 * cc:32 * cc + 32], rows.rearrange("b i t d -> (b i) t d")) \
                            .then_inc(m.a_loaded[i], 16)

            def iteration(seq, g, maxima, operands):
                unit = seq * NG + g
                if g == NG - 2 and operands and not isinstance(seq, int):
                    sp.wait_ge(m.a_q, (unit + 2) * STACK_STEPS)
                    sp.wait_ge(m.a_k, (unit + 2) * STACK_STEPS)
                    load((1, 0), seq + 1)
                    sp.wait_ge(m.v_vg, unit + 2)
                    load((2,), seq + 1)
                if g == 0:
                    sp.dma_start(m.xres[:], m.x_seq[:, bass.ds(seq * NQ, NQ), :]).then_inc(m.o_x, 16)
                if maxima:
                    sp.wait_ge(m.m_rows, unit + 2)
                    sp.dma_start(m.max_dram, m.mrows[:]).then_inc(m.m_out, 16)
                    sp.wait_ge(m.m_out, unit * 16 + 32)
                    h = 4 * ((g + 1) % NG)
                    sp.dma_start(m.qs[QROWS:SROWS, h:h + 4, :], m.max_dram.rearrange("(r h) t -> r h t", r=3)) \
                        .then_inc(m.m_in, 16)
                    hold(sp, m.m_in, unit * 16 + 32, m.held_sp)
                if g == NG - 1 and not (isinstance(seq, int) and seq < 0):
                    for t in range(NQ):
                        sp.wait_ge(m.o_x1, seq * NQ + t + 2)
                        sp.dma_start(m.x1_dram[:, bass.ds(seq * NQ + t, 1), :], m.xres[:, t:t + 1, :]) \
                            .then_inc(m.o_st, 16)
                    hold(sp, m.o_st, seq * (16 * NQ) + 16 * NQ, m.held_sp)
                    hold(sp, m.o_bn, seq * NQ + NQ, m.held_sp)

            load((1, 0, 2), 0)
            sp.dma_start(m.wo[:], m.wo_dram).then_inc(m.a_const, 16)
            sp.dma_start(m.masks[:], m.c_masks).then_inc(m.a_const, 16)
            everywhere(sp, iteration)

        @block.gpsimd
        def _(pool):
            def iteration(seq, g, maxima, operands):
                unit = seq * NG + g
                if maxima:
                    if g == NG - 1:
                        hold(pool, m.a_loaded[2], seq * 64 + 128, m.held_pool)
                    if not isinstance(seq, int) or seq >= 0:
                        hold(pool, m.v_o, unit * NQ + 2, m.held_pool)
                    h = 4 * ((g + 1) % NG)
                    nc.gpsimd.tensor_copy(
                        m.vg[:, (g + 1) % 2, :, :, 0:HD],
                        m.vn2[:, :, HD * h:HD * h + 64].rearrange("p t (j e) -> p t j e", j=4)).then_inc(m.v_vg, 1)
                if operands:
                    if not isinstance(seq, int) or seq >= 0:
                        hold(pool, m.a_t, unit * FILLS + FILLS, m.held_pool)
                    h = 4 * ((g + 2) % NG)
                    for i, stage, source, parts, done in ((1, m.stage_q, m.qn, Q_PARTS, m.a_q),
                                                          (0, m.stage_k, m.kn, K_PARTS, m.a_k)):
                        if g == NG - 2:
                            hold(pool, m.a_loaded[i], seq * 64 + 128, m.held_pool)
                        split_and_stack(nc.gpsimd, m.held_pool, stage[:, g % 2],
                                        source[:, :, HD * h:HD * h + 64].rearrange("p t (j e) -> p t j e", j=4),
                                        m.rest[:], parts, done, (unit + 2) * STACK_STEPS)

            nc.gpsimd.memset(m.vg[:], 0.0).then_inc(m.a_vg, 1)
            pool.wait_ge(m.a_vg, 1)
            nc.gpsimd.memset(m.vg[:, :, :, :, HD:HD + 1], 1.0).then_inc(m.a_vg, 1)
            everywhere(pool, iteration)

        @block.tensor
        def _(pe):
            def iteration(seq, g, maxima, operands):
                unit = seq * NG + g
                now, after, later = 4 * g, 4 * ((g + 1) % NG), 4 * ((g + 2) % NG)
                first = isinstance(seq, int) and seq < 0

                def score(kt, j):
                    pe.wait_ge(m.v_exp, unit * STEPS + 4 * kt + j + 1)
                    if kt == 0 and j == 0:
                        pe.wait_ge(m.m_in, unit * 16 + 16)
                    out = scores(j)
                    k = m.ks[0:SROWS, now + j, P * kt:P * kt + P]
                    cuts = [P * kt, 512, N] if kt < 4 else [P * kt, N]
                    for a, z in zip(cuts, cuts[1:]):
                        last = nc.tensor.matmul(out[:, a:z], k, m.qs[0:SROWS, now + j, a:z],
                                                start=True, stop=a != P * kt)
                        if a == P * kt:
                            last = nc.tensor.matmul(out[:, a:a + P], m.ident16[:], m.mask_kq[:],
                                                    start=False, stop=True)
                    last.then_inc(m.v_s, 1)

                def values(kt, i):
                    piece, pair = divmod(i, 2)
                    a, z = max(512 * piece, P * kt), 512 * piece + 512
                    if a >= z:
                        return
                    if i == 0 or (a == P * kt and pair == 0):
                        pe.wait_ge(m.v_exp, unit * STEPS + 4 * kt + 6)
                    if kt == 0 and i == 0:
                        pe.wait_ge(m.v_read, unit + 1)
                        pe.wait_ge(m.v_vg, unit + 1)
                        if g == 0:
                            pe.wait_ge(m.o_x1, seq * NQ + 1)
                    for j in (2 * pair, 2 * pair + 1):
                        last = nc.tensor.matmul(sums[32 * j:32 * j + 32, a:z], m.vg[:, g % 2, kt, j, :],
                                                m.p[:, 4 * (kt % 2) + j, a:z], start=kt == 0,
                                                stop=kt == 4 * piece + 3)
                    if i == 3:
                        last.then_inc(m.v_o, 1)

                def maximum(i):
                    j, t, a, z = PIECES[i]
                    if i == 0:
                        pe.wait_ge(m.a_ke, (unit + 2) * NG)
                    elif i > 1:
                        pe.wait_ge(m.m_max, (unit + 1) * NP + i - 1)
                    out = bank(6 + i % 2)[:, 0:z - a]
                    diagonal = z == P * t + P
                    last = nc.tensor.matmul(out, m.qs[0:QROWS, after + j, P * t:P * t + P],
                                            m.ks[0:QROWS, after + j, a:z], start=True, stop=not diagonal)
                    if diagonal:
                        last = nc.tensor.matmul(out[:, z - a - P:z - a], m.ident16[:], m.mask_qk[:],
                                                start=False, stop=True)
                    last.then_inc(m.m_s, 1)

                def maxima_parts():
                    pe.wait_ge(m.m_part, (unit + 2) * MAX_OPS)
                    if operands:
                        pe.wait_ge(m.a_qe, (unit + 2) * NG + 1)
                    for t in range(NQ):
                        last = nc.tensor.transpose(bank16(6)[0:12, P * t:P * t + P],
                                                   m.mparts[:, t].rearrange("p r h -> p (r h)"), m.ident16[:])
                    last.then_inc(m.m_t, 1)

                def fill(n):
                    staged, stage = ((m.a_q, m.stage_q), (m.a_k, m.stage_k))[n // 4]
                    if n % 4 == 0:
                        pe.wait_ge(staged, (unit + 3) * STACK_STEPS)
                    done = (unit + 2) * NG
                    if n < 2:
                        if maxima:
                            pe.wait_ge(m.m_max, (unit + 1) * NP + NP - 1 + n)
                    elif n == 3 and maxima:
                        pe.wait_ge(m.m_rows, unit + 2)
                    elif n < 6:
                        pe.wait_ge(m.a_qe, done + (2, 1, 3, 4)[n - 2])
                    else:
                        pe.wait_ge(m.a_ke, done + n - 5)
                    for j in range(4):
                        for i in range(2):
                            last = nc.tensor.transpose(
                                bank16(FILL_BANKS[n])[0:QROWS, P * (2 * j + i):P * (2 * j + i + 1)],
                                stage[:, g % 2, 2 * (n % 4) + i, j].rearrange("p r e -> p (r e)"), m.ident16[:])
                    last.then_inc(m.a_t, 1)

                for kt in range(NQ + 1):
                    for j in range(4):
                        step = 4 * kt + j
                        if kt < NQ and not first:
                            score(kt, j)
                        if maxima and step < MAX_STEPS:
                            maximum(2 * step)
                        if maxima and step == PARTS_STEP:
                            maxima_parts()
                        if operands and step in FILL_STEPS:
                            fill(FILL_STEPS.index(step))
                        if kt > 0 and not first:
                            values(kt - 1, j)
                        if maxima and step < MAX_STEPS:
                            maximum(2 * step + 1)
                if g == NG - 1 and not first:
                    output(seq)

            def output(seq):
                def turn(t):
                    if t >= 2:
                        pe.wait_ge(m.o_n, seq * (2 * NQ) + 2 * t - 2)
                    for g in range(NG):
                        last = nc.tensor.transpose(bank(t % 2)[:, P * g:P * g + P], m.ot[:, g, P * t:P * t + P],
                                                   m.ident[:])
                    last.then_inc(m.o_t, 1)

                pe.wait_ge(m.v_read, seq * NG + NG + 1)
                turn(0)
                for t in range(NQ):
                    if t + 1 < NQ:
                        turn(t + 1)
                    pe.wait_ge(m.o_n, seq * (2 * NQ) + 2 * t + 2)
                    if t >= 2:
                        pe.wait_ge(m.o_te, seq * NQ + t - 1)
                    for k in range(2):
                        last = nc.tensor.transpose(bank(2 + t % 2)[:, P * k:P * k + P],
                                                   m.on[:, t % 2, P * k:P * k + P], m.ident[:])
                    last.then_inc(m.o_tt, 1)
                    pe.wait_ge(m.o_te, seq * NQ + t + 1)
                    if t >= 2:
                        pe.wait_ge(m.o_x1, seq * NQ + t)
                    for k in range(2):
                        last = nc.tensor.matmul(bank(4 + t % 2)[:, 0:D], m.ont[:, t % 2, k, :], m.wo[:, k, :],
                                                start=k == 0, stop=k == 1)
                    last.then_inc(m.o_mm, 1)

            pe.wait_ge(m.a_masks, 3)
            pe.wait_ge(m.a_vg, 2)
            everywhere(pe, iteration)

        @block.scalar
        def _(act):
            def iteration(seq, g, maxima, operands):
                unit = seq * NG + g
                first = isinstance(seq, int) and seq < 0
                for step in range(STEPS):
                    kt, j = divmod(step, 4)
                    if not first:
                        act.wait_ge(m.v_s, unit * STEPS + step + 1)
                        if j == 0:
                            act.wait_ge(m.v_o, unit * NQ + kt + 1)
                        nc.scalar.activation(m.p[:, 4 * (kt % 2) + j, P * kt:N], scores(j)[:, P * kt:N],
                                             ACT.Exp).then_inc(m.v_exp, 1)
                    if operands and step in FILL_STEPS[:NG]:
                        n = FILL_STEPS.index(step)
                        act.wait_ge(m.a_t, (unit + 2) * FILLS + n + 1)
                        copy_operand(nc.scalar.copy, m.qs, g, n).then_inc(m.a_qe, 1)
                if g == NG - 1 and not first:
                    for t in range(NQ):
                        act.wait_ge(m.o_tt, seq * NQ + t + 1)
                        if t >= 2:
                            act.wait_ge(m.o_mm, seq * NQ + t - 1)
                        nc.scalar.copy(flat(m.ont[:, t % 2]), bank(2 + t % 2)[:, 0:D]).then_inc(m.o_te, 1)

            everywhere(act, iteration)

        @block.vector
        def _(dve):
            def maxima_of(unit):
                for i, (j, t, a, z) in enumerate(PIECES):
                    dve.wait_ge(m.m_s, unit * NP + i + 1)
                    nc.vector.tensor_reduce(m.nmax[:, a // 512, t, j:j + 1], bank(6 + i % 2)[:, 0:z - a], AX, ALU.max,
                                            negate=True).then_inc(m.m_max, 1)
                dve.wait_ge(m.m_max, unit * NP + NP)
                nm = m.nmax[:, 0]
                nc.vector.tensor_tensor(nm[:, 4:NQ], nm[:, 4:NQ], m.nmax[:, 1, 4:NQ], ALU.min).then_inc(m.m_part, 1)
                n = 1
                dve.wait_ge(m.m_part, unit * MAX_OPS + n)
                for k in range(3):
                    nc.vector.tensor_copy(m.mparts[:, :, k, :], nm).then_inc(m.m_part, 1)
                    n += 1
                    dve.wait_ge(m.m_part, unit * MAX_OPS + n)
                    if k < 2:
                        nc.vector.tensor_tensor(nm, nm, m.mparts[:, :, k, :], ALU.subtract).then_inc(m.m_part, 1)
                        n += 1
                        dve.wait_ge(m.m_part, unit * MAX_OPS + n)
                assert n == MAX_OPS
                dve.wait_ge(m.m_t, unit + 1)
                if not isinstance(unit, int) or unit > 0:
                    dve.wait_ge(m.m_out, unit * 16)
                nc.vector.tensor_copy(m.mrows[:], bank16(6)[0:12, :]).then_inc(m.m_rows, 1)

            def output(seq):
                def divide(t):
                    dve.wait_ge(m.o_t, seq * NQ + t + 1)
                    o = bank(t % 2).rearrange("p (h e) -> p h e", h=H)
                    nc.vector.reciprocal(m.rsum[:, t % 2], o[:, :, HD]).then_inc(m.o_n, 1)
                    dve.wait_ge(m.o_n, seq * (2 * NQ) + 2 * t + 1)
                    if t >= 2:
                        dve.wait_ge(m.o_tt, seq * NQ + t - 1)
                    nc.vector.tensor_tensor(m.on[:, t % 2].rearrange("p (h e) -> p h e", h=H), o[:, :, 0:HD],
                                            bc(m.rsum[:, t % 2], 2, HD), ALU.mult).then_inc(m.o_n, 1)

                divide(0)
                dve.wait_ge(m.o_x, seq * 16 + 16)
                for t in range(NQ):
                    if t + 1 < NQ:
                        divide(t + 1)
                    dve.wait_ge(m.o_mm, seq * NQ + t + 1)
                    nc.vector.tensor_tensor(m.xres[:, t, :], bank(4 + t % 2)[:, 0:D], m.xres[:, t, :], ALU.add) \
                        .then_inc(m.o_x1, 1)
                for t in range(NQ):
                    dve.wait_ge(m.o_x1, seq * NQ + t + 2)
                    nc.vector.bn_stats(m.stats2[:, bass.ds(seq * NQ + t, 1), :].rearrange("p a f -> p (a f)"),
                                       m.xres[:, t, :]).then_inc(m.o_bn, 1)

            def iteration(seq, g, maxima, operands):
                unit = seq * NG + g
                if maxima:
                    maxima_of(unit + 1)
                if operands:
                    for n in range(NG, FILLS):
                        dve.wait_ge(m.a_t, (unit + 2) * FILLS + n + 1)
                        copy_operand(nc.vector.tensor_copy, m.ks, g, n).then_inc(m.a_ke, 1)
                if not isinstance(seq, int) or seq >= 0:
                    dve.wait_ge(m.v_o, unit * NQ + NQ + 2)
                    nc.vector.tensor_copy(m.ot[:, g, :], sums).then_inc(m.v_read, 1)
                    if g == NG - 1:
                        output(seq)

            nc.vector.memset(m.ks[QROWS:SROWS], 1.0).then_inc(m.a_masks, 1)
            dve.wait_ge(m.a_const, 32)
            nc.vector.tensor_copy(m.mask_qk[:], m.masks[:, 0, :]).then_inc(m.a_masks, 1)
            nc.vector.tensor_copy(m.mask_kq[:], m.masks[:, 1, :]).then_inc(m.a_masks, 1)
            everywhere(dve, iteration)


def second_norm(nc, m):
    bank = m.bank
    experts_in, shared_in = slice(0, E * I), slice(E * I, IT)
    whole = E * I // P
    cut = NI // 2

    def up_piece(w, shared, k):
        return [(lambda buf: buf[:, experts_in].rearrange("p (e i) -> p e i", e=E),
                 w.rearrange("e (k p) i -> k p e i", p=P)[k]),
                (lambda buf: buf[:, shared_in], shared.rearrange("(k p) i -> k p i", p=P)[k])]

    def down(n0, n1):
        return lambda buf: buf[:, D * n0:D * n1].rearrange("p (n h) -> p n h", h=D)

    experts_down = m.w_down.rearrange("e i h -> (e i) h").rearrange("(n p) h -> p n h", p=P)
    pieces = [up_piece(m.w_gate, m.sw_gate, 0), up_piece(m.w_gate, m.sw_gate, 1),
              up_piece(m.w_up, m.sw_up, 0), up_piece(m.w_up, m.sw_up, 1),
              [(lambda buf: buf[0:3 * (E + 1), 0:NI * P], m.c_sel)],
              [(down(0, cut), experts_down[:, 0:cut, :])],
              [(down(0, whole - cut), experts_down[:, cut:whole, :]),
               (down(whole - cut, NI - 1 - cut), m.sw_down[0:IS - LAST, :].rearrange("(n p) h -> p n h", p=P)),
               (lambda buf: buf[0:LAST, D * (NI - 1 - cut):D * (NI - cut)], m.sw_down[IS - LAST:IS, :])]]
    parts = [[w[:, i, k, :] for i in range(2)] for w in (m.wg, m.wu_ffn) for k in range(2)]
    parts += [None, [m.wd[:, i, 0:cut].rearrange("p n h -> p (n h)") for i in range(2)],
              [m.wd[:, i, cut:NI].rearrange("p n h -> p (n h)") for i in range(2)]]
    SELECTION = 4

    def raw(i):
        width = NI * P if i <= SELECTION else (cut if i == 5 else NI - cut) * D
        return m.piece[:, i % 2, 0:width]

    def loaded(i):
        return 16 * sum(len(pieces[j]) for j in range(i % 2, i + 1, 2))

    with nc.Block() as block:

        @block.sync
        def _(sp):
            def load(s):
                sp.dma_start(m.xg[:, s % 2], m.x1_dram[:, 4 * s:4 * s + 4, :]).then_inc(m.f_x[s % 2], 16)

            load(0)
            load(1)
            sp.dma_start(m.gt[:], m.router_w.rearrange("(k p) e -> p k e", p=P)).then_inc(m.f_gate, 16)
            sp.dma_start(m.key[:], m.c_key).then_inc(m.f_const, 16)
            for s in range(NTG):
                if s + 2 < NTG:
                    sp.wait_ge(m.f_xn, s + 1)
                    load(s + 2)
                sp.wait_ge(m.f_te, 2 * s + 2)
                sp.dma_start(m.xt_dram[:, s], m.xs[:, s % 2]).then_inc(m.f_xs[s % 2], 16)
            for u in range(2):
                sp.wait_ge(m.f_xs[u], 16 * (NTG // 2))
            sp.wait_ge(m.f_const, 16)

        @block.scalar
        def _(act):
            def load(i):
                for dst, src in pieces[i]:
                    act.dma_start(dst(m.piece[:, i % 2]), src).then_inc(m.f_w[i % 2], 16)

            act.wait_ge(m.f_pad, 1)
            load(0)
            load(1)
            act.wait_ge(m.f_ln, 3)
            nc.scalar.activation(m.rstd[:], m.rstd[:], ACT.Sqrt).then_inc(m.f_sqrt, 1)
            for s in range(NTG):
                act.wait_ge(m.f_t, s + 1)
                if s >= 2:
                    act.wait_ge(m.f_xs[s % 2], 16 * (s // 2))
                    act.wait_ge(m.f_lg, s - 1)
                for k in range(2):
                    nc.scalar.copy(m.xs[:, s % 2, k, :], bank(k)[:]).then_inc(m.f_te, 1)
                if s < len(pieces):
                    act.wait_ge(m.f_w[s % 2], loaded(s))
                    if s == SELECTION:
                        nc.scalar.copy(m.sel[:].rearrange("p n j -> p (n j)"), raw(s)[0:3 * (E + 1)]) \
                            .then_inc(m.f_high, 1)
                    else:
                        nc.scalar.copy(parts[s][0], raw(s)).then_inc(m.f_high, 1)
                if 1 <= s < len(pieces) - 1:
                    act.wait_ge(m.f_low, s)
                    act.wait_ge(m.f_high, s)
                    if s + 1 == len(pieces) - 1:
                        act.wait_ge(m.f_pad, 2)
                    load(s + 1)

        @block.vector
        def _(dve):
            nc.vector.memset(m.piece[:, :, IT:NI * P], 0.0).then_inc(m.f_pad, 1)
            for t in range(NB * NQ):
                last = nc.vector.bn_aggr(m.mv[:, t, :], m.stats2[:, t, :])
            last.then_inc(m.f_ln, 1)
            dve.wait_ge(m.f_ln, 1)
            nc.vector.tensor_scalar(m.rstd[:], m.mv[:, :, 1], 1e-5, None, ALU.add).then_inc(m.f_ln, 1)
            nc.vector.tensor_copy(m.mean[:], m.mv[:, :, 0]).then_inc(m.f_ln, 1)
            dve.wait_ge(m.f_sqrt, 1)
            nc.vector.reciprocal(m.rstd[:], m.rstd[:]).then_inc(m.f_ln, 1)
            dve.wait_ge(m.f_ln, 4)
            for s in range(NTG):
                dve.wait_ge(m.f_x[s % 2], 16 * (s // 2) + 16)
                if s > 0:
                    dve.wait_ge(m.f_t, s)
                for q in range(4):
                    last = nc.vector.tensor_scalar(
                        m.xm[:, q, :], m.xg[:, s % 2, q, :], m.mean[:, 4 * s + q:4 * s + q + 1],
                        m.rstd[:, 4 * s + q:4 * s + q + 1], ALU.subtract, ALU.mult)
                last.then_inc(m.f_xn, 1)
                if s < len(pieces):
                    dve.wait_ge(m.f_high, s + 1)
                    if s == SELECTION:
                        nc.vector.memset(m.piece[LAST:, s % 2, D * (NI - 1 - cut):D * (NI - cut)], 0.0) \
                            .then_inc(m.f_pad, 1)
                        dve.sem_inc(m.f_low, 1)
                    else:
                        nc.vector.tensor_tensor(parts[s][1], raw(s), parts[s][0].bitcast(F32), ALU.subtract) \
                            .then_inc(m.f_low, 1)
                dve.wait_ge(m.f_lg, s + 1)
                nc.vector.tensor_copy(m.lg[:, 4 * s:4 * s + 4, :],
                                      bank(2)[:, 0:4 * (E + 1)].rearrange("p (q e) -> p q e", q=4)) \
                    .then_inc(m.f_lge, 1)

        @block.tensor
        def _(pe):
            pe.wait_ge(m.f_gate, 16)
            for s in range(NTG):
                pe.wait_ge(m.f_xn, s + 1)
                if s > 0:
                    pe.wait_ge(m.f_te, 2 * s)
                for k in range(2):
                    for q in range(4):
                        last = nc.tensor.transpose(bank(k)[:, P * q:P * q + P], m.xm[:, q, P * k:P * k + P],
                                                   m.ident[:])
                last.then_inc(m.f_t, 1)
                pe.wait_ge(m.f_te, 2 * s + 2)
                if s > 0:
                    pe.wait_ge(m.f_lge, s)
                for q in range(4):
                    for k in range(2):
                        last = nc.tensor.matmul(bank(2)[:, (E + 1) * q:(E + 1) * (q + 1)],
                                                m.xs[:, s % 2, k, P * q:P * q + P], m.gt[:, k, :],
                                                start=k == 0, stop=k == 1)
                last.then_inc(m.f_lg, 1)


def router(nc, m):
    NT = NB * NQ
    le, ex, gate = m.lg[:, :, 0:E], m.ex[:], m.lg[:, :, E]
    with nc.Block() as block:

        @block.vector
        def _(dve):
            n = 0

            def step(instruction):
                nonlocal n
                n += 1
                instruction.then_inc(m.t_dve, 1)
                dve.wait_ge(m.t_dve, n)

            key = bc(m.key[:], 1, NT)
            step(nc.vector.tensor_reduce(m.top[:], le, AX, ALU.max))
            step(nc.vector.tensor_tensor(ex, le, bc(m.top[:], 2, E), ALU.subtract))
            dve.wait_ge(m.t_exp, 2)
            step(nc.vector.tensor_reduce(m.top[:], ex, AX, ALU.max))
            step(nc.vector.tensor_copy(m.total[:], m.top[:]))
            step(nc.vector.tensor_copy(m.left[:], ex))
            for rank in range(2):
                step(nc.vector.tensor_tensor(m.hit[:], m.left[:], bc(m.top[:], 2, E), ALU.is_equal))
                step(nc.vector.tensor_tensor(m.hit[:], m.hit[:], key, ALU.mult))
                step(nc.vector.tensor_reduce(m.top[:], m.hit[:], AX, ALU.max))
                step(nc.vector.tensor_tensor(m.hit[:], key, bc(m.top[:], 2, E), ALU.is_equal))
                if rank == 0:
                    step(nc.vector.tensor_copy(m.chosen[:], m.hit[:]))
                    step(nc.vector.scalar_tensor_tensor(m.left[:], m.hit[:], -2.0, m.left[:], ALU.mult, ALU.add))
                    step(nc.vector.tensor_reduce(m.top[:], m.left[:], AX, ALU.max))
                    step(nc.vector.tensor_tensor(m.total[:], m.total[:], m.top[:], ALU.add))
                else:
                    step(nc.vector.tensor_tensor(m.chosen[:], m.chosen[:], m.hit[:], ALU.add))
            step(nc.vector.reciprocal(m.total[:], m.total[:]))
            step(nc.vector.tensor_tensor(m.chosen[:], m.chosen[:], ex, ALU.mult))
            step(nc.vector.tensor_tensor(m.comb[:, :, 0:E], m.chosen[:], bc(m.total[:], 2, E), ALU.mult))
            step(nc.vector.tensor_scalar(gate, gate, 1.0, None, ALU.add))
            step(nc.vector.reciprocal(m.comb[:, :, E], gate))
            for k in range(3):
                step(nc.vector.tensor_copy(m.cparts[:, :, k, :], m.comb[:]))
                if k < 2:
                    step(nc.vector.tensor_tensor(m.comb[:], m.comb[:], m.cparts[:, :, k, :], ALU.subtract))
            for g in range(4):
                dve.wait_ge(m.t_turn, g + 1)
                nc.vector.tensor_copy(m.ct[:, 1024 * g:1024 * g + 1024], m.bank16(g)[0:3 * (E + 1), :]) \
                    .then_inc(m.t_out, 1)

        @block.scalar
        def _(act):
            act.wait_ge(m.t_dve, 2)
            nc.scalar.activation(ex, ex, ACT.Exp).then_inc(m.t_exp, 1)
            nc.scalar.activation(gate, gate, ACT.Exp, scale=-1.0).then_inc(m.t_exp, 1)

        @block.tensor
        def _(pe):
            pe.wait_ge(m.t_dve, 5 + 8 + 5 + 5 + 5)
            for t in range(NT):
                last = nc.tensor.transpose(m.bank16(t // 8)[0:3 * (E + 1), P * (t % 8):P * (t % 8) + P],
                                           m.cparts[:, t].rearrange("p r e -> p (r e)"), m.ident16[:])
                if t % 8 == 7:
                    last.then_inc(m.t_turn, 1)


def experts(nc, m):
    bank = m.bank

    def before(s, n):
        return s * NI + n - 1 if n >= 2 else s * NI

    with nc.Block() as block:

        @block.sync
        def _(sp):
            def load(s, u):
                sp.dma_start(m.xt[:, u], m.xt_dram[:, bass.ds(s, 1)].rearrange("p a k t -> p (a k) t")) \
                    .then_inc(m.e_xt[u], 16)

            def group(s, u, more):
                sp.wait_ge(m.e_st, s * 16 + 1)
                sp.dma_start(m.xg[:, 0], m.x1_dram[:, bass.ds(s * 4, 4), :]).then_inc(m.e_x, 16)
                if more:
                    sp.wait_ge(m.e_parts, s * 2 + 2)
                    load(s + 2, u)
                sp.wait_ge(m.e_y, s * 2 + 3)
                sp.dma_start(m.out_seq[:, bass.ds(s * 4, 4), :], m.xg[:, 0]).then_inc(m.e_st, 16)

            for u in range(2):
                load(u, u)
            with sp.Fori(0, NTG // 2 - 1) as ss:
                for u in range(2):
                    group(ss * 2 + u, u, True)
            for u in range(2):
                group(NTG - 2 + u, u, False)
            sp.wait_ge(m.e_st, 16 * NTG + 1)

        @block.gpsimd
        def _(pool):
            def split(s, ss, u, first):
                hold(pool, m.e_xt[u], ss * 16 + 16, m.held_pool)
                if not first:
                    hold(pool, m.e_g, s * NI - NI, m.held_pool)
                nc.gpsimd.tensor_copy(m.xtp[:, u, 0], m.xt[:, u]).then_inc(m.e_parts, 1)
                hold(pool, m.e_parts, s * 2 + 1, m.held_pool)
                nc.gpsimd.tensor_tensor(m.xtp[:, u, 1], m.xt[:, u], m.xtp[:, u, 0].bitcast(F32), ALU.subtract) \
                    .then_inc(m.e_parts, 1)

            for u in range(2):
                split(u, 0, u, True)
            with pool.Fori(1, NTG // 2) as ss:
                for u in range(2):
                    split(ss * 2 + u, ss, u, False)

        @block.tensor
        def _(pe):
            def up(s, u, n):
                if n == 0:
                    pe.wait_ge(m.e_parts, s * 2 + 2)
                pe.wait_ge(m.e_h, before(s, n) + 1)
                f = slice(P * n, P * n + P)
                for i, w in enumerate((m.wg, m.wu_ffn)):
                    for k in range(2):
                        for a, b in PRODUCTS:
                            nc.tensor.matmul(bank(3 * (n % 2) + i)[:], w[:, a, k, f], m.xtp[:, u, b, k],
                                             start=(k, a, b) == (0, 0, 1), stop=(k, a, b) == (1, 0, 0))
                nc.tensor.matmul(bank(3 * (n % 2) + 2)[:], m.sel[:, n, :], m.ct[:, bass.ds(s * TG, TG)],
                                 start=True, stop=True).then_inc(m.e_g, 1)

            def down(s, n):
                pe.wait_ge(m.e_h, s * NI + n + 2)
                pe.wait_ge(m.e_low, s * NI + n + 1)
                if n == 0:
                    pe.wait_ge(m.e_y, s * 2 + 1)
                for q in range(4):
                    for a, b in PRODUCTS:
                        last = nc.tensor.matmul(bank(6 + q // 2)[:, D * (q % 2):D * (q % 2) + D],
                                                m.h[:, n % 2, a, P * q:P * q + P], m.wd[:, b, n, :],
                                                start=n == 0 and q % 2 == 0 and (a, b) == (0, 1),
                                                stop=n == NI - 1 and (a, b) == (0, 0), skip_group_check=True)
                last.then_inc(m.e_d, 1)

            with pe.Fori(0, NTG // 2) as ss:
                for u in range(2):
                    s = ss * 2 + u
                    up(s, u, 0)
                    for n in range(NI):
                        if n + 1 < NI:
                            up(s, u, n + 1)
                        down(s, n)

        @block.scalar
        def _(act):
            with act.Fori(0, NTG) as s:
                for n in range(NI):
                    act.wait_ge(m.e_g, s * NI + n + 1)
                    act.wait_ge(m.e_h, before(s, n) + 1)
                    nc.scalar.activation(m.sg[:, n % 2, :], bank(3 * (n % 2))[:], ACT.Silu).then_inc(m.e_s, 1)

        @block.vector
        def _(dve):
            with dve.Fori(0, NTG) as s:
                for n in range(NI):
                    dve.wait_ge(m.e_s, s * NI + n + 1)
                    nc.vector.tensor_tensor(m.sg[:, n % 2, :], m.sg[:, n % 2, :], bank(3 * (n % 2) + 1)[:],
                                            ALU.mult).then_inc(m.e_t, 1)
                    dve.wait_ge(m.e_t, s * NI + n + 1)
                    nc.vector.tensor_tensor(m.hw[:, n % 2], m.sg[:, n % 2, :], bank(3 * (n % 2) + 2)[:],
                                            ALU.mult).then_inc(m.e_h, 1)
                    dve.wait_ge(m.e_h, s * NI + n + 2)
                    dve.wait_ge(m.e_d, before(s, n) + 1)
                    nc.vector.tensor_copy(m.h[:, n % 2, 0], m.hw[:, n % 2]).then_inc(m.e_high, 1)
                    dve.wait_ge(m.e_high, s * NI + n + 1)
                    nc.vector.tensor_tensor(m.h[:, n % 2, 1], m.hw[:, n % 2], m.h[:, n % 2, 0].bitcast(F32),
                                            ALU.subtract).then_inc(m.e_low, 1)
                dve.wait_ge(m.e_d, s * NI + NI + 1)
                dve.wait_ge(m.e_x, s * 16 + 16)
                for i in range(2):
                    x = flat(m.xg[:, 0, 2 * i:2 * i + 2, :])
                    nc.vector.tensor_tensor(x, bank(6 + i)[:], x, ALU.add).then_inc(m.e_y, 1)


def layer(nc, ins, consts, out):
    m = Memory()
    (m.x_in, m.Wq, m.Wk, m.Wv, m.wo_dram, m.Wb, m.w_gate, m.w_up, m.w_down, m.sw_gate, m.sw_up, m.sw_down,
     m.router_w) = ins
    (m.c_cos, m.c_sin, m.c_ident, m.c_rowmask, m.c_pairmask, m.c_masks, m.c_sel, m.c_key) = consts
    m.x_seq = m.x_in.rearrange("b (t p) d -> p (b t) d", p=P)
    m.out_seq = out.rearrange("b (t p) d -> p (b t) d", p=P)
    m.wo_dram = m.wo_dram.rearrange("(k p) n -> p k n", p=P)

    def dram(name, shape, dt=F32):
        return nc.dram_tensor(name, shape, dt, kind="Internal").ap()

    m.q_dram = dram("q_dram", [P, NC, D])
    m.kb_dram = dram("kb_dram", [P, NC, D])
    m.v_dram = dram("v_dram", [P, NC, D])
    m.x1_dram = dram("x1_dram", [P, NB * NQ, D])
    m.xt_dram = dram("xt_dram", [P, NTG, 2, TG])
    m.max_dram = dram("max_dram", [12, N], BF16)

    with ExitStack() as whole:
        def sems(names):
            return [whole.enter_context(nc.semaphore(name)) for name in names.split()]

        m.const_loaded, m.w_split, m.ln_ready, m.ln_sqrt, m.ln_done, m.bn_done = sems(
            "const_loaded w_split ln_ready ln_sqrt ln_done bn_done")
        m.p_xn, m.p_xt, m.p_high, m.p_low, m.p_qk, m.p_rot, m.p_rope, m.p_v = sems(
            "p_xn p_xt p_high p_low p_qk p_rot p_rope p_v")
        m.k_sq, m.k_ss, m.k_sqrt, m.k_beta, m.k_lane, m.k_norm, m.k_kb, m.k_kb_last, m.k_stored = sems(
            "k_sq k_ss k_sqrt k_beta k_lane k_norm k_kb k_kb_last k_stored")
        m.g_kc, m.g_kt, m.g_kt1, m.g_kt2, m.g_mm, m.g_out, m.g_tr = sems("g_kc g_kt g_kt1 g_kt2 g_mm g_out g_tr")
        m.solve, m.x_back, m.x_clear, m.g_an, m.held, m.held_sp, m.held_pool = sems("solve x_back x_clear g_an held held_sp held_pool")
        m.r_xc, m.r_wu_mm, m.r_wu, m.r_wt_mm, m.r_wt, m.r_kb, m.r_ws = sems("r_xc r_wu_mm r_wu r_wt_mm r_wt r_kb r_ws")
        m.r_vn, m.r_ds, m.r_dsm, m.r_s, m.r_vo, m.r_v, m.r_stored = sems("r_vn r_ds r_dsm r_s r_vo r_v r_stored")
        m.a_const, m.a_masks, m.a_vg, m.a_k, m.a_q, m.a_t, m.a_qe = sems("a_const a_masks a_vg a_k a_q a_t a_qe")
        m.a_ke, = sems("a_ke")
        m.m_max, m.m_s, m.m_part, m.m_t, m.m_rows, m.m_out, m.m_in = sems("m_max m_s m_part m_t m_rows m_out m_in")
        m.v_read, m.v_vg, m.v_exp, m.v_s, m.v_o = sems("v_read v_vg v_exp v_s v_o")
        m.o_x, m.o_x1, m.o_st, m.o_n, m.o_t, m.o_te, m.o_tt = sems("o_x o_x1 o_st o_n o_t o_te o_tt")
        m.o_mm, m.o_bn = sems("o_mm o_bn")
        m.f_gate, m.f_pad, m.f_const, m.f_xn, m.f_ln, m.f_sqrt = sems("f_gate f_pad f_const f_xn f_ln f_sqrt")
        m.f_t, m.f_lg, m.f_lge, m.f_te, m.f_high, m.f_low = sems("f_t f_lg f_lge f_te f_high f_low")
        m.t_dve, m.t_exp, m.t_turn, m.t_out = sems("t_dve t_exp t_turn t_out")
        m.e_st, m.e_x, m.e_y, m.e_h, m.e_g, m.e_d, m.e_t = sems("e_st e_x e_y e_h e_g e_d e_t")
        m.e_s, m.e_parts, m.e_high, m.e_low = sems("e_s e_parts e_high e_low")
        m.starts = [
            (m.e_d, 1), (m.e_h, 1), (m.e_st, 1), (m.e_y, 1), (m.g_an, 1), (m.g_kt, 1), (m.g_kt1, 1), (m.g_mm, 1), (m.g_out, 1),
            (m.o_x1, 1), (m.p_rope, 2), (m.p_rot, 5), (m.p_v, 2),
            (m.r_ds, 2), (m.r_v, 1), (m.r_vo, 2), (m.v_exp, 2), (m.v_o, 2), (m.v_read, 1), 
        ]
        m.x_loaded = sems("x_loaded0 x_loaded1 x_loaded2 x_loaded3")
        m.a_loaded = sems("a_loaded0 a_loaded1 a_loaded2")
        m.f_x = sems("f_x0 f_x1")
        m.f_xs = sems("f_xs0 f_xs1")
        m.f_w = sems("f_w0 f_w1")
        m.e_xt = sems("e_xt0 e_xt1")
        m.psum = whole.enter_context(nc.psum_tensor("psum", [P, 8, 512], F32))[:]
        m.bank = lambda i: m.psum[:, i, :]
        m.bank16 = lambda i: m.psum[:, i, :].bitcast(BF16)

        def sb(stack, name, shape, dt=F32):
            return stack.enter_context(nc.sbuf_tensor(name, shape, dt))[:]

        m.ident = sb(whole, "ident", [P, P])
        m.ident16 = sb(whole, "ident16", [P, P], BF16)
        m.mv = sb(whole, "mv", [P, NC, 2])
        m.mean = sb(whole, "mean", [P, NC])
        m.rstd = sb(whole, "rstd", [P, NC])
        m.stats2 = sb(whole, "stats2", [P, NC, 6])
        with ExitStack() as first:
            m.q = sb(first, "q", [P, NC, D])
            m.kv = sb(first, "kv", [P, NC, 2, D])
            m.beta = sb(first, "beta", [P, NC, H])
            m.beta_half = sb(first, "beta_half", [P, 2, NC * H])
            m.beta_lane = sb(first, "beta_lane", [P, NC // 2, 2 * H])
            m.rowmask = sb(first, "rowmask", [P, 2])
            m.pairmask = sb(first, "pairmask", [P, 34])
            with ExitStack() as stack:
                m.x = sb(stack, "x", [P, NC, D])
                m.cosq = sb(stack, "cosq", [P, NC, 8])
                m.sinq = sb(stack, "sinq", [P, NC, 8])
                m.w_in = sb(stack, "w_in", [P, 2, 3 * D + H])
                m.stats = sb(stack, "stats", [P, NC, 6])
                m.xn = sb(stack, "xn", [P, 2, D])
                m.xnt = sb(stack, "xnt", [P, 2, 2, 2, P], F32R)
                m.w_parts = sb(stack, "w_parts", [P, 2, 2, 3 * D + H], F32R)
                m.rc = sb(stack, "rc", [P, 2, 2 * H, 2, 8])
                m.rs = sb(stack, "rs", [P, 2, 2 * H, 2, 8])
                m.rn = sb(stack, "rn", [P, NC, H])
                m.sq = m.x
                load_constants(nc, m)
                projections(nc, m)
                normalise_keys(nc, m)
            with ExitStack() as stack:
                m.xl = sb(stack, "xl", [P, GP, 1024])
                m.xb = sb(stack, "xb", [P, GP, 1024])
                m.an = sb(stack, "an", [P, 2, GP, SUB, SUB])
                m.prod = sb(stack, "prod", [P, 2, GP, SUB - 1, SUB - 1])
                m.gs = sb(stack, "gs", [P, GP, 1024])
                m.gram = sb(stack, "gram", [P, 1024])
                m.kc = sb(stack, "kc", [P, D])
                m.kt1 = sb(stack, "kt1", [P, 2, P])
                m.kt2 = sb(stack, "kt2", [P, 2, 2, P])
                m.xc = sb(stack, "xc", [P, 2, H, CT])
                m.kvc = sb(stack, "kvc", [P, 2, 2, D])
                m.wu = sb(stack, "wu", [P, 2, 2, D])
                m.wt = sb(stack, "wt", [P, 2, 2, P])
                m.kb = sb(stack, "kb", [P, 2, D])
                m.vn = sb(stack, "vn", [P, 2, D])
                m.vt = sb(stack, "vt", [P, 2, D])
                m.s = sb(stack, "s", [P, NB, 2, 32])
                m.ds = sb(stack, "ds", [P, NB, 2, 32])
                m.v = m.q
                delta_rule(nc, m)
        with ExitStack() as stack:
            m.kn = sb(stack, "kn", [P, NQ, D])
            m.qn = sb(stack, "qn", [P, NQ, D])
            m.vn2 = sb(stack, "vn2", [P, NQ, D])
            m.rest = sb(stack, "rest", [P, NQ, 4, HD])
            m.stage_k = sb(stack, "stage_k", [P, 2, NQ, 4, TERMS, HD], BF16)
            m.stage_q = sb(stack, "stage_q", [P, 2, NQ, 4, TERMS, HD], BF16)
            m.ks = sb(stack, "ks", [P, H, N], BF16)
            m.qs = sb(stack, "qs", [P, H, N], BF16)
            m.wo = sb(stack, "wo", [P, 2, D])
            m.masks = sb(stack, "masks", [P, 2, P])
            m.mask_qk = sb(stack, "mask_qk", [P, P], BF16)
            m.mask_kq = sb(stack, "mask_kq", [P, P], BF16)
            m.nmax = sb(stack, "nmax", [P, 2, NQ, 4])
            m.mparts = sb(stack, "mparts", [P, NQ, 3, 4], BF16)
            m.mrows = sb(stack, "mrows", [12, N], BF16)
            m.rsum = sb(stack, "rsum", [P, 2, H])
            m.vg = sb(stack, "vg", [P, 2, NQ, 4, 32])
            m.p = sb(stack, "p", [P, 8, N])
            m.ot = sb(stack, "ot", [P, NG, N])
            m.xres = sb(stack, "xres", [P, NQ, D])
            m.on = sb(stack, "on", [P, 2, D])
            m.ont = sb(stack, "ont", [P, 2, 2, P])
            attention(nc, m)
        with ExitStack() as stack:
            m.wg = sb(stack, "wg", [P, 2, 2, NI * P], F32R)
            m.wu_ffn = sb(stack, "wu_ffn", [P, 2, 2, NI * P], F32R)
            m.wd = sb(stack, "wd", [P, 2, NI, D], F32R)
            m.sel = sb(stack, "sel", [3 * (E + 1), NI, P], BF16)
            m.ct = sb(stack, "ct", [3 * (E + 1), NB * N], BF16)
            m.xg = sb(stack, "xg", [P, 2, 4, D])
            with ExitStack() as inner:
                m.piece = sb(inner, "piece", [P, 2, (NI - NI // 2) * D])
                m.gt = sb(inner, "gt", [P, 2, E + 1])
                m.key = sb(inner, "key", [P, E])
                m.xm = sb(inner, "xm", [P, 4, D])
                m.xs = sb(inner, "xs", [P, 2, 2, TG])
                m.lg = sb(inner, "lg", [P, NC, E + 1])
                m.ex = sb(inner, "ex", [P, NC, E])
                m.left = sb(inner, "left", [P, NC, E])
                m.hit = sb(inner, "hit", [P, NC, E])
                m.chosen = sb(inner, "chosen", [P, NC, E])
                m.top = sb(inner, "top", [P, NC])
                m.total = sb(inner, "total", [P, NC])
                m.comb = sb(inner, "comb", [P, NC, E + 1])
                m.cparts = sb(inner, "cparts", [P, NC, 3, E + 1], BF16)
                second_norm(nc, m)
                router(nc, m)
            m.xt = sb(stack, "xt_raw", [P, 2, 2, TG])
            m.xtp = sb(stack, "xt_parts", [P, 2, 2, 2, TG], F32R)
            m.sg = sb(stack, "sg", [P, 2, TG])
            m.hw = sb(stack, "hw", [P, 2, TG])
            m.h = sb(stack, "h", [P, 2, 2, TG], F32R)
            experts(nc, m)


def constants():
    p = np.arange(P)
    pos = (p[:, None] % CT + CT * np.arange(NC)[None, :]).astype(np.float32)
    inv = (np.float32(1.0) / np.float32(10000.0) ** (np.arange(0, HD, 2, dtype=np.float32) / np.float32(HD)))
    angle = pos[:, :, None] * inv.astype(np.float32)
    pair = np.zeros((P, 34), np.float32)
    pair[:, 0:32] = (p[:, None] % 32 // HD) == (np.arange(32)[None, :] // HD)
    pair[:, 32], pair[:, 33] = p % 32 < HD, p % 32 >= HD
    unit = np.arange(NI * P)
    owner = np.minimum(unit // I, E)
    sel = np.zeros((3 * (E + 1), NI * P), np.float32)
    for k in range(3):
        sel[k * (E + 1) + owner, unit] = 1.0
    return {
        "c_cos": np.cos(angle).astype(np.float32), "c_sin": np.sin(angle).astype(np.float32),
        "c_ident": np.eye(P, dtype=np.float32),
        "c_rowmask": np.stack([p % CT < SUB, p % CT >= SUB], 1).astype(np.float32), "c_pairmask": pair,
        "c_masks": np.stack([np.where(p[None, :] > p[:, None], NEG, 0.0),
                             np.where(p[:, None] > p[None, :], NEG, 0.0)], 1).astype(np.float32),
        "c_sel": sel,
        "c_key": np.tile(np.arange(E, 0, -1, dtype=np.float32), (P, 1)),
    }


_INS = ["L0_attn_x", "L0_attn_Wq", "L0_attn_Wk", "L0_attn_Wv", "L0_attn_Wo", "L0_attn_Wb", "L0_ffn_w_gate",
        "L0_ffn_w_up", "L0_ffn_w_down", "L0_ffn_sw_gate", "L0_ffn_sw_up", "L0_ffn_sw_down"]


def kernel(**inputs):
    import numpy as _np
    import concourse.bacc as _bacc
    from concourse import mybir as _mybir
    from concourse.bass_utils import run_bass_kernel_spmd as _run

    nc = _bacc.Bacc("TRN2", target_bir_lowering=False, num_devices=1)
    given = {f"in_{name}_dram": _np.ascontiguousarray(inputs[name]) for name in _INS}
    given["in_router_dram"] = _np.ascontiguousarray(_np.concatenate(
        [_np.asarray(inputs["L0_ffn_gate_w"]).T, _np.asarray(inputs["L0_ffn_shared_gate_w"])], axis=1))
    tables = constants()

    def tensor(name, a):
        return nc.dram_tensor(name, a.shape, _mybir.dt.from_np(a.dtype), kind="ExternalInput").ap()

    ins = [tensor(name, a) for name, a in given.items()]
    consts = [tensor(name, a) for name, a in tables.items()]
    out = nc.dram_tensor("out_0_dram", (NB, N, D), _mybir.dt.float32, kind="ExternalOutput").ap()
    layer(nc, ins, consts, out)
    r = _run(nc, [{**given, **tables}], core_ids=[0])
    return r.results[0]["out_0_dram"]
```

```python
from contextlib import ExitStack

import concourse.bass as bass
import numpy as np
from concourse import mybir
from concourse.alu_op_type import AluOpType as ALU

F32 = mybir.dt.float32
BF16 = mybir.dt.bfloat16
F32R = mybir.dt.float32r
ACT = mybir.ActivationFunctionType
AX = mybir.AxisListType.X

P = 128
NB, N, D, H, HD = 4, 1024, 256, 16, 16
CT = 32
NC = N // CT
SUB = 16
NQ = N // P
NG = H // 4
E, I, IS = 8, 176, 704
IT = E * I + IS
NI = -(-IT // P)
LAST = IT - P * (NI - 1)
GP = 4
TG = 512
NTG = NB * N // TG
TERMS = 6
QROWS = TERMS * HD
SROWS = QROWS + 3
NEG = -1.0e30
Q_PARTS = (0, 0, 1, 1, 2, 0)
K_PARTS = (0, 1, 0, 1, 0, 2)
PRODUCTS = ((0, 1), (1, 0), (0, 0))


class Memory:
    pass


def flat(ap):
    return ap.rearrange("p a b -> p (a b)")


def bc(ap, axis, n):
    shape = list(ap.shape)
    shape.insert(axis, n)
    return ap.unsqueeze(axis).broadcast_to(shape)


def is_first(i):
    return isinstance(i, int) and i == 0


def leads_in(seq):
    return isinstance(seq, int) and seq < 0


def hold(engine, semaphore, value, held):
    engine.wait_ge(semaphore, value)
    engine.sem_inc(held, 1)


def load_constants(nc, m):
    loads = [
        (m.cosq[:], m.c_cos), (m.sinq[:], m.c_sin), (m.ident[:], m.c_ident),
        (m.rowmask[:], m.c_rowmask), (m.pairmask[:], m.c_pairmask),
        (m.w_in[:, :, 0:D], m.Wq.rearrange("(k p) n -> p k n", p=P)),
        (m.w_in[:, :, D:2 * D], m.Wk.rearrange("(k p) n -> p k n", p=P)),
        (m.w_in[:, :, 2 * D:3 * D], m.Wv.rearrange("(k p) n -> p k n", p=P)),
        (m.w_in[:, :, 3 * D:3 * D + H], m.Wb.rearrange("(k p) n -> p k n", p=P)),
    ]
    with nc.Block() as block:

        @block.sync
        def _(sp):
            for k in range(4):
                for b in range(NB):
                    sp.dma_start(m.x[32 * b:32 * b + 32, 8 * k:8 * k + 8, :],
                                 m.x_in[b].rearrange("(c i) d -> i c d", i=CT)[:, 8 * k:8 * k + 8, :]) \
                        .then_inc(m.x_loaded[k], 16)

        @block.scalar
        def _(act):
            for dst, src in loads:
                act.dma_start(dst, src).then_inc(m.const_loaded, 16)
            act.wait_ge(m.ln_ready, NC + 2)
            nc.scalar.activation(m.rstd[:], m.rstd[:], ACT.Sqrt).then_inc(m.ln_sqrt, 1)

        @block.vector
        def _(dve):
            for semaphore, value in m.starts:
                dve.sem_inc(semaphore, value)

            def statistics(tiles):
                for c in tiles:
                    if c % 8 == 0:
                        dve.wait_ge(m.x_loaded[c // 8], 16 * NB)
                    nc.vector.bn_stats(m.stats[:, c, :], m.x[:, c, :]).then_inc(m.bn_done, 1)

            statistics(range(NC // 2))
            dve.wait_ge(m.const_loaded, 16 * len(loads))
            nc.vector.tensor_copy(m.ident16[:], m.ident[:])
            nc.vector.tensor_scalar(m.w_in[:, :, 0:D], m.w_in[:, :, 0:D], HD ** -0.5, None, ALU.mult) \
                .then_inc(m.w_split, 1)
            dve.wait_ge(m.w_split, 1)
            nc.vector.tensor_copy(m.w_parts[:, 0], m.w_in[:]).then_inc(m.w_split, 1)
            dve.wait_ge(m.w_split, 2)
            nc.vector.tensor_tensor(m.w_parts[:, 1], m.w_in[:], m.w_parts[:, 0].bitcast(F32), ALU.subtract)
            statistics(range(NC // 2, NC))
            for c in range(NC):
                dve.wait_ge(m.bn_done, c + 1)
                nc.vector.bn_aggr(m.mv[:, c, :], m.stats[:, c, :]).then_inc(m.ln_ready, 1)
            dve.wait_ge(m.ln_ready, NC)
            nc.vector.tensor_scalar(m.rstd[:], m.mv[:, :, 1], 1e-5, None, ALU.add).then_inc(m.ln_ready, 1)
            nc.vector.tensor_copy(m.mean[:], m.mv[:, :, 0]).then_inc(m.ln_ready, 1)
            dve.wait_ge(m.ln_sqrt, 1)
            nc.vector.reciprocal(m.rstd[:], m.rstd[:]).then_inc(m.ln_done, 1)


def projections(nc, m):
    bank = m.bank

    def everywhere(engine, start, iteration):
        start()
        with engine.Fori(0, NC // 2 - 2) as cc:
            for u in range(2):
                iteration(cc * 2 + u, u, 3)
        for c in range(NC - 4, NC):
            iteration(c, c % 2, NC - 1 - c)

    def nothing():
        pass

    with nc.Block() as block:

        @block.vector
        def _(dve):
            def normalise(c, u):
                if not isinstance(c, int) or c >= 2:
                    dve.wait_ge(m.p_xt, c - 1)
                nc.vector.tensor_scalar(
                    m.xn[:, u, :], m.x[:, bass.ds(c, 1), :].rearrange("p a d -> p (a d)"),
                    m.mean[:, bass.ds(c, 1)], m.rstd[:, bass.ds(c, 1)],
                    ALU.subtract, ALU.mult).then_inc(m.p_xn, 1)

            def rest(c, u):
                dve.wait_ge(m.p_high, c + 1)
                nc.vector.tensor_tensor(flat(m.xnt[:, u, 1]), bank(u)[:, 0:D],
                                        flat(m.xnt[:, u, 0]).bitcast(F32), ALU.subtract).then_inc(m.p_low, 1)

            def start():
                for c in range(3):
                    normalise(c, c % 2)
                rest(0, 0)

            def iteration(c, u, ahead):
                if ahead >= 3:
                    normalise(c + 3, 1 - u)
                if ahead >= 1:
                    rest(c + 1, 1 - u)
                dve.wait_ge(m.p_qk, c + 1)
                dve.wait_ge(m.p_rope, c + 1)
                qk = bank(2 + u)[:, 0:2 * D].rearrange("p (h w e) -> p h w e", h=2 * H, w=2)
                cos = bc(m.cosq[:, bass.ds(c, 1), :].rearrange("p a e -> p (a e)"), 1, 2 * H)
                sin = bc(m.sinq[:, bass.ds(c, 1), :].rearrange("p a e -> p (a e)"), 1, 2 * H)
                for w in range(2):
                    nc.vector.tensor_tensor(m.rc[:, u, :, w, :], qk[:, :, w, :], cos, ALU.mult) \
                        .then_inc(m.p_rot, 1)
                    nc.vector.tensor_tensor(m.rs[:, u, :, w, :], qk[:, :, 1 - w, :], sin, ALU.mult) \
                        .then_inc(m.p_rot, 1)

            everywhere(dve, start, iteration)

        @block.gpsimd
        def _(pool):
            def iteration(c, u, ahead):
                pool.wait_ge(m.p_rot, 4 * c + 9)
                for i in range(2):
                    out = (m.q[:, bass.ds(c, 1), :] if i == 0 else m.kv[:, bass.ds(c, 1), 0, :]) \
                        .rearrange("p a (h w e) -> p (a h) w e", h=H, w=2)
                    hs = slice(H * i, H * i + H)
                    for w, op in ((0, ALU.subtract), (1, ALU.add)):
                        last = nc.gpsimd.tensor_tensor(
                            out[:, :, w, :], m.rc[:, u, hs, w, :], m.rs[:, u, hs, w, :], op)
                last.then_inc(m.p_rope, 1)

            everywhere(pool, nothing, iteration)

        @block.tensor
        def _(pe):
            def turn(c, u):
                pe.wait_ge(m.p_xn, c + 1)
                for k in range(2):
                    last = nc.tensor.transpose(bank(u)[:, k * P:(k + 1) * P],
                                               m.xn[:, u, k * P:(k + 1) * P], m.ident[:])
                last.then_inc(m.p_xt, 1)

            def start():
                turn(0, 0)
                turn(1, 1)

            def iteration(c, u, ahead):
                pe.wait_ge(m.p_low, c + 1)
                pe.wait_ge(m.p_rot, 4 * c + 1)
                pe.wait_ge(m.p_v, c + 1)
                for out, columns in ((bank(2 + u), slice(0, 2 * D)), (bank(4 + u), slice(2 * D, 3 * D + H))):
                    for k in range(2):
                        for a, b in PRODUCTS:
                            last = nc.tensor.matmul(out[:, 0:columns.stop - columns.start], m.xnt[:, u, a, k, :],
                                                    m.w_parts[:, b, k, columns],
                                                    start=(k, a, b) == (0, 0, 1), stop=(k, a, b) == (1, 0, 0))
                last.then_inc(m.p_qk, 1)
                if ahead >= 2:
                    turn(c + 2, u)

            everywhere(pe, start, iteration)

        @block.scalar
        def _(act):
            def high(c, u):
                act.wait_ge(m.p_xt, c + 1)
                nc.scalar.copy(flat(m.xnt[:, u, 0]), bank(u)[:, 0:D]).then_inc(m.p_high, 1)

            def start():
                high(0, 0)
                high(1, 1)

            def iteration(c, u, ahead):
                act.wait_ge(m.p_qk, c + 1)
                nc.scalar.copy(m.kv[:, bass.ds(c, 1), 1, :].rearrange("p a d -> p (a d)"), bank(4 + u)[:, 0:D])
                nc.scalar.copy(m.beta[:, bass.ds(c, 1), :].rearrange("p a h -> p (a h)"),
                               bank(4 + u)[:, D:D + H]).then_inc(m.p_v, 1)
                if ahead >= 2:
                    high(c + 2, u)

            everywhere(act, start, iteration)


def normalise_keys(nc, m):
    k_all = m.kv[:, :, 0, :].rearrange("p c (h e) -> p c h e", h=H)
    with nc.Block() as block:

        @block.vector
        def _(dve):
            sq = m.sq[:].rearrange("p c (h e) -> p c h e", h=H)
            for j in range(4):
                cs = slice(8 * j, 8 * j + 8)
                dve.wait_ge(m.k_sq, j + 1)
                nc.vector.tensor_reduce(m.rn[:, cs, :], sq[:, cs], AX, ALU.add).then_inc(m.k_ss, 1)
            dve.wait_ge(m.k_ss, 4)
            nc.vector.tensor_scalar(m.rn[:], m.rn[:], 1e-6, None, ALU.add).then_inc(m.k_ss, 1)
            dve.wait_ge(m.k_sqrt, 1)
            nc.vector.reciprocal(m.rn[:], m.rn[:]).then_inc(m.k_ss, 1)
            dve.wait_ge(m.k_sqrt, 2)
            nc.vector.tensor_scalar(m.beta[:], m.beta[:], 1.0, None, ALU.add).then_inc(m.k_beta, 1)
            dve.wait_ge(m.k_beta, 1)
            nc.vector.reciprocal(m.beta[:], m.beta[:]).then_inc(m.k_beta, 1)
            dve.wait_ge(m.k_beta, 2)
            nc.vector.tensor_scalar(m.beta[:], m.beta[:], 2.0, None, ALU.mult).then_inc(m.k_beta, 1)
            dve.wait_ge(m.k_ss, 6)
            for j in range(4):
                cs = slice(8 * j, 8 * j + 8)
                for c in range(8 * j, 8 * j + 8):
                    last = nc.vector.tensor_tensor(k_all[:, c], k_all[:, c], bc(m.rn[:, c, :], 2, HD), ALU.mult)
                last.then_inc(m.k_norm, 1)
            dve.wait_ge(m.k_stored, 16)
            dve.wait_ge(m.k_norm, 4)
            dve.wait_ge(m.k_beta, 3)
            for c in range(24, NC):
                last = nc.vector.tensor_tensor(
                    m.q[:, c, :].rearrange("p (h e) -> p h e", h=H), k_all[:, c],
                    bc(m.beta[:, c, :], 2, HD), ALU.mult)
            last.then_inc(m.k_kb_last, 1)
            for s in range(2):
                nc.vector.tensor_scalar(m.beta_half[:, s, :], m.beta[:].rearrange("p c h -> p (c h)"),
                                        m.rowmask[:, s:s + 1], None, ALU.mult).then_inc(m.k_beta, 1)
            nc.vector.transpose(m.beta_lane[:], m.beta[:].rearrange("p c h -> p (c h)")).then_inc(m.k_lane, 1)
            dve.wait_ge(m.k_lane, 1)
            nc.vector.tensor_scalar(m.beta_lane[:], m.beta_lane[:], -1.0, None, ALU.mult).then_inc(m.k_lane, 1)

        @block.scalar
        def _(act):
            for j in range(4):
                cs = slice(8 * j, 8 * j + 8)
                nc.scalar.activation(m.sq[:, cs, :], m.kv[:, cs, 0, :], ACT.Square).then_inc(m.k_sq, 1)
            act.wait_ge(m.k_ss, 5)
            nc.scalar.activation(m.rn[:], m.rn[:], ACT.Sqrt).then_inc(m.k_sqrt, 1)
            nc.scalar.activation(m.beta[:], m.beta[:], ACT.Exp, scale=-1.0).then_inc(m.k_sqrt, 1)

        @block.gpsimd
        def _(pool):
            pool.wait_ge(m.k_stored, 16)
            pool.wait_ge(m.k_beta, 3)
            for j in range(3):
                pool.wait_ge(m.k_norm, j + 1)
                for c in range(8 * j, 8 * j + 8):
                    last = nc.gpsimd.tensor_tensor(
                        m.q[:, c, :].rearrange("p (h e) -> p h e", h=H), k_all[:, c],
                        bc(m.beta[:, c, :], 2, HD), ALU.mult)
                last.then_inc(m.k_kb, 1)

        @block.sync
        def _(sp):
            sp.dma_start(m.q_dram, m.q[:]).then_inc(m.k_stored, 16)
            for j in range(4):
                if j < 3:
                    sp.wait_ge(m.k_kb, j + 1)
                else:
                    sp.wait_ge(m.k_kb_last, 1)
                sp.dma_start(m.kb_dram[:, 8 * j:8 * j + 8, :], m.q[:, 8 * j:8 * j + 8, :]) \
                    .then_inc(m.k_kb_stored, 16)


PT = 2 * GP
KEYS_BANK = 4
ROW_STEPS = 4
WHOLE_ROWS = 10
SLOTS = GP + WHOLE_ROWS + 2 * (SUB - 1 - WHOLE_ROWS) + 2


def delta_rule(nc, m):
    bank = m.bank

    def everywhere(engine, iteration, prelude):
        prelude()
        with engine.Fori(0, NC // PT - 2) as p:
            iteration(p, True, True)
        iteration(NC // PT - 2, True, False)
        iteration(NC // PT - 1, False, False)

    with nc.Block() as block:

        @block.gpsimd
        def _(pool):
            def keys(c, u):
                hold(pool, m.g_kt, c + 1, m.held_pool)
                nc.gpsimd.tensor_copy(m.kc[:, u], m.kv[:, bass.ds(c, 1), 0, :].rearrange("p a d -> p (a d)")) \
                    .then_inc(m.g_kc, 1)

            def steps(p, i, gram, more):
                c = p * PT + i
                for s in range(2):
                    pool.wait_ge(m.r_ds, 2 * c + s + 1)
                    nc.gpsimd.tensor_tensor(
                        m.kb[:, s].rearrange("p (h e) -> p h e", h=H),
                        m.kv[:, bass.ds(c, 1), 0, :].rearrange("p a (h e) -> p (a h) e", h=H),
                        bc(m.beta_half[:, s, bass.ds(c * H, H)], 2, HD), ALU.mult).then_inc(m.r_kb, 1)
                if gram:
                    keys(c + 2 * PT, i % 2)
                if more:
                    hold(pool, m.r_wu_mm, c + 1, m.held_pool)
                    fetch(p, i + 2)
                for s in range(2):
                    hold(pool, m.r_vn, 2 * c + s + 1, m.held_pool)
                    if s == 0:
                        hold(pool, m.r_v, c + 1, m.held_pool)
                    nc.gpsimd.tensor_tensor(m.vt[:, s], m.vn[:, s], m.rowmask[:, s:s + 1].broadcast_to([P, D]),
                                            ALU.mult).then_inc(m.r_vo, 1)
                hold(pool, m.r_vo, 2 * c + 4, m.held_pool)
                nc.gpsimd.tensor_tensor(m.v[:, bass.ds(c, 1), :].rearrange("p a d -> p (a d)"), m.vt[:, 0],
                                        m.vt[:, 1], ALU.add).then_inc(m.r_v, 1)

            def fetch(p, i):
                c, u, g = p * PT + i, i % 2, i % PT // 2
                hold(pool, m.x_back, p * GP + i // 2 + 1, m.held_pool)
                x_t = m.xb[:, g].rearrange("p (i u h) -> p u h i", i=32, u=2)
                nc.gpsimd.tensor_copy(m.xc[:, u], x_t[:, u]).then_inc(m.r_xc, 1)
                nc.gpsimd.tensor_copy(m.kvc[:, u], m.kv[:, bass.ds(c, 1), :, :]
                                      .rearrange("p a w d -> p (a w) d")).then_inc(m.r_xc, 1)

            def iteration(p, solve, gram):
                for i in range(PT):
                    steps(p, i, gram, solve or i < PT - 2)

            def prelude():
                for c in range(2 * PT):
                    keys(c, c % 2)
                pool.wait_ge(m.k_kb_stored, 64)
                fetch(0, 0)
                fetch(0, 1)

            everywhere(pool, iteration, prelude)

        @block.tensor
        def _(pe):
            def turn_keys(c, u, to):
                pe.wait_ge(m.g_kc, c + 1)
                pe.wait_ge(m.g_kt1, c + 1)
                for k in range(2):
                    last = nc.tensor.transpose(bank(to)[:, k * P:(k + 1) * P], m.kc[:, u, k * P:(k + 1) * P],
                                               m.ident[:])
                last.then_inc(m.g_kt, 1)

            def gram_matrices(c, u):
                hold(pe, m.g_kt2, 2 * c + 2, m.held)
                hold(pe, m.g_out, 2 * c + 1, m.held)
                for k in range(2):
                    for shift in range(4):
                        for j in range(4):
                            b = (j + shift) % NB
                            r = slice(32 * j, 32 * j + 32)
                            out = bank(j)[32 * b:32 * b + 32, 64 * k:64 * k + 64] \
                                .rearrange("p (s t) -> p s t", s=2)
                            last = nc.tensor.matmul(out, m.kt1[r, u, k, 32 * b:32 * b + 32],
                                                    m.kt2[r, u, :, k, 32 * b:32 * b + 32], start=True, stop=True)
                last.then_inc(m.g_mm, 1)

            def heads_wu(u, hs):
                for h in hs:
                    for b in range(NB):
                        r = slice(32 * b, 32 * b + 32)
                        last = nc.tensor.matmul(bank(b)[r, 32 * h:32 * h + 32].rearrange("p (w e) -> p w e", w=2),
                                                m.xc[r, u, h, :], m.kvc[r, u, :, HD * h:HD * h + HD],
                                                start=True, stop=True)
                return last

            def transpose_w(c, u):
                pe.wait_ge(m.r_wu, 4 * c + 4)
                for k in range(2):
                    last = nc.tensor.transpose(bank(0)[:, k * P:(k + 1) * P], m.wu[:, u, 0, k * P:(k + 1) * P],
                                               m.ident[:])
                last.then_inc(m.r_wt_mm, 1)

            def steps(p, i, gram, more):
                c, u = p * PT + i, i % 2
                hold(pe, m.r_wt, c + 1, m.held)
                for s in range(2):
                    hold(pe, m.r_s, 2 * c + s + 1, m.held)
                    for k in range(2):
                        for shift in range(4):
                            for j in range(4):
                                b = (j + shift) % NB
                                r = slice(32 * j, 32 * j + 32)
                                last = nc.tensor.matmul(bank(4 + j)[32 * b:32 * b + 32, 32 * k:32 * k + 32],
                                                        m.wt[r, u, k, 32 * b:32 * b + 32], m.s[r, b, k, :],
                                                        start=True, stop=True)
                    last.then_inc(m.r_ws, 1)
                    if s == 0:
                        if more >= 1:
                            transpose_w(c + 1, 1 - u)
                        if gram:
                            turn_keys(c + 2 * PT, u, 1)
                    elif more == 2:
                        hold(pe, m.r_wt, c + 2, m.held)
                        if gram:
                            hold(pe, m.g_out, 2 * (c + 2 * PT) + 3, m.held)
                        hold(pe, m.r_xc, 2 * c + 6, m.held)
                        heads_wu(u, range(H // 2))
                    pe.wait_ge(m.r_vn, 2 * c + s + 1)
                    hold(pe, m.r_kb, 2 * c + s + 1, m.held)
                    for k in range(2):
                        for shift in range(4):
                            for b in range(NB):
                                j = (b + shift) % 4
                                r = slice(32 * b, 32 * b + 32)
                                f = slice(k * P + 32 * j, k * P + 32 * j + 32)
                                last = nc.tensor.matmul(bank(4 + b)[32 * j:32 * j + 32, 64 + 32 * k:96 + 32 * k],
                                                        m.kb[r, s, f], m.vn[r, s, f], start=True, stop=True)
                    last.then_inc(m.r_ds, 1)
                    if s == 0:
                        if gram:
                            hold(pe, m.r_wt, c + 2, m.held)
                            gram_matrices(c + 2 * PT, u)
                    elif more == 2:
                        heads_wu(u, range(H // 2, H)).then_inc(m.r_wu_mm, 1)

            def iteration(p, solve, gram):
                for i in range(PT):
                    steps(p, i, gram, 2 if solve else min(2, PT - 1 - i))

            def prelude():
                turn_keys(0, 0, KEYS_BANK)
                for c in range(2 * PT):
                    if c + 1 < 2 * PT:
                        turn_keys(c + 1, (c + 1) % 2, KEYS_BANK)
                    gram_matrices(c, c % 2)
                pe.wait_ge(m.g_out, 4 * PT + 1)
                pe.wait_ge(m.r_xc, 2)
                heads_wu(0, range(H)).then_inc(m.r_wu_mm, 1)
                transpose_w(0, 0)
                pe.wait_ge(m.r_xc, 4)
                pe.wait_ge(m.r_wt, 1)
                heads_wu(1, range(H)).then_inc(m.r_wu_mm, 1)

            everywhere(pe, iteration, prelude)

        @block.scalar
        def _(act):
            def keys(c, u, at):
                act.wait_ge(m.g_kt, c + 3)
                act.wait_ge(m.g_mm, c + 1)
                nc.scalar.copy(flat(m.kt1[:, u]), bank(at)[:, 0:D]).then_inc(m.g_kt1, 1)
                act.wait_ge(m.g_kt1, c + 2)
                for s in range(2):
                    nc.scalar.activation(flat(m.kt2[:, u, s]), flat(m.kt1[:, u]), ACT.Copy,
                                         scale=m.pairmask[:, 32 + s:33 + s]).then_inc(m.g_kt2, 1)

            def gram_out(p, i):
                act.wait_ge(m.g_mm, p * PT + i + 3)
                if i % 2 == 0 and not is_first(p):
                    act.wait_ge(m.g_tr, (p - 1) * GP + i // 2 + 1)
                for k in range(2):
                    src = m.psum[:, 0:4, 64 * k:64 * k + 64].rearrange("p j (s t) -> p j s t", s=2)
                    dst = m.gs[:, i // 2].rearrange("p (t u k j s) -> p u k j s t", t=32, u=2, k=2, j=4)
                    dst = dst[:, i % 2, k]
                    nc.scalar.copy(dst, src).then_inc(m.g_out, 1)

            def w_and_u(c, u):
                act.wait_ge(m.r_wu_mm, c + 1)
                for b in range(NB):
                    r = slice(32 * b, 32 * b + 32)
                    nc.scalar.copy(m.wu[r, u].rearrange("p w (h e) -> p w h e", h=H),
                                   bank(b)[r, :].rearrange("p (h w e) -> p w h e", h=H, w=2)).then_inc(m.r_wu, 1)

            def w_turned(c, u):
                act.wait_ge(m.r_wt_mm, c + 1)
                nc.scalar.copy(flat(m.wt[:, u]), bank(0)[:, 0:D]).then_inc(m.r_wt, 1)

            def iteration(p, solve, gram):
                for i in range(PT):
                    c = p * PT + i
                    if solve or i < PT - 1:
                        w_turned(c + 1, 1 - i % 2)
                    if gram:
                        keys(c + 2 * PT, i % 2, 1)
                        gram_out(p + 2, i)
                    if solve or i < PT - 2:
                        w_and_u(c + 2, i % 2)

            def prelude():
                keys(0, 0, KEYS_BANK)
                for c in range(2 * PT):
                    if c + 1 < 2 * PT:
                        keys(c + 1, (c + 1) % 2, KEYS_BANK)
                    gram_out(c // PT, c % PT)
                w_and_u(0, 0)
                w_turned(0, 0)
                w_and_u(1, 1)

            everywhere(act, iteration, prelude)

        @block.vector
        def _(dve):
            xl = m.xl[:].rearrange("p g (i k) -> p g i k", i=32)
            gram_t = m.gram[:].rearrange("p (j i) -> p i j", j=32)

            def systems(p, g):
                pair = p * GP + g
                dve.wait_ge(m.g_out, 4 * pair + 5)
                dve.wait_ge(m.g_an, 2 * pair + 1)
                nc.vector.transpose(m.gram[:], m.gs[:, g]).then_inc(m.g_tr, 1)
                dve.wait_ge(m.g_tr, pair + 1)
                beta = m.beta_lane[:, bass.ds(pair, 1), :].rearrange("p a j -> p (a j)")
                for s in range(2):
                    r = slice(SUB * s, SUB * s + SUB)
                    nc.vector.tensor_tensor(m.an[:, s, g], gram_t[:, r, r], bc(beta[:, r], 1, SUB),
                                            ALU.mult).then_inc(m.g_an, 1)

            def products(p, i):
                done = p * (ROW_STEPS * (SUB - 1)) + ROW_STEPS * (i - 1)
                if i == 1:
                    dve.wait_ge(m.g_an, (p + 1) * (2 * GP) + 1)
                for s in range(2):
                    if i > 1:
                        dve.wait_ge(m.solve, done - 1 + s)
                    r = slice(SUB * s, SUB * s + i)
                    nc.vector.tensor_tensor(m.prod[:, s, :, 0:i, 0:i], bc(m.an[:, s, :, i, 0:i], 2, i),
                                            xl[:, :, r, r].rearrange("p g j k -> p g k j"),
                                            ALU.mult).then_inc(m.solve, 1)

            def sums(p, i):
                done = p * (ROW_STEPS * (SUB - 1)) + ROW_STEPS * (i - 1)
                for s in range(2):
                    dve.wait_ge(m.solve, done + 1 + s)
                    nc.vector.tensor_reduce(xl[:, :, SUB * s + i, SUB * s:SUB * s + i],
                                            m.prod[:, s, :, 0:i, 0:i], AX, ALU.add).then_inc(m.solve, 1)

            def back(p, half):
                if half == 0:
                    dve.wait_ge(m.solve, (p + 1) * (ROW_STEPS * (SUB - 1)))
                    if not is_first(p):
                        dve.wait_ge(m.r_xc, p * (2 * PT))
                for g in range(half * GP // 2, (half + 1) * GP // 2):
                    nc.vector.transpose(m.xb[:, g, :], m.xl[:, g, :]).then_inc(m.x_back, 1)
                if half == 1:
                    dve.wait_ge(m.x_back, (p + 1) * GP)

            def solve_slot(p, n):
                if n < GP:
                    systems(p, n)
                elif n < GP + WHOLE_ROWS:
                    products(p, n - GP + 1)
                    sums(p, n - GP + 1)
                elif n < SLOTS - 2:
                    i, part = divmod(n - GP - WHOLE_ROWS, 2)
                    (products, sums)[part](p, WHOLE_ROWS + 1 + i)
                elif n < SLOTS:
                    back(p, n - (SLOTS - 2))

            def prelude():
                for n in range(SLOTS):
                    solve_slot(0, n)

            def iteration(p, solve, gram):
                for i in range(PT):
                    c, u = p * PT + i, i % 2
                    dve.wait_ge(m.r_wu, 4 * c + 4)
                    for s in range(2):
                        dve.wait_ge(m.r_ws, 2 * c + s + 1)
                        dve.wait_ge(m.r_vo, 2 * c + s + 1)
                        split = "p (k j e) -> p k j e"
                        nc.vector.tensor_tensor(
                            m.vn[:, s].rearrange(split, k=2, j=4), m.wu[:, u, 1].rearrange(split, k=2, j=4),
                            m.psum[:, 4:8, 0:64].rearrange("p j (k e) -> p k j e", k=2),
                            ALU.subtract).then_inc(m.r_vn, 1)
                        if solve:
                            solve_slot(p + 1, 4 * i + 2 * s)
                        dve.wait_ge(m.r_ds, 2 * c + s + 3)
                        nc.vector.tensor_tensor(
                            m.ds[:], m.psum[:, 4:8, 64:128].rearrange("p b (k e) -> p b k e", k=2),
                            bc(bc(m.pairmask[:, 0:32], 1, 2), 1, NB), ALU.mult).then_inc(m.r_dsm, 1)
                        dve.wait_ge(m.r_dsm, 2 * c + s + 1)
                        nc.vector.tensor_tensor(m.s[:], m.s[:], m.ds[:], ALU.add).then_inc(m.r_s, 1)
                        if solve:
                            solve_slot(p + 1, 4 * i + 2 * s + 1)

            nc.vector.memset(m.xl[:], 0.0).then_inc(m.x_clear, 1)
            dve.wait_ge(m.x_clear, 1)
            nc.vector.memset(m.xl[:, :, 0:1024:33], 1.0).then_inc(m.x_clear, 1)
            nc.vector.memset(m.s[:], 0.0).then_inc(m.r_s, 1)
            dve.wait_ge(m.x_clear, 2)
            everywhere(dve, iteration, prelude)

        @block.sync
        def _(sp):
            for p in range(NC // PT):
                sp.wait_ge(m.r_v, PT * (p + 1) + 1)
                sp.dma_start(m.v_dram[:, PT * p:PT * p + PT, :], m.v[:, PT * p:PT * p + PT, :]) \
                    .then_inc(m.r_stored, 16)
            sp.wait_ge(m.r_stored, 16 * (NC // PT))


def split_and_stack(engine, held, stack, x, rest, parts, done, base):
    term = [[t for t in range(TERMS) if parts[t] == k] for k in range(3)]
    n = 0
    for k in range(3):
        out = stack[:, :, :, term[k][0], :]
        source = x if k == 0 else rest
        if n:
            hold(engine, done, base + n, held)
        engine.tensor_copy(out, source).then_inc(done, 1)
        n += 1
        hold(engine, done, base + n, held)
        if k < 2:
            engine.tensor_tensor(rest, source, out, ALU.subtract).then_inc(done, 1)
            n += 1
        for t in term[k][1:]:
            engine.tensor_copy(stack[:, :, :, t, :], out).then_inc(done, 1)
            n += 1
    return n


STACK_STEPS = 3 + 2 + 3
ACT_FILLS, DVE_FILLS = 2, 6
FILLS = 8
MAX_TILES = [(j, t) for i in range(NQ // 2) for j in range(4) for t in (NQ - 1 - i, i)]
PIECES = [(j, t, a, min(a + 512, P * t + P)) for j, t in MAX_TILES for a in range(0, P * t + P, 512)]
NP = len(PIECES)
STEPS = 4 * NQ
MAX_STEPS = STEPS - 8
PARTS_STEP = MAX_STEPS + 2
FILL_STEPS = [MAX_STEPS, MAX_STEPS + 1] + [PARTS_STEP + 1 + i for i in range(FILLS - 2)]
FILL_BANKS = (6, 7, 7, 6, 7, 6, 7, 6)
MAX_OPS = 6


def attention(nc, m):
    bank, bank16 = m.bank, m.bank16

    def everywhere(engine, iteration):
        iteration(-1, NG - 2, False, True)
        iteration(-1, NG - 1, True, True)
        with engine.Fori(0, NB - 1) as seq:
            for g in range(NG):
                iteration(seq, g, True, True)
        for g in range(NG):
            iteration(NB - 1, g, g < NG - 1, g < NG - 2)

    def copy_operand(copy, g, n):
        h = 4 * ((g + 2) % NG)
        operand = (m.qs, m.ks)[n // 4]
        return copy(operand[0:QROWS, h:h + 4, 2 * P * (n % 4):2 * P * (n % 4) + 2 * P],
                    bank16(FILL_BANKS[n])[0:QROWS, :].rearrange("p (h t) -> p h t", h=4))

    def scores(n):
        return flat(m.psum[:, 2 * (n % 2):2 * (n % 2) + 2, :])

    sums = flat(m.psum[:, 4:6, :])

    with nc.Block() as block:

        @block.sync
        def _(sp):
            def load(buffers, seq):
                for i in buffers:
                    dst, src = ((m.kn, m.kb_dram), (m.qn, m.q_dram), (m.vn2, m.v_dram))[i]
                    for cc in range(4):
                        rows = src.rearrange("(b i) (t c) d -> c b i t d", b=NB, c=4)[cc, bass.ds(seq, 1)]
                        sp.dma_start(dst[32 * cc:32 * cc + 32], rows.rearrange("b i t d -> (b i) t d")) \
                            .then_inc(m.a_loaded[i], 16)

            def iteration(seq, g, maxima, operands):
                unit = seq * NG + g
                if g == NG - 2 and operands and not isinstance(seq, int):
                    sp.wait_ge(m.a_q, (unit + 2) * STACK_STEPS)
                    sp.wait_ge(m.a_k, (unit + 2) * STACK_STEPS)
                    load((1, 0), seq + 1)
                    sp.wait_ge(m.v_vg, unit + 2)
                    load((2,), seq + 1)
                if g == 0:
                    sp.dma_start(m.xres[:], m.x_seq[:, bass.ds(seq * NQ, NQ), :]).then_inc(m.o_x, 16)
                if maxima:
                    sp.wait_ge(m.m_rows, unit + 2)
                    sp.dma_start(m.max_dram, m.mrows[:]).then_inc(m.m_out, 16)
                    sp.wait_ge(m.m_out, unit * 16 + 32)
                    h = 4 * ((g + 1) % NG)
                    sp.dma_start(m.qs[QROWS:SROWS, h:h + 4, :], m.max_dram.rearrange("(r h) t -> r h t", r=3)) \
                        .then_inc(m.m_in, 16)
                    hold(sp, m.m_in, unit * 16 + 32, m.held_sp)
                if g == NG - 1 and not leads_in(seq):
                    for t in range(NQ):
                        sp.wait_ge(m.o_x1, seq * NQ + t + 2)
                        sp.dma_start(m.x1_dram[:, bass.ds(seq * NQ + t, 1), :], m.xres[:, t:t + 1, :]) \
                            .then_inc(m.o_st, 16)
                    hold(sp, m.o_st, seq * (16 * NQ) + 16 * NQ, m.held_sp)
                    hold(sp, m.o_bn, seq * NQ + NQ, m.held_sp)

            load((0, 1, 2), 0)
            sp.dma_start(m.wo[:], m.wo_dram).then_inc(m.a_const, 16)
            sp.dma_start(m.masks[:], m.c_masks).then_inc(m.a_const, 16)
            everywhere(sp, iteration)

        @block.gpsimd
        def _(pool):
            def iteration(seq, g, maxima, operands):
                unit = seq * NG + g
                if maxima:
                    if g == NG - 1:
                        hold(pool, m.a_loaded[2], seq * 64 + 128, m.held_pool)
                    if not leads_in(seq):
                        hold(pool, m.v_o, unit * NQ + 2, m.held_pool)
                    h = 4 * ((g + 1) % NG)
                    nc.gpsimd.tensor_copy(
                        m.vg[:, (g + 1) % 2, :, :, 0:HD],
                        m.vn2[:, :, HD * h:HD * h + 64].rearrange("p t (j e) -> p t j e", j=4)).then_inc(m.v_vg, 1)
                if operands:
                    if not leads_in(seq):
                        hold(pool, m.a_t, unit * FILLS + FILLS, m.held_pool)
                    h = 4 * ((g + 2) % NG)
                    for i, stage, source, parts, done in ((1, m.stage_q, m.qn, Q_PARTS, m.a_q),
                                                          (0, m.stage_k, m.kn, K_PARTS, m.a_k)):
                        if i == 0 and leads_in(seq):
                            continue
                        if g == NG - 2 or (i == 0 and g == 0):
                            hold(pool, m.a_loaded[i], seq * 64 + (128 if g == NG - 2 else 64), m.held_pool)
                        split_and_stack(nc.gpsimd, m.held_pool, stage[:, g % 2],
                                        source[:, :, HD * h:HD * h + 64].rearrange("p t (j e) -> p t j e", j=4),
                                        m.rest[:], parts, done, (unit + 2) * STACK_STEPS)

            nc.gpsimd.memset(m.vg[:], 0.0).then_inc(m.a_vg, 1)
            pool.wait_ge(m.a_vg, 1)
            nc.gpsimd.memset(m.vg[:, :, :, :, HD:HD + 1], 1.0).then_inc(m.a_vg, 1)
            everywhere(pool, iteration)

        @block.tensor
        def _(pe):
            def iteration(seq, g, maxima, operands):
                unit = seq * NG + g
                now, after, later = 4 * g, 4 * ((g + 1) % NG), 4 * ((g + 2) % NG)
                first = leads_in(seq)

                def score(kt, j):
                    pe.wait_ge(m.v_exp, unit * STEPS + 4 * kt + j + 1)
                    if kt == 0 and j == 0:
                        pe.wait_ge(m.m_in, unit * 16 + 16)
                        pe.wait_ge(m.a_ones, 2)
                    out = scores(j)
                    k = m.ks[0:SROWS, now + j, P * kt:P * kt + P]
                    cuts = [P * kt, 512, N] if kt < 4 else [P * kt, N]
                    for a, z in zip(cuts, cuts[1:]):
                        last = nc.tensor.matmul(out[:, a:z], k, m.qs[0:SROWS, now + j, a:z],
                                                start=True, stop=a != P * kt)
                        if a == P * kt:
                            last = nc.tensor.matmul(out[:, a:a + P], m.ident16[:], m.mask_kq[:],
                                                    start=False, stop=True)
                    last.then_inc(m.v_s, 1)

                def values(kt, i):
                    piece, pair = divmod(i, 2)
                    a, z = max(512 * piece, P * kt), 512 * piece + 512
                    if a >= z:
                        return
                    if i == 0 or (a == P * kt and pair == 0):
                        pe.wait_ge(m.v_exp, unit * STEPS + 4 * kt + 6)
                    if kt == 0 and i == 0:
                        pe.wait_ge(m.v_read, unit + 1)
                        pe.wait_ge(m.v_vg, unit + 1)
                        if g == 0:
                            pe.wait_ge(m.o_x1, seq * NQ + 1)
                    for j in (2 * pair, 2 * pair + 1):
                        last = nc.tensor.matmul(sums[32 * j:32 * j + 32, a:z], m.vg[:, g % 2, kt, j, :],
                                                m.p[:, 4 * (kt % 2) + j, a:z], start=kt == 0,
                                                stop=kt == 4 * piece + 3)
                    if i == 3:
                        last.then_inc(m.v_o, 1)

                def maximum(i):
                    j, t, a, z = PIECES[i]
                    if i == 0:
                        pe.wait_ge(m.a_fd, (unit + 2) * DVE_FILLS)
                    elif i > 1:
                        pe.wait_ge(m.m_max, (unit + 1) * NP + i - 1)
                    out = bank(6 + i % 2)[:, 0:z - a]
                    diagonal = z == P * t + P
                    last = nc.tensor.matmul(out, m.qs[0:QROWS, after + j, P * t:P * t + P],
                                            m.ks[0:QROWS, after + j, a:z], start=True, stop=not diagonal)
                    if diagonal:
                        last = nc.tensor.matmul(out[:, z - a - P:z - a], m.ident16[:], m.mask_qk[:],
                                                start=False, stop=True)
                    last.then_inc(m.m_s, 1)

                def maxima_parts():
                    pe.wait_ge(m.m_part, (unit + 2) * MAX_OPS)
                    if operands:
                        pe.wait_ge(m.a_fa, (unit + 2) * ACT_FILLS + 1)
                    for t in range(NQ):
                        last = nc.tensor.transpose(bank16(6)[0:12, P * t:P * t + P],
                                                   m.mparts[:, t].rearrange("p r h -> p (r h)"), m.ident16[:])
                    last.then_inc(m.m_t, 1)

                def fill(n):
                    staged, stage = ((m.a_q, m.stage_q), (m.a_k, m.stage_k))[n // 4]
                    if n % 4 == 0:
                        pe.wait_ge(staged, (unit + 3) * STACK_STEPS)
                    if n < 2:
                        if maxima:
                            pe.wait_ge(m.m_max, (unit + 1) * NP + NP - 1 + n)
                    elif n == 2:
                        pe.wait_ge(m.a_fa, (unit + 2) * ACT_FILLS + 2)
                    elif n == 3 and maxima:
                        pe.wait_ge(m.m_rows, unit + 2)
                    elif n == 3:
                        pe.wait_ge(m.a_fa, (unit + 2) * ACT_FILLS + 1)
                    else:
                        pe.wait_ge(m.a_fd, (unit + 2) * DVE_FILLS + n - 3)
                    for j in range(4):
                        for i in range(2):
                            last = nc.tensor.transpose(
                                bank16(FILL_BANKS[n])[0:QROWS, P * (2 * j + i):P * (2 * j + i + 1)],
                                stage[:, g % 2, 2 * (n % 4) + i, j].rearrange("p r e -> p (r e)"), m.ident16[:])
                    last.then_inc(m.a_t, 1)

                for kt in range(NQ + 1):
                    for j in range(4):
                        step = 4 * kt + j
                        if kt < NQ and not first:
                            score(kt, j)
                        if maxima and step < MAX_STEPS:
                            maximum(2 * step)
                        if maxima and step == PARTS_STEP:
                            maxima_parts()
                        if operands and step in FILL_STEPS:
                            fill(FILL_STEPS.index(step))
                        if kt > 0 and not first:
                            values(kt - 1, j)
                        if maxima and step < MAX_STEPS:
                            maximum(2 * step + 1)
                if g == NG - 1 and not first:
                    output(seq)

            def output(seq):
                def turn(t):
                    if t >= 2:
                        pe.wait_ge(m.o_n, seq * (2 * NQ) + 2 * t - 2)
                    for g in range(NG):
                        last = nc.tensor.transpose(bank(t % 2)[:, P * g:P * g + P], m.ot[:, g, P * t:P * t + P],
                                                   m.ident[:])
                    last.then_inc(m.o_t, 1)

                pe.wait_ge(m.v_read, seq * NG + NG + 1)
                turn(0)
                for t in range(NQ):
                    if t + 1 < NQ:
                        turn(t + 1)
                    pe.wait_ge(m.o_n, seq * (2 * NQ) + 2 * t + 2)
                    if t >= 2:
                        pe.wait_ge(m.o_te, seq * NQ + t - 1)
                    for k in range(2):
                        last = nc.tensor.transpose(bank(2 + t % 2)[:, P * k:P * k + P],
                                                   m.on[:, t % 2, P * k:P * k + P], m.ident[:])
                    last.then_inc(m.o_tt, 1)
                    pe.wait_ge(m.o_te, seq * NQ + t + 1)
                    if t >= 2:
                        pe.wait_ge(m.o_x1, seq * NQ + t)
                    for k in range(2):
                        last = nc.tensor.matmul(bank(4 + t % 2)[:, 0:D], m.ont[:, t % 2, k, :], m.wo[:, k, :],
                                                start=k == 0, stop=k == 1)
                    last.then_inc(m.o_mm, 1)

            pe.wait_ge(m.a_masks, 2)
            pe.wait_ge(m.a_vg, 2)
            everywhere(pe, iteration)

        @block.scalar
        def _(act):
            def iteration(seq, g, maxima, operands):
                unit = seq * NG + g
                first = leads_in(seq)
                for step in range(STEPS):
                    kt, j = divmod(step, 4)
                    if not first:
                        act.wait_ge(m.v_s, unit * STEPS + step + 1)
                        if j == 0:
                            act.wait_ge(m.v_o, unit * NQ + kt + 1)
                        nc.scalar.activation(m.p[:, 4 * (kt % 2) + j, P * kt:N], scores(j)[:, P * kt:N],
                                             ACT.Exp).then_inc(m.v_exp, 1)
                    if operands and step in FILL_STEPS[:ACT_FILLS]:
                        n = FILL_STEPS.index(step)
                        act.wait_ge(m.a_t, (unit + 2) * FILLS + n + 1)
                        copy_operand(nc.scalar.copy, g, n).then_inc(m.a_fa, 1)
                if g == NG - 1 and not first:
                    for t in range(NQ):
                        act.wait_ge(m.o_tt, seq * NQ + t + 1)
                        if t >= 2:
                            act.wait_ge(m.o_mm, seq * NQ + t - 1)
                        nc.scalar.copy(flat(m.ont[:, t % 2]), bank(2 + t % 2)[:, 0:D]).then_inc(m.o_te, 1)

            act.wait_ge(m.a_ones, 1)
            nc.scalar.copy(m.ks[QROWS:SROWS, H // 2:H], m.ks[QROWS:SROWS, 0:H // 2]).then_inc(m.a_ones, 1)
            everywhere(act, iteration)

        @block.vector
        def _(dve):
            def maxima_of(unit):
                for i, (j, t, a, z) in enumerate(PIECES):
                    dve.wait_ge(m.m_s, unit * NP + i + 1)
                    nc.vector.tensor_reduce(m.nmax[:, a // 512, t, j:j + 1], bank(6 + i % 2)[:, 0:z - a], AX,
                                            ALU.max, negate=True).then_inc(m.m_max, 1)
                dve.wait_ge(m.m_max, unit * NP + NP)
                nm = m.nmax[:, 0]
                nc.vector.tensor_tensor(nm[:, 4:NQ], nm[:, 4:NQ], m.nmax[:, 1, 4:NQ], ALU.min) \
                    .then_inc(m.m_part, 1)
                n = 1
                dve.wait_ge(m.m_part, unit * MAX_OPS + n)
                for k in range(3):
                    nc.vector.tensor_copy(m.mparts[:, :, k, :], nm).then_inc(m.m_part, 1)
                    n += 1
                    dve.wait_ge(m.m_part, unit * MAX_OPS + n)
                    if k < 2:
                        nc.vector.tensor_tensor(nm, nm, m.mparts[:, :, k, :], ALU.subtract).then_inc(m.m_part, 1)
                        n += 1
                        dve.wait_ge(m.m_part, unit * MAX_OPS + n)
                assert n == MAX_OPS
                dve.wait_ge(m.m_t, unit + 1)
                if not is_first(unit):
                    dve.wait_ge(m.m_out, unit * 16)
                nc.vector.tensor_copy(m.mrows[:], bank16(6)[0:12, :]).then_inc(m.m_rows, 1)

            def output(seq):
                def divide(t):
                    dve.wait_ge(m.o_t, seq * NQ + t + 1)
                    o = bank(t % 2).rearrange("p (h e) -> p h e", h=H)
                    nc.vector.reciprocal(m.rsum[:, t % 2], o[:, :, HD]).then_inc(m.o_n, 1)
                    dve.wait_ge(m.o_n, seq * (2 * NQ) + 2 * t + 1)
                    if t >= 2:
                        dve.wait_ge(m.o_tt, seq * NQ + t - 1)
                    nc.vector.tensor_tensor(m.on[:, t % 2].rearrange("p (h e) -> p h e", h=H), o[:, :, 0:HD],
                                            bc(m.rsum[:, t % 2], 2, HD), ALU.mult).then_inc(m.o_n, 1)

                divide(0)
                dve.wait_ge(m.o_x, seq * 16 + 16)
                for t in range(NQ):
                    if t + 1 < NQ:
                        divide(t + 1)
                    dve.wait_ge(m.o_mm, seq * NQ + t + 1)
                    nc.vector.tensor_tensor(m.xres[:, t, :], bank(4 + t % 2)[:, 0:D], m.xres[:, t, :], ALU.add) \
                        .then_inc(m.o_x1, 1)
                for t in range(NQ):
                    dve.wait_ge(m.o_x1, seq * NQ + t + 2)
                    nc.vector.bn_stats(m.stats2[:, bass.ds(seq * NQ + t, 1), :].rearrange("p a f -> p (a f)"),
                                       m.xres[:, t, :]).then_inc(m.o_bn, 1)

            def iteration(seq, g, maxima, operands):
                unit = seq * NG + g
                if maxima:
                    maxima_of(unit + 1)
                if operands:
                    for n in range(ACT_FILLS, FILLS):
                        dve.wait_ge(m.a_t, (unit + 2) * FILLS + n + 1)
                        copy_operand(nc.vector.tensor_copy, g, n).then_inc(m.a_fd, 1)
                if not leads_in(seq):
                    dve.wait_ge(m.v_o, unit * NQ + NQ + 2)
                    nc.vector.tensor_copy(m.ot[:, g, :], sums).then_inc(m.v_read, 1)
                    if g == NG - 1:
                        output(seq)

            nc.vector.memset(m.ks[QROWS:SROWS, 0:H // 2], 1.0).then_inc(m.a_ones, 1)
            dve.wait_ge(m.a_loaded[0], 64)
            for unit in range(2):
                split_and_stack(nc.vector, m.held_dve, m.stage_k[:, unit],
                                m.kn[:, :, 64 * unit:64 * unit + 64].rearrange("p t (j e) -> p t j e", j=4),
                                m.rest_dve[:], K_PARTS, m.a_k, unit * STACK_STEPS)
            dve.wait_ge(m.a_const, 32)
            nc.vector.tensor_copy(m.mask_qk[:], m.masks[:, 0, :]).then_inc(m.a_masks, 1)
            nc.vector.tensor_copy(m.mask_kq[:], m.masks[:, 1, :]).then_inc(m.a_masks, 1)
            everywhere(dve, iteration)


def second_norm(nc, m):
    bank = m.bank
    experts_in, shared_in = slice(0, E * I), slice(E * I, IT)
    whole = E * I // P
    cut = NI // 2

    def up_piece(w, shared, k):
        return [(lambda buf: buf[:, experts_in].rearrange("p (e i) -> p e i", e=E),
                 w.rearrange("e (k p) i -> k p e i", p=P)[k]),
                (lambda buf: buf[:, shared_in], shared.rearrange("(k p) i -> k p i", p=P)[k])]

    def down(n0, n1):
        return lambda buf: buf[:, D * n0:D * n1].rearrange("p (n h) -> p n h", h=D)

    experts_down = m.w_down.rearrange("e i h -> (e i) h").rearrange("(n p) h -> p n h", p=P)
    pieces = [up_piece(m.w_gate, m.sw_gate, 0), up_piece(m.w_gate, m.sw_gate, 1),
              up_piece(m.w_up, m.sw_up, 0), up_piece(m.w_up, m.sw_up, 1),
              [(lambda buf: buf[0:3 * (E + 1), 0:NI * P], m.c_sel)],
              [(down(0, cut), experts_down[:, 0:cut, :])],
              [(down(0, whole - cut), experts_down[:, cut:whole, :]),
               (down(whole - cut, NI - 1 - cut), m.sw_down[0:IS - LAST, :].rearrange("(n p) h -> p n h", p=P)),
               (lambda buf: buf[0:LAST, D * (NI - 1 - cut):D * (NI - cut)], m.sw_down[IS - LAST:IS, :])]]
    parts = [[w[:, i, k, :] for i in range(2)] for w in (m.wg, m.wu_ffn) for k in range(2)]
    parts += [None, [m.wd[:, i, 0:cut].rearrange("p n h -> p (n h)") for i in range(2)],
              [m.wd[:, i, cut:NI].rearrange("p n h -> p (n h)") for i in range(2)]]
    SELECTION = 4

    def raw(i):
        width = NI * P if i <= SELECTION else (cut if i == 5 else NI - cut) * D
        return m.piece[:, i % 2, 0:width]

    def loaded(i):
        return 16 * sum(len(pieces[j]) for j in range(i % 2, i + 1, 2))

    with nc.Block() as block:

        @block.sync
        def _(sp):
            def load(s):
                sp.dma_start(m.xg[:, s % 2], m.x1_dram[:, 4 * s:4 * s + 4, :]).then_inc(m.f_x[s % 2], 16)

            load(0)
            load(1)
            sp.dma_start(m.gt[:], m.router_w.rearrange("(k p) e -> p k e", p=P)).then_inc(m.f_gate, 16)
            sp.dma_start(m.key[:], m.c_key).then_inc(m.f_const, 16)
            for s in range(NTG):
                if s + 2 < NTG:
                    sp.wait_ge(m.f_xn, s + 1)
                    load(s + 2)
                sp.wait_ge(m.f_te, 2 * s + 2)
                sp.dma_start(m.xt_dram[:, s], m.xs[:, s % 2]).then_inc(m.f_xs[s % 2], 16)
            for u in range(2):
                sp.wait_ge(m.f_xs[u], 16 * (NTG // 2))
            sp.wait_ge(m.f_const, 16)

        @block.scalar
        def _(act):
            def load(i):
                for dst, src in pieces[i]:
                    act.dma_start(dst(m.piece[:, i % 2]), src).then_inc(m.f_w[i % 2], 16)

            act.wait_ge(m.f_pad, 1)
            load(0)
            load(1)
            act.wait_ge(m.f_ln, 3)
            nc.scalar.activation(m.rstd[:], m.rstd[:], ACT.Sqrt).then_inc(m.f_sqrt, 1)

            def copy_out(s):
                act.wait_ge(m.f_t, s + 1)
                if s >= 2:
                    act.wait_ge(m.f_xs[s % 2], 16 * (s // 2))
                    act.wait_ge(m.f_lg, s - 1)
                for k in range(2):
                    nc.scalar.copy(m.xs[:, s % 2, k, :], bank(3 * (s % 2) + k)[:]).then_inc(m.f_te, 1)

            copy_out(0)
            for s in range(NTG):
                if s < len(pieces):
                    act.wait_ge(m.f_w[s % 2], loaded(s))
                    if s == SELECTION:
                        nc.scalar.copy(m.sel[:].rearrange("p n j -> p (n j)"), raw(s)[0:3 * (E + 1)]) \
                            .then_inc(m.f_high, 1)
                    else:
                        nc.scalar.copy(parts[s][0], raw(s)).then_inc(m.f_high, 1)
                if s + 1 < NTG:
                    copy_out(s + 1)
                if 1 <= s < len(pieces) - 1:
                    act.wait_ge(m.f_low, s)
                    act.wait_ge(m.f_high, s)
                    if s + 1 == len(pieces) - 1:
                        act.wait_ge(m.f_pad, 2)
                    load(s + 1)

        @block.vector
        def _(dve):
            nc.vector.memset(m.piece[:, :, IT:NI * P], 0.0).then_inc(m.f_pad, 1)
            for t in range(NB * NQ):
                last = nc.vector.bn_aggr(m.mv[:, t, :], m.stats2[:, t, :])
            last.then_inc(m.f_ln, 1)
            dve.wait_ge(m.f_ln, 1)
            nc.vector.tensor_scalar(m.rstd[:], m.mv[:, :, 1], 1e-5, None, ALU.add).then_inc(m.f_ln, 1)
            nc.vector.tensor_copy(m.mean[:], m.mv[:, :, 0]).then_inc(m.f_ln, 1)
            dve.wait_ge(m.f_sqrt, 1)
            nc.vector.reciprocal(m.rstd[:], m.rstd[:]).then_inc(m.f_ln, 1)
            dve.wait_ge(m.f_ln, 4)

            def normalise(s):
                dve.wait_ge(m.f_x[s % 2], 16 * (s // 2) + 16)
                if s >= 2:
                    dve.wait_ge(m.f_t, s - 1)
                for q in range(4):
                    last = nc.vector.tensor_scalar(
                        m.xm[:, s % 2, q, :], m.xg[:, s % 2, q, :], m.mean[:, 4 * s + q:4 * s + q + 1],
                        m.rstd[:, 4 * s + q:4 * s + q + 1], ALU.subtract, ALU.mult)
                last.then_inc(m.f_xn, 1)

            normalise(0)
            for s in range(NTG):
                if s + 1 < NTG:
                    normalise(s + 1)
                if s < len(pieces):
                    dve.wait_ge(m.f_high, s + 1)
                    if s == SELECTION:
                        nc.vector.memset(m.piece[LAST:, s % 2, D * (NI - 1 - cut):D * (NI - cut)], 0.0) \
                            .then_inc(m.f_pad, 1)
                        dve.sem_inc(m.f_low, 1)
                    else:
                        nc.vector.tensor_tensor(parts[s][1], raw(s), parts[s][0].bitcast(F32), ALU.subtract) \
                            .then_inc(m.f_low, 1)
                dve.wait_ge(m.f_lg, s + 1)
                nc.vector.tensor_copy(m.lg[:, 4 * s:4 * s + 4, :],
                                      bank(2)[:, 0:4 * (E + 1)].rearrange("p (q e) -> p q e", q=4)) \
                    .then_inc(m.f_lge, 1)

        @block.tensor
        def _(pe):
            pe.wait_ge(m.f_gate, 16)

            def turn(s):
                pe.wait_ge(m.f_xn, s + 1)
                if s >= 2:
                    pe.wait_ge(m.f_te, 2 * s - 2)
                for k in range(2):
                    for q in range(4):
                        last = nc.tensor.transpose(bank(3 * (s % 2) + k)[:, P * q:P * q + P],
                                                   m.xm[:, s % 2, q, P * k:P * k + P], m.ident[:])
                last.then_inc(m.f_t, 1)

            turn(0)
            for s in range(NTG):
                if s + 1 < NTG:
                    turn(s + 1)
                pe.wait_ge(m.f_te, 2 * s + 2)
                if s > 0:
                    pe.wait_ge(m.f_lge, s)
                for q in range(4):
                    for k in range(2):
                        last = nc.tensor.matmul(bank(2)[:, (E + 1) * q:(E + 1) * (q + 1)],
                                                m.xs[:, s % 2, k, P * q:P * q + P], m.gt[:, k, :],
                                                start=k == 0, stop=k == 1)
                last.then_inc(m.f_lg, 1)


def router(nc, m):
    NT = NB * NQ
    le, ex, gate = m.lg[:, :, 0:E], m.ex[:], m.lg[:, :, E]
    with nc.Block() as block:

        @block.vector
        def _(dve):
            n = 0

            def step(instruction):
                nonlocal n
                n += 1
                instruction.then_inc(m.t_dve, 1)
                dve.wait_ge(m.t_dve, n)

            key = bc(m.key[:], 1, NT)
            step(nc.vector.tensor_reduce(m.top[:], le, AX, ALU.max))
            step(nc.vector.tensor_tensor(ex, le, bc(m.top[:], 2, E), ALU.subtract))
            dve.wait_ge(m.t_exp, 2)
            step(nc.vector.tensor_reduce(m.top[:], ex, AX, ALU.max))
            step(nc.vector.tensor_copy(m.total[:], m.top[:]))
            step(nc.vector.tensor_copy(m.left[:], ex))
            for rank in range(2):
                step(nc.vector.tensor_tensor(m.hit[:], m.left[:], bc(m.top[:], 2, E), ALU.is_equal))
                step(nc.vector.tensor_tensor(m.hit[:], m.hit[:], key, ALU.mult))
                step(nc.vector.tensor_reduce(m.top[:], m.hit[:], AX, ALU.max))
                step(nc.vector.tensor_tensor(m.hit[:], key, bc(m.top[:], 2, E), ALU.is_equal))
                if rank == 0:
                    step(nc.vector.tensor_copy(m.chosen[:], m.hit[:]))
                    step(nc.vector.scalar_tensor_tensor(m.left[:], m.hit[:], -2.0, m.left[:], ALU.mult, ALU.add))
                    step(nc.vector.tensor_reduce(m.top[:], m.left[:], AX, ALU.max))
                    step(nc.vector.tensor_tensor(m.total[:], m.total[:], m.top[:], ALU.add))
                else:
                    step(nc.vector.tensor_tensor(m.chosen[:], m.chosen[:], m.hit[:], ALU.add))
            step(nc.vector.reciprocal(m.total[:], m.total[:]))
            step(nc.vector.tensor_tensor(m.chosen[:], m.chosen[:], ex, ALU.mult))
            step(nc.vector.tensor_tensor(m.comb[:, :, 0:E], m.chosen[:], bc(m.total[:], 2, E), ALU.mult))
            step(nc.vector.tensor_scalar(gate, gate, 1.0, None, ALU.add))
            step(nc.vector.reciprocal(m.comb[:, :, E], gate))
            for k in range(3):
                step(nc.vector.tensor_copy(m.cparts[:, :, k, :], m.comb[:]))
                if k < 2:
                    step(nc.vector.tensor_tensor(m.comb[:], m.comb[:], m.cparts[:, :, k, :], ALU.subtract))
            for g in range(4):
                dve.wait_ge(m.t_turn, g + 1)
                nc.vector.tensor_copy(m.ct[:, 1024 * g:1024 * g + 1024], m.bank16(g)[0:3 * (E + 1), :]) \
                    .then_inc(m.t_out, 1)

        @block.scalar
        def _(act):
            act.wait_ge(m.t_dve, 2)
            nc.scalar.activation(ex, ex, ACT.Exp).then_inc(m.t_exp, 1)
            nc.scalar.activation(gate, gate, ACT.Exp, scale=-1.0).then_inc(m.t_exp, 1)

        @block.tensor
        def _(pe):
            pe.wait_ge(m.t_dve, 5 + 8 + 5 + 5 + 5)
            for t in range(NT):
                last = nc.tensor.transpose(m.bank16(t // 8)[0:3 * (E + 1), P * (t % 8):P * (t % 8) + P],
                                           m.cparts[:, t].rearrange("p r e -> p (r e)"), m.ident16[:])
                if t % 8 == 7:
                    last.then_inc(m.t_turn, 1)


def experts(nc, m):
    bank = m.bank

    def parity(u, n):
        return (u + n) % 2

    assert NI % 2 == 1

    with nc.Block() as block:

        @block.sync
        def _(sp):
            def load(s, u):
                sp.dma_start(m.xt[:, u], m.xt_dram[:, bass.ds(s, 1)].rearrange("p a k t -> p (a k) t")) \
                    .then_inc(m.e_xt[u], 16)

            def group(s, u, more):
                sp.wait_ge(m.e_st, s * 16 + 1)
                sp.dma_start(m.xg[:, 0], m.x1_dram[:, bass.ds(s * 4, 4), :]).then_inc(m.e_x, 16)
                if more:
                    sp.wait_ge(m.e_parts, s * 2 + 2)
                    load(s + 2, u)
                sp.wait_ge(m.e_y, s * 2 + 3)
                sp.dma_start(m.out_seq[:, bass.ds(s * 4, 4), :], m.xg[:, 0]).then_inc(m.e_st, 16)

            for u in range(2):
                load(u, u)
            with sp.Fori(0, NTG // 2 - 1) as ss:
                for u in range(2):
                    group(ss * 2 + u, u, True)
            for u in range(2):
                group(NTG - 2 + u, u, False)
            sp.wait_ge(m.e_st, 16 * NTG + 1)

        @block.gpsimd
        def _(pool):
            def split(s, ss, u, first):
                hold(pool, m.e_xt[u], ss * 16 + 16, m.held_pool)
                if not first:
                    hold(pool, m.e_g, s * NI - NI, m.held_pool)
                nc.gpsimd.tensor_copy(m.xtp[:, u, 0], m.xt[:, u]).then_inc(m.e_parts, 1)
                hold(pool, m.e_parts, s * 2 + 1, m.held_pool)
                nc.gpsimd.tensor_tensor(m.xtp[:, u, 1], m.xt[:, u], m.xtp[:, u, 0].bitcast(F32), ALU.subtract) \
                    .then_inc(m.e_parts, 1)

            for u in range(2):
                split(u, 0, u, True)
            with pool.Fori(1, NTG // 2) as ss:
                for u in range(2):
                    split(ss * 2 + u, ss, u, False)

        @block.tensor
        def _(pe):
            def up(s, u, n):
                if n == 0:
                    pe.wait_ge(m.e_parts, s * 2 + 2)
                pe.wait_ge(m.e_h, s * NI + n + 1)
                f, first = slice(P * n, P * n + P), 3 * parity(u, n)
                for i, w in enumerate((m.wg, m.wu_ffn)):
                    for k in range(2):
                        for a, b in PRODUCTS:
                            nc.tensor.matmul(bank(first + i)[:], w[:, a, k, f], m.xtp[:, u, b, k],
                                             start=(k, a, b) == (0, 0, 1), stop=(k, a, b) == (1, 0, 0))
                nc.tensor.matmul(bank(first + 2)[:], m.sel[:, n, :], m.ct[:, bass.ds(s * TG, TG)],
                                 start=True, stop=True).then_inc(m.e_g, 1)

            def down(s, u, n):
                pe.wait_ge(m.e_low, s * NI + n + 1)
                if n == 0:
                    pe.wait_ge(m.e_y, s * 2 + 1)
                for q in range(4):
                    for a, b in PRODUCTS:
                        last = nc.tensor.matmul(bank(6 + q // 2)[:, D * (q % 2):D * (q % 2) + D],
                                                m.h[:, parity(u, n), a, P * q:P * q + P], m.wd[:, b, n, :],
                                                start=n == 0 and q % 2 == 0 and (a, b) == (0, 1),
                                                stop=n == NI - 1 and (a, b) == (0, 0), skip_group_check=True)
                last.then_inc(m.e_d, 1)

            def group(s, u, more):
                for n in range(NI):
                    if n + 1 < NI:
                        up(s, u, n + 1)
                    elif more:
                        up(s + 1, 1 - u, 0)
                    down(s, u, n)

            up(0, 0, 0)
            with pe.Fori(0, NTG // 2 - 1) as ss:
                for u in range(2):
                    group(ss * 2 + u, u, True)
            for u in range(2):
                group(NTG - 2 + u, u, u == 0)

        @block.scalar
        def _(act):
            with act.Fori(0, NTG // 2) as ss:
                for u in range(2):
                    for n in range(NI):
                        v, chunk = parity(u, n), (ss * 2 + u) * NI + n
                        act.wait_ge(m.e_g, chunk + 1)
                        act.wait_ge(m.e_h, chunk + 1)
                        nc.scalar.activation(m.sg[:, v, :], bank(3 * v)[:], ACT.Silu).then_inc(m.e_s, 1)

        @block.vector
        def _(dve):
            with dve.Fori(0, NTG // 2) as ss:
                for u in range(2):
                    s = ss * 2 + u
                    for n in range(NI):
                        v, chunk = parity(u, n), s * NI + n
                        dve.wait_ge(m.e_s, chunk + 1)
                        nc.vector.tensor_tensor(m.sg[:, v, :], m.sg[:, v, :], bank(3 * v + 1)[:],
                                                ALU.mult).then_inc(m.e_t, 1)
                        dve.wait_ge(m.e_t, chunk + 1)
                        nc.vector.tensor_tensor(m.hw[:, v], m.sg[:, v, :], bank(3 * v + 2)[:],
                                                ALU.mult).then_inc(m.e_h, 1)
                        dve.wait_ge(m.e_h, chunk + 3)
                        dve.wait_ge(m.e_d, chunk + 1)
                        nc.vector.tensor_copy(m.h[:, v, 0], m.hw[:, v]).then_inc(m.e_high, 1)
                        dve.wait_ge(m.e_high, chunk + 1)
                        nc.vector.tensor_tensor(m.h[:, v, 1], m.hw[:, v], m.h[:, v, 0].bitcast(F32),
                                                ALU.subtract).then_inc(m.e_low, 1)
                    dve.wait_ge(m.e_d, s * NI + NI + 2)
                    dve.wait_ge(m.e_x, s * 16 + 16)
                    for i in range(2):
                        x = flat(m.xg[:, 0, 2 * i:2 * i + 2, :])
                        nc.vector.tensor_tensor(x, bank(6 + i)[:], x, ALU.add).then_inc(m.e_y, 1)


def layer(nc, ins, consts, out):
    m = Memory()
    (m.x_in, m.Wq, m.Wk, m.Wv, m.wo_dram, m.Wb, m.w_gate, m.w_up, m.w_down, m.sw_gate, m.sw_up, m.sw_down,
     m.router_w) = ins
    (m.c_cos, m.c_sin, m.c_ident, m.c_rowmask, m.c_pairmask, m.c_masks, m.c_sel, m.c_key) = consts
    m.x_seq = m.x_in.rearrange("b (t p) d -> p (b t) d", p=P)
    m.out_seq = out.rearrange("b (t p) d -> p (b t) d", p=P)
    m.wo_dram = m.wo_dram.rearrange("(k p) n -> p k n", p=P)

    def dram(name, shape, dt=F32):
        return nc.dram_tensor(name, shape, dt, kind="Internal").ap()

    m.q_dram = dram("q_dram", [P, NC, D])
    m.kb_dram = dram("kb_dram", [P, NC, D])
    m.v_dram = dram("v_dram", [P, NC, D])
    m.x1_dram = dram("x1_dram", [P, NB * NQ, D])
    m.xt_dram = dram("xt_dram", [P, NTG, 2, TG])
    m.max_dram = dram("max_dram", [12, N], BF16)

    with ExitStack() as whole:
        def sems(names):
            return [whole.enter_context(nc.semaphore(name)) for name in names.split()]

        m.const_loaded, m.w_split, m.ln_ready, m.ln_sqrt, m.ln_done, m.bn_done = sems(
            "const_loaded w_split ln_ready ln_sqrt ln_done bn_done")
        m.p_xn, m.p_xt, m.p_high, m.p_low, m.p_qk, m.p_rot, m.p_rope, m.p_v = sems(
            "p_xn p_xt p_high p_low p_qk p_rot p_rope p_v")
        m.k_sq, m.k_ss, m.k_sqrt, m.k_beta, m.k_lane = sems("k_sq k_ss k_sqrt k_beta k_lane")
        m.k_norm, m.k_kb, m.k_kb_last, m.k_stored, m.k_kb_stored = sems(
            "k_norm k_kb k_kb_last k_stored k_kb_stored")
        m.g_kc, m.g_kt, m.g_kt1, m.g_kt2 = sems("g_kc g_kt g_kt1 g_kt2")
        m.g_mm, m.g_out, m.g_tr = sems("g_mm g_out g_tr")
        m.solve, m.x_back, m.x_clear, m.g_an = sems("solve x_back x_clear g_an")
        m.held, m.held_sp, m.held_pool, m.held_dve = sems("held held_sp held_pool held_dve")
        m.r_xc, m.r_wu_mm, m.r_wu, m.r_wt_mm = sems("r_xc r_wu_mm r_wu r_wt_mm")
        m.r_wt, m.r_kb, m.r_ws = sems("r_wt r_kb r_ws")
        m.r_vn, m.r_ds, m.r_dsm, m.r_s = sems("r_vn r_ds r_dsm r_s")
        m.r_vo, m.r_v, m.r_stored = sems("r_vo r_v r_stored")
        m.a_const, m.a_masks, m.a_vg, m.a_k, m.a_q, m.a_t = sems("a_const a_masks a_vg a_k a_q a_t")
        m.a_fa, m.a_fd, m.a_ones = sems("a_fa a_fd a_ones")
        m.m_max, m.m_s, m.m_part, m.m_t = sems("m_max m_s m_part m_t")
        m.m_rows, m.m_out, m.m_in = sems("m_rows m_out m_in")
        m.v_read, m.v_vg, m.v_exp, m.v_s, m.v_o = sems("v_read v_vg v_exp v_s v_o")
        m.o_x, m.o_x1, m.o_st, m.o_n = sems("o_x o_x1 o_st o_n")
        m.o_t, m.o_te, m.o_tt = sems("o_t o_te o_tt")
        m.o_mm, m.o_bn = sems("o_mm o_bn")
        m.f_gate, m.f_pad, m.f_const = sems("f_gate f_pad f_const")
        m.f_xn, m.f_ln, m.f_sqrt = sems("f_xn f_ln f_sqrt")
        m.f_t, m.f_lg, m.f_lge, m.f_te, m.f_high, m.f_low = sems("f_t f_lg f_lge f_te f_high f_low")
        m.t_dve, m.t_exp, m.t_turn, m.t_out = sems("t_dve t_exp t_turn t_out")
        m.e_st, m.e_x, m.e_y, m.e_h, m.e_g, m.e_d, m.e_t = sems("e_st e_x e_y e_h e_g e_d e_t")
        m.e_s, m.e_parts, m.e_high, m.e_low = sems("e_s e_parts e_high e_low")
        m.starts = [
            (m.e_d, 2), (m.e_h, 2), (m.e_st, 1), (m.e_y, 1), (m.g_an, 1), (m.g_kt, 2), (m.g_kt1, 1),
            (m.g_mm, 2), (m.g_out, 1), (m.o_x1, 1), (m.p_rope, 2), (m.p_rot, 5), (m.p_v, 2), (m.r_ds, 2),
            (m.r_v, 1), (m.r_vo, 2), (m.v_exp, 2), (m.v_o, 2), (m.v_read, 1),
        ]
        m.x_loaded = sems("x_loaded0 x_loaded1 x_loaded2 x_loaded3")
        m.a_loaded = sems("a_loaded0 a_loaded1 a_loaded2")
        m.f_x = sems("f_x0 f_x1")
        m.f_xs = sems("f_xs0 f_xs1")
        m.f_w = sems("f_w0 f_w1")
        m.e_xt = sems("e_xt0 e_xt1")
        m.psum = whole.enter_context(nc.psum_tensor("psum", [P, 8, 512], F32))[:]
        m.bank = lambda i: m.psum[:, i, :]
        m.bank16 = lambda i: m.psum[:, i, :].bitcast(BF16)

        def sb(stack, name, shape, dt=F32):
            return stack.enter_context(nc.sbuf_tensor(name, shape, dt))[:]

        m.ident = sb(whole, "ident", [P, P])
        m.ident16 = sb(whole, "ident16", [P, P], BF16)
        m.mv = sb(whole, "mv", [P, NC, 2])
        m.mean = sb(whole, "mean", [P, NC])
        m.rstd = sb(whole, "rstd", [P, NC])
        m.stats2 = sb(whole, "stats2", [P, NC, 6])
        with ExitStack() as first:
            m.q = sb(first, "q", [P, NC, D])
            m.kv = sb(first, "kv", [P, NC, 2, D])
            m.beta = sb(first, "beta", [P, NC, H])
            m.beta_half = sb(first, "beta_half", [P, 2, NC * H])
            m.beta_lane = sb(first, "beta_lane", [P, NC // 2, 2 * H])
            m.rowmask = sb(first, "rowmask", [P, 2])
            m.pairmask = sb(first, "pairmask", [P, 34])
            with ExitStack() as stack:
                m.x = sb(stack, "x", [P, NC, D])
                m.cosq = sb(stack, "cosq", [P, NC, 8])
                m.sinq = sb(stack, "sinq", [P, NC, 8])
                m.w_in = sb(stack, "w_in", [P, 2, 3 * D + H])
                m.stats = sb(stack, "stats", [P, NC, 6])
                m.xn = sb(stack, "xn", [P, 2, D])
                m.xnt = sb(stack, "xnt", [P, 2, 2, 2, P], F32R)
                m.w_parts = sb(stack, "w_parts", [P, 2, 2, 3 * D + H], F32R)
                m.rc = sb(stack, "rc", [P, 2, 2 * H, 2, 8])
                m.rs = sb(stack, "rs", [P, 2, 2 * H, 2, 8])
                m.rn = sb(stack, "rn", [P, NC, H])
                m.sq = m.x
                load_constants(nc, m)
                projections(nc, m)
                normalise_keys(nc, m)
            with ExitStack() as stack:
                m.xl = sb(stack, "xl", [P, GP, 1024])
                m.xb = sb(stack, "xb", [P, GP, 1024])
                m.an = sb(stack, "an", [P, 2, GP, SUB, SUB])
                m.prod = sb(stack, "prod", [P, 2, GP, SUB - 1, SUB - 1])
                m.gs = sb(stack, "gs", [P, GP, 1024])
                m.gram = sb(stack, "gram", [P, 1024])
                m.kc = sb(stack, "kc", [P, 2, D])
                m.kt1 = sb(stack, "kt1", [P, 2, 2, P])
                m.kt2 = sb(stack, "kt2", [P, 2, 2, 2, P])
                m.xc = sb(stack, "xc", [P, 2, H, CT])
                m.kvc = sb(stack, "kvc", [P, 2, 2, D])
                m.wu = sb(stack, "wu", [P, 2, 2, D])
                m.wt = sb(stack, "wt", [P, 2, 2, P])
                m.kb = sb(stack, "kb", [P, 2, D])
                m.vn = sb(stack, "vn", [P, 2, D])
                m.vt = sb(stack, "vt", [P, 2, D])
                m.s = sb(stack, "s", [P, NB, 2, 32])
                m.ds = sb(stack, "ds", [P, NB, 2, 32])
                m.v = m.q
                delta_rule(nc, m)
        with ExitStack() as stack:
            m.kn = sb(stack, "kn", [P, NQ, D])
            m.qn = sb(stack, "qn", [P, NQ, D])
            m.vn2 = sb(stack, "vn2", [P, NQ, D])
            m.rest = sb(stack, "rest", [P, NQ, 4, HD])
            m.rest_dve = sb(stack, "rest_dve", [P, NQ, 4, HD])
            m.stage_k = sb(stack, "stage_k", [P, 2, NQ, 4, TERMS, HD], BF16)
            m.stage_q = sb(stack, "stage_q", [P, 2, NQ, 4, TERMS, HD], BF16)
            m.ks = sb(stack, "ks", [P, H, N], BF16)
            m.qs = sb(stack, "qs", [P, H, N], BF16)
            m.wo = sb(stack, "wo", [P, 2, D])
            m.masks = sb(stack, "masks", [P, 2, P])
            m.mask_qk = sb(stack, "mask_qk", [P, P], BF16)
            m.mask_kq = sb(stack, "mask_kq", [P, P], BF16)
            m.nmax = sb(stack, "nmax", [P, 2, NQ, 4])
            m.mparts = sb(stack, "mparts", [P, NQ, 3, 4], BF16)
            m.mrows = sb(stack, "mrows", [12, N], BF16)
            m.rsum = sb(stack, "rsum", [P, 2, H])
            m.vg = sb(stack, "vg", [P, 2, NQ, 4, 32])
            m.p = sb(stack, "p", [P, 8, N])
            m.ot = sb(stack, "ot", [P, NG, N])
            m.xres = sb(stack, "xres", [P, NQ, D])
            m.on = sb(stack, "on", [P, 2, D])
            m.ont = sb(stack, "ont", [P, 2, 2, P])
            attention(nc, m)
        with ExitStack() as stack:
            m.wg = sb(stack, "wg", [P, 2, 2, NI * P], F32R)
            m.wu_ffn = sb(stack, "wu_ffn", [P, 2, 2, NI * P], F32R)
            m.wd = sb(stack, "wd", [P, 2, NI, D], F32R)
            m.sel = sb(stack, "sel", [3 * (E + 1), NI, P], BF16)
            m.ct = sb(stack, "ct", [3 * (E + 1), NB * N], BF16)
            m.xg = sb(stack, "xg", [P, 2, 4, D])
            with ExitStack() as inner:
                m.piece = sb(inner, "piece", [P, 2, (NI - NI // 2) * D])
                m.gt = sb(inner, "gt", [P, 2, E + 1])
                m.key = sb(inner, "key", [P, E])
                m.xm = sb(inner, "xm", [P, 2, 4, D])
                m.xs = sb(inner, "xs", [P, 2, 2, TG])
                m.lg = sb(inner, "lg", [P, NC, E + 1])
                m.ex = sb(inner, "ex", [P, NC, E])
                m.left = sb(inner, "left", [P, NC, E])
                m.hit = sb(inner, "hit", [P, NC, E])
                m.chosen = sb(inner, "chosen", [P, NC, E])
                m.top = sb(inner, "top", [P, NC])
                m.total = sb(inner, "total", [P, NC])
                m.comb = sb(inner, "comb", [P, NC, E + 1])
                m.cparts = sb(inner, "cparts", [P, NC, 3, E + 1], BF16)
                second_norm(nc, m)
                router(nc, m)
            m.xt = sb(stack, "xt_raw", [P, 2, 2, TG])
            m.xtp = sb(stack, "xt_parts", [P, 2, 2, 2, TG], F32R)
            m.sg = sb(stack, "sg", [P, 2, TG])
            m.hw = sb(stack, "hw", [P, 2, TG])
            m.h = sb(stack, "h", [P, 2, 2, TG], F32R)
            experts(nc, m)


def constants():
    p = np.arange(P)
    pos = (p[:, None] % CT + CT * np.arange(NC)[None, :]).astype(np.float32)
    inv = (np.float32(1.0) / np.float32(10000.0) ** (np.arange(0, HD, 2, dtype=np.float32) / np.float32(HD)))
    angle = pos[:, :, None] * inv.astype(np.float32)
    pair = np.zeros((P, 34), np.float32)
    pair[:, 0:32] = (p[:, None] % 32 // HD) == (np.arange(32)[None, :] // HD)
    pair[:, 32], pair[:, 33] = p % 32 < HD, p % 32 >= HD
    unit = np.arange(NI * P)
    owner = np.minimum(unit // I, E)
    sel = np.zeros((3 * (E + 1), NI * P), np.float32)
    for k in range(3):
        sel[k * (E + 1) + owner, unit] = 1.0
    return {
        "c_cos": np.cos(angle).astype(np.float32), "c_sin": np.sin(angle).astype(np.float32),
        "c_ident": np.eye(P, dtype=np.float32),
        "c_rowmask": np.stack([p % CT < SUB, p % CT >= SUB], 1).astype(np.float32), "c_pairmask": pair,
        "c_masks": np.stack([np.where(p[None, :] > p[:, None], NEG, 0.0),
                             np.where(p[:, None] > p[None, :], NEG, 0.0)], 1).astype(np.float32),
        "c_sel": sel,
        "c_key": np.tile(np.arange(E, 0, -1, dtype=np.float32), (P, 1)),
    }


_INS = ["L0_attn_x", "L0_attn_Wq", "L0_attn_Wk", "L0_attn_Wv", "L0_attn_Wo", "L0_attn_Wb", "L0_ffn_w_gate",
        "L0_ffn_w_up", "L0_ffn_w_down", "L0_ffn_sw_gate", "L0_ffn_sw_up", "L0_ffn_sw_down"]


def kernel(**inputs):
    import numpy as _np
    import concourse.bacc as _bacc
    from concourse import mybir as _mybir
    from concourse.bass_utils import run_bass_kernel_spmd as _run

    nc = _bacc.Bacc("TRN2", target_bir_lowering=False, num_devices=1)
    given = {f"in_{name}_dram": _np.ascontiguousarray(inputs[name]) for name in _INS}
    given["in_router_dram"] = _np.ascontiguousarray(_np.concatenate(
        [_np.asarray(inputs["L0_ffn_gate_w"]).T, _np.asarray(inputs["L0_ffn_shared_gate_w"])], axis=1))
    tables = constants()

    def tensor(name, a):
        return nc.dram_tensor(name, a.shape, _mybir.dt.from_np(a.dtype), kind="ExternalInput").ap()

    ins = [tensor(name, a) for name, a in given.items()]
    consts = [tensor(name, a) for name, a in tables.items()]
    out = nc.dram_tensor("out_0_dram", (NB, N, D), _mybir.dt.float32, kind="ExternalOutput").ap()
    layer(nc, ins, consts, out)
    r = _run(nc, [{**given, **tables}], core_ids=[0])
    return r.results[0]["out_0_dram"]
```
